# Optimizing a Trainium2 kernel written in Bass

```python
import numpy as np
import jax
import jax.numpy as jnp

def _softmax(x, axis=-1):
    return jax.nn.softmax(x, axis=axis)

def _gelu(x):
    return jax.nn.gelu(x, approximate=True)

def _silu(x):
    return jax.nn.silu(x)

def _sigmoid(x):
    return jax.nn.sigmoid(x)

def _layernorm(x, axis=-1, eps=1e-05):
    m = jnp.mean(x, axis=axis, keepdims=True)
    v = jnp.var(x, axis=axis, keepdims=True)
    return (x - m) / jnp.sqrt(v + eps)

def _scatter_add(tgt, idx, src, axis=0):
    return tgt.at[idx].add(src)

def _segment_sum(src, seg, n):
    return jax.ops.segment_sum(src, seg, n)
kernel_name = 'mk_gnn_resnorm_d4_gnn_r64_f7ae83'

def setup_inputs(seed: int=0):
    np.random.seed(seed)
    _w = jnp.asarray

    def _rec_inputs():
        import jax
        import jax.numpy as jnp
        _gk = jax.random.key(seed)
        x = -0.000202 + 1 * jax.random.normal(jax.random.fold_in(_gk, 1), (100000, 128), jnp.float32)
        src = jax.random.randint(jax.random.fold_in(_gk, 2), (50000,), 0, 100000, jnp.int32)
        dst = jax.random.randint(jax.random.fold_in(_gk, 3), (50000,), 0, 100000, jnp.int32)
        _o = jnp.argsort(dst, stable=True)
        src = src[_o]
        dst = dst[_o]
        edge_attr_3 = -0.000451519 + 1.00018 * jax.random.normal(jax.random.fold_in(_gk, 12), (50000, 3), jnp.float32)
        edge_weight = jax.random.uniform(jax.random.fold_in(_gk, 14), (50000,), jnp.float32, 0.0, 0.999998)
        return (x, src, dst, edge_attr_3, edge_weight)
    x, src, dst, edge_attr_3, edge_weight = _rec_inputs()

    def _L0_gnn_setup():
        import jax, jax.numpy as jnp
        import numpy as np
        N_NODES = 50000
        N_EDGES = 12500
        IN_CH = 128
        HEADS = 4
        OUT_CH = 32
        key = jax.random.key(seed)
        k1, k2, k3, k4, k5 = jax.random.split(key, 5)
        x = jax.random.normal(k1, (N_NODES, IN_CH), dtype=jnp.float32)
        edge_index = jax.random.randint(k2, (2, N_EDGES), 0, N_NODES, dtype=jnp.int64)
        W = jax.random.normal(k3, (IN_CH, HEADS * OUT_CH), dtype=jnp.float32) * 0.1
        att = jax.random.normal(k4, (1, HEADS, 2 * OUT_CH), dtype=jnp.float32) * 0.1
        bias = jax.random.normal(k5, (HEADS * OUT_CH,), dtype=jnp.float32) * 0.01
        return {'x': x, 'edge_index': edge_index, 'W': W, 'att': att, 'bias': bias}
    _L0_gnn_all = _L0_gnn_setup()
    _L0_gnn_in = {k: v for k, v in _L0_gnn_all.items() if k in ('W', 'att', 'bias')}
    del _L0_gnn_all

    def _L1_gnn_setup():
        import jax, jax.numpy as jnp
        import numpy as np
        N, D, E = (625, 128, 10000)
        key = jax.random.key(seed)
        ks = jax.random.split(key, 6)
        x = jax.random.normal(ks[0], (N, D), dtype=jnp.float32)
        edge_index = jax.random.randint(ks[1], (2, E), 0, N, dtype=jnp.int64)
        s = 1.0 / np.sqrt(D)
        Wq = jax.random.normal(ks[2], (D, D), dtype=jnp.float32) * s
        Wk = jax.random.normal(ks[3], (D, D), dtype=jnp.float32) * s
        Wv = jax.random.normal(ks[4], (D, D), dtype=jnp.float32) * s
        Wo = jax.random.normal(ks[5], (D, D), dtype=jnp.float32) * s
        return {'x': x, 'Wq': Wq, 'Wk': Wk, 'Wv': Wv, 'Wo': Wo, 'edge_index': edge_index}
    _L1_gnn_all = _L1_gnn_setup()
    _L1_gnn_in = {k: v for k, v in _L1_gnn_all.items() if k in ('Wq', 'Wk', 'Wv', 'Wo')}
    del _L1_gnn_all

    def _L2_gnn_setup():
        import jax, jax.numpy as jnp
        import numpy as np
        N = 50000
        E = 25000
        D = 128

        def _gcn_norm(edge_index, num_nodes):
            loop = jnp.arange(num_nodes, dtype=edge_index.dtype)
            src = jnp.concatenate([edge_index[0], loop])
            dst = jnp.concatenate([edge_index[1], loop])
            deg = jax.ops.segment_sum(jnp.ones_like(dst, jnp.float32), dst, num_segments=num_nodes)
            dinv = jnp.where(deg > 0, jax.lax.rsqrt(deg), 0.0)
            norm = dinv[dst] * dinv[src]
            return (src, dst, norm)

        def _gcn_layer(x, src, dst, norm, W, b, num_nodes):
            h = x @ W
            msg = h[src] * norm[:, None]
            out = jax.ops.segment_sum(msg, dst, num_segments=num_nodes)
            return out + b
        key = jax.random.key(seed)
        k1, k2, k3, k4 = jax.random.split(key, 4)
        scale = 1.0 / np.sqrt(D)
        return {'x': jax.random.normal(k1, (N, D), jnp.float32), 'edge_index': jax.random.randint(k2, (2, E), 0, N, dtype=jnp.int32), 'W0': jax.random.normal(k3, (D, D), jnp.float32) * scale, 'b0': jnp.zeros((D,), jnp.float32), 'W1': jax.random.normal(k4, (D, D), jnp.float32) * scale, 'b1': jnp.zeros((D,), jnp.float32)}
    _L2_gnn_all = _L2_gnn_setup()
    _L2_gnn_in = {k: v for k, v in _L2_gnn_all.items() if k in ('W0', 'b0', 'W1', 'b1')}
    del _L2_gnn_all

    def _L3_gnn_setup():
        import jax, jax.numpy as jnp
        import numpy as np
        N = 50000
        E = 12500
        MUL = 32
        NB = 8
        R_MAX = 1.0
        AVG = 16.0
        SQ3 = 3.0 ** 0.5

        def _radial_embedding(r):
            x = jnp.clip(r / R_MAX, 0.0, 1.0)
            centers = jnp.arange(NB, dtype=jnp.float32) / (NB - 1)
            sigma = 1.0 / (NB - 1)
            emb = jnp.exp(-0.5 * ((x[:, None] - centers[None, :]) / sigma) ** 2)
            emb = emb * NB ** 0.5 * (r <= R_MAX).astype(jnp.float32)[:, None]
            return emb
        key = jax.random.key(seed)
        k = jax.random.split(key, 12)
        inp = {'node_feats': jax.random.normal(k[0], (N, 4 * MUL), dtype=jnp.float32), 'edge_vec': jax.random.normal(k[1], (E, 3), dtype=jnp.float32), 'edge_length': jax.random.uniform(k[2], (E,), dtype=jnp.float32), 'senders': jax.random.randint(k[3], (E,), 0, N, dtype=jnp.int32), 'receivers': jax.random.randint(k[4], (E,), 0, N, dtype=jnp.int32), 'num_nodes': N, 'W_up0': jax.random.normal(k[5], (MUL, MUL), dtype=jnp.float32), 'W_up1': jax.random.normal(k[6], (MUL, MUL), dtype=jnp.float32), 'mlp_w0': jax.random.normal(k[7], (NB, 64), dtype=jnp.float32) / NB ** 0.5, 'mlp_b0': jnp.zeros((64,), dtype=jnp.float32), 'mlp_w1': jax.random.normal(k[8], (64, 64), dtype=jnp.float32) / 8.0, 'mlp_b1': jnp.zeros((64,), dtype=jnp.float32), 'mlp_w2': jax.random.normal(k[9], (64, 4 * MUL), dtype=jnp.float32) / 8.0, 'mlp_b2': jnp.zeros((4 * MUL,), dtype=jnp.float32), 'W_out0': jax.random.normal(k[10], (2 * MUL, MUL), dtype=jnp.float32), 'W_out1': jax.random.normal(k[11], (2 * MUL, MUL), dtype=jnp.float32)}
        return inp
    _L3_gnn_all = _L3_gnn_setup()
    _L3_gnn_in = {k: v for k, v in _L3_gnn_all.items() if k in ('W_up0', 'W_up1', 'mlp_w0', 'mlp_b0', 'mlp_w1', 'mlp_b1', 'mlp_w2', 'mlp_b2', 'W_out0', 'W_out1')}
    del _L3_gnn_all
    return {'x': x, 'src': src, 'dst': dst, 'edge_attr_3': edge_attr_3, 'edge_weight': edge_weight, 'L0_gnn_W': _L0_gnn_in['W'], 'L0_gnn_att': _L0_gnn_in['att'], 'L0_gnn_bias': _L0_gnn_in['bias'], 'L1_gnn_Wq': _L1_gnn_in['Wq'], 'L1_gnn_Wk': _L1_gnn_in['Wk'], 'L1_gnn_Wv': _L1_gnn_in['Wv'], 'L1_gnn_Wo': _L1_gnn_in['Wo'], 'L2_gnn_W0': _L2_gnn_in['W0'], 'L2_gnn_b0': _L2_gnn_in['b0'], 'L2_gnn_W1': _L2_gnn_in['W1'], 'L2_gnn_b1': _L2_gnn_in['b1'], 'L3_gnn_W_up0': _L3_gnn_in['W_up0'], 'L3_gnn_W_up1': _L3_gnn_in['W_up1'], 'L3_gnn_mlp_w0': _L3_gnn_in['mlp_w0'], 'L3_gnn_mlp_b0': _L3_gnn_in['mlp_b0'], 'L3_gnn_mlp_w1': _L3_gnn_in['mlp_w1'], 'L3_gnn_mlp_b1': _L3_gnn_in['mlp_b1'], 'L3_gnn_mlp_w2': _L3_gnn_in['mlp_w2'], 'L3_gnn_mlp_b2': _L3_gnn_in['mlp_b2'], 'L3_gnn_W_out0': _L3_gnn_in['W_out0'], 'L3_gnn_W_out1': _L3_gnn_in['W_out1']}

def reference(x, src, dst, edge_attr_3, edge_weight, L0_gnn_W, L0_gnn_att, L0_gnn_bias, L1_gnn_Wq, L1_gnn_Wk, L1_gnn_Wv, L1_gnn_Wo, L2_gnn_W0, L2_gnn_b0, L2_gnn_W1, L2_gnn_b1, L3_gnn_W_up0, L3_gnn_W_up1, L3_gnn_mlp_w0, L3_gnn_mlp_b0, L3_gnn_mlp_w1, L3_gnn_mlp_b1, L3_gnn_mlp_w2, L3_gnn_mlp_b2, L3_gnn_W_out0, L3_gnn_W_out1):
    import jax
    import jax.numpy as jnp

    def _L0_gnn_ref(x, edge_index, W, att, bias):
        import jax, jax.numpy as jnp
        import numpy as np
        N_NODES = 50000
        N_EDGES = 12500
        IN_CH = 128
        HEADS = 4
        OUT_CH = 32
        N = x.shape[0]
        E = edge_index.shape[1]
        H, C = (HEADS, OUT_CH)
        h = (x @ W).reshape(N, H, C)
        row, col = (edge_index[0], edge_index[1])
        a_src = att[0, :, :C]
        a_dst = att[0, :, C:]
        s_src = jnp.einsum('nhc,hc->nh', h, a_src)
        s_dst = jnp.einsum('nhc,hc->nh', h, a_dst)
        alpha = jax.nn.leaky_relu(s_src[row] + s_dst[col], negative_slope=0.2)
        seg_max = jax.ops.segment_max(alpha, row, num_segments=N)
        m = jnp.maximum(seg_max, 0.0)
        ex = jnp.exp(alpha - m[row])
        seg_sum = jax.ops.segment_sum(ex, row, num_segments=N)
        deg = jax.ops.segment_sum(jnp.ones((E,), x.dtype), row, num_segments=N)
        denom = seg_sum + (jnp.float32(E) - deg)[:, None] * jnp.exp(-m)
        alpha_n = ex / denom[row]
        msg = alpha_n[:, :, None] * h[col]
        out = jax.ops.segment_sum(msg, col, num_segments=N)
        out = out.reshape(N, H * C) + bias
        return out

    def _L1_gnn_ref(x, Wq, Wk, Wv, Wo, edge_index):
        import jax, jax.numpy as jnp
        import numpy as np
        N, D, E = (625, 128, 10000)
        num_nodes, d = x.shape
        scale = d ** (-0.5)
        sender, receiver = (edge_index[0], edge_index[1])
        Q = x @ Wq
        K = x @ Wk
        V = x @ Wv
        e = jnp.sum(Q[receiver] * K[sender], axis=-1) * scale
        m = jax.ops.segment_max(e, receiver, num_segments=num_nodes)
        m = jnp.where(jnp.isfinite(m), m, 0.0)
        w = jnp.exp(e - m[receiver])
        denom = jax.ops.segment_sum(w, receiver, num_segments=num_nodes)
        numer = jax.ops.segment_sum(w[:, None] * V[sender], receiver, num_segments=num_nodes)
        attn = jnp.where(denom[:, None] > 0, numer / jnp.maximum(denom, 1e-30)[:, None], 0.0)
        return x + attn @ Wo

    def _L2_gnn_ref(x, edge_index, W0, b0, W1, b1):
        import jax, jax.numpy as jnp
        import numpy as np
        N = 50000
        E = 25000
        D = 128

        def _gcn_norm(edge_index, num_nodes):
            loop = jnp.arange(num_nodes, dtype=edge_index.dtype)
            src = jnp.concatenate([edge_index[0], loop])
            dst = jnp.concatenate([edge_index[1], loop])
            deg = jax.ops.segment_sum(jnp.ones_like(dst, jnp.float32), dst, num_segments=num_nodes)
            dinv = jnp.where(deg > 0, jax.lax.rsqrt(deg), 0.0)
            norm = dinv[dst] * dinv[src]
            return (src, dst, norm)

        def _gcn_layer(x, src, dst, norm, W, b, num_nodes):
            h = x @ W
            msg = h[src] * norm[:, None]
            out = jax.ops.segment_sum(msg, dst, num_segments=num_nodes)
            return out + b
        num_nodes = x.shape[0]
        src, dst, norm = _gcn_norm(edge_index, num_nodes)
        x = jax.nn.relu(_gcn_layer(x, src, dst, norm, W0, b0, num_nodes))
        x = jax.nn.relu(_gcn_layer(x, src, dst, norm, W1, b1, num_nodes))
        return x

    def _L3_gnn_ref(node_feats, edge_vec, edge_length, senders, receivers, num_nodes, W_up0, W_up1, mlp_w0, mlp_b0, mlp_w1, mlp_b1, mlp_w2, mlp_b2, W_out0, W_out1):
        import jax, jax.numpy as jnp
        import numpy as np
        N = 50000
        E = 12500
        MUL = 32
        NB = 8
        R_MAX = 1.0
        AVG = 16.0
        SQ3 = 3.0 ** 0.5

        def _radial_embedding(r):
            x = jnp.clip(r / R_MAX, 0.0, 1.0)
            centers = jnp.arange(NB, dtype=jnp.float32) / (NB - 1)
            sigma = 1.0 / (NB - 1)
            emb = jnp.exp(-0.5 * ((x[:, None] - centers[None, :]) / sigma) ** 2)
            emb = emb * NB ** 0.5 * (r <= R_MAX).astype(jnp.float32)[:, None]
            return emb
        f32 = jnp.float32
        rhat = edge_vec / (jnp.linalg.norm(edge_vec, axis=-1, keepdims=True) + 1e-12)
        Y1 = SQ3 * rhat
        emb = _radial_embedding(edge_length)
        h = jax.nn.silu(emb @ mlp_w0 + mlp_b0)
        h = jax.nn.silu(h @ mlp_w1 + mlp_b1)
        w = (h @ mlp_w2 + mlp_b2).reshape(-1, 4, MUL)
        s = node_feats[:, :MUL]
        v = node_feats[:, MUL:].reshape(-1, MUL, 3)
        xs = s @ W_up0 / f32(MUL) ** 0.5
        xv = jnp.einsum('nmc,mk->nkc', v, W_up1) / f32(MUL) ** 0.5
        ss = xs[senders]
        vv = xv[senders]
        m0 = w[:, 0] * ss
        m1 = w[:, 1][:, :, None] * ss[:, :, None] * Y1[:, None, :]
        m2 = w[:, 2][:, :, None] * vv
        m3 = w[:, 3] * (jnp.einsum('emc,ec->em', vv, Y1) / SQ3)
        mid_s = jnp.concatenate([m0, m3], axis=1)
        mid_v = jnp.concatenate([m1, m2], axis=1)
        msg_s = jax.ops.segment_sum(mid_s, receivers, num_segments=num_nodes)
        msg_v = jax.ops.segment_sum(mid_v, receivers, num_segments=num_nodes)
        out_s = msg_s @ W_out0 / f32(2 * MUL) ** 0.5
        out_v = jnp.einsum('nmc,mk->nkc', msg_v, W_out1) / f32(2 * MUL) ** 0.5
        out = jnp.concatenate([out_s, out_v.reshape(-1, 3 * MUL)], axis=1)
        return out / max(AVG, 1e-08)
    edge_index = jnp.stack([src, dst])
    x = _layernorm(x + _L0_gnn_ref(x, edge_index, L0_gnn_W, L0_gnn_att, L0_gnn_bias), axis=-1)
    x = _layernorm(x + _L1_gnn_ref(x, L1_gnn_Wq, L1_gnn_Wk, L1_gnn_Wv, L1_gnn_Wo, edge_index), axis=-1)
    x = _layernorm(x + _L2_gnn_ref(x, edge_index, L2_gnn_W0, L2_gnn_b0, L2_gnn_W1, L2_gnn_b1), axis=-1)
    x = _layernorm(x + _L3_gnn_ref(x, edge_attr_3, edge_weight, src, dst, 100000, L3_gnn_W_up0, L3_gnn_W_up1, L3_gnn_mlp_w0, L3_gnn_mlp_b0, L3_gnn_mlp_w1, L3_gnn_mlp_b1, L3_gnn_mlp_w2, L3_gnn_mlp_b2, L3_gnn_W_out0, L3_gnn_W_out1), axis=-1)
    return x

_drawn_inputs = setup_inputs


def setup_inputs(seed=0):
    import zlib

    import numpy as np

    out = dict(_drawn_inputs(seed))
    spreads = {'L2_gnn_b0': (0.0, 0.1),
     'L2_gnn_b1': (0.0, 0.1),
     'L3_gnn_mlp_b0': (0.0, 0.8),
     'L3_gnn_mlp_b1': (0.0, 0.8),
     'L3_gnn_mlp_b2': (0.0, 0.8)}
    factors = {'edge_attr_3': 4.401,
     'edge_weight': 4.415,
     'L0_gnn_W': 8.0,
     'L0_gnn_att': 8.0,
     'L0_gnn_bias': 5.198,
     'L3_gnn_W_up0': 4.379,
     'L3_gnn_W_up1': 4.265,
     'L3_gnn_mlp_w0': 3.66,
     'L3_gnn_mlp_w1': 3.111,
     'L3_gnn_mlp_w2': 3.041,
     'L3_gnn_W_out0': 6.046,
     'L3_gnn_W_out1': 3.625}
    for name, (base, spread) in spreads.items():
        noise = np.random.default_rng([zlib.crc32(name.encode()), seed]).standard_normal(out[name].shape)
        drawn = base * np.exp(spread * noise) if base else spread * noise
        out[name] = jnp.asarray(drawn.astype(out[name].dtype))
    for name, factor in factors.items():
        out[name] = (out[name] * factor).astype(out[name].dtype)
    return out
```

```python
from contextlib import ExitStack

import concourse.bass as bass
from concourse import mybir

ALU = mybir.AluOpType
ACT = mybir.ActivationFunctionType
F32 = mybir.dt.float32
I32 = mybir.dt.int32

P = 128
N = 100000
E = 50000
D = 128
HEADS = 4
HC = D // HEADS
CHUNKS = 392
EP = CHUNKS * P
LOOPS = CHUNKS // 8
SORTN = 65536
SORTF = SORTN // P
G = 8
SUPER = P * G
NSUPER = -(-N // SUPER)
LAST = N - SUPER
NLOOPS = NSUPER // 2
PAD_ID = 1 << 17
NO_ROW = 1 << 20
BIG = 1.0e30
EPS = 1e-5
NB = 8
MUL = 32
AVG = 16.0
assert CHUNKS % 8 == 0 and EP >= E and NSUPER % 2 == 0 and N < PAD_ID


def stage_makers(nc, ctx, stage):
    owned = []

    def sb(name, shape, dtype=F32):
        return ctx.enter_context(nc.sbuf_tensor(f"{stage}_{name}", shape, dtype))

    def ps(name, shape, dtype=F32):
        return ctx.enter_context(nc.psum_tensor(f"{stage}_{name}", shape, dtype))

    def sem(name):
        owned.append(nc.alloc_semaphore(f"{stage}_{name}"))
        return owned[-1]

    def sems(name):
        return [sem(f"{name}{i}") for i in range(2)]

    return sb, ps, sem, sems, owned


def end_stage(nc, owned):
    nc.clear_and_free_semaphores(owned)
    nc.all_engine_barrier()


def chain_of(engine, sem):
    count = [0]

    def link(instruction):
        count[0] += 1
        instruction.then_inc(sem, 1)
        engine.wait_ge(sem, count[0])
    return link


def loop_chain_of(engine, sem, t, per):
    count = [0]

    def link(instruction):
        count[0] += 1
        assert count[0] <= per
        instruction.then_inc(sem, 1)
        engine.wait_ge(sem, t * per + count[0])
    return link


def wait_for(engine, sem, value):
    if not isinstance(value, int) or value > 0:
        engine.wait_ge(sem, value)


def node_base(t, h):
    if isinstance(t, int) and 2 * t + h == NSUPER - 1:
        return LAST
    return t * (2 * SUPER) + h * SUPER


def node_rows(table, t, h):
    return table[bass.ds(node_base(t, h), SUPER), :].rearrange("(p g) d -> p g d", g=G)


def node_loop(engine, body):
    for h in range(2):
        body(0, h)
    with engine.Fori(1, NLOOPS - 1) as t:
        for h in range(2):
            body(t, h)
    for h in range(2):
        body(NLOOPS - 1, h)




def prepare(nc, A, T, K):
    with ExitStack() as ctx:
        sb, ps, sem, sems, owned = stage_makers(nc, ctx, "prep")
        ints = sb("ints", [P, 2, CHUNKS], I32)
        flts = sb("flts", [P, 2, CHUNKS])
        wts = sb("wts", [P, 6, D])
        wT = sb("wT", [P, 5, D])
        att8 = sb("att8", [P, 8])
        zeros = sb("zeros", [P, SUPER])
        ew = sb("ew", [P, CHUNKS])
        ones = sb("ones", [P, P])
        rows = CHUNKS // 4
        cur = sb("cur", [P, 4, P])
        nxt = sb("nxt", [P, 4, P])
        srow = sb("srow", [P, 4, P])
        vec = sb("vec", [P, 4 * P, 3])
        scat = sb("scat", [P, 4, P])
        rnorm = sb("rnorm", [P, 4 * P])
        sq = sb("sq", [P, 4 * P, 3])
        rinv = sb("rinv", [P, 4 * P])
        rhatR = sb("rhatR", [P, 3, 4, P])
        scatB = sb("scatB", [P, CHUNKS])
        dshift = sb("dshift", [P, CHUNKS])
        srcB = sb("srcB", [P, CHUNKS])
        wo0 = sb("wo0", [P, 2, MUL])
        pw = ps("pw", [P, 4, P])
        pw2 = ps("pw2", [P, 4, P])
        pt = ps("pt", [P, 4, P])
        chain_v = sem("chain_v")
        chain_g = sem("chain_g")
        pads_set = sem("pads_set")
        ids_loaded = sem("ids_loaded")
        ids_float = sem("ids_float")
        ids_stored = sem("ids_stored")
        small_loaded = sem("small_loaded")
        vec_loaded = sem("vec_loaded")
        rows_loaded = sem("rows_loaded")
        ident_ready = sem("ident_ready")
        w_loaded = sem("w_loaded")
        agg_zeroed = sem("agg_zeroed")
        zeros_set = sem("zeros_set")
        up_built = sem("up_built")
        pe_done = sem("pe_done")
        pe_used = sem("pe_used")
        sumsq_ready = sem("sumsq_ready")
        norm_ready = sem("norm_ready")
        chunkify = sem("chunkify")
        full_rows, tail = E // (4 * P), E % (4 * P)
        full_lines, tail_line = E // CHUNKS, E % CHUNKS
        block = ctx.enter_context(nc.Block())

        @block.gpsimd
        def _(pool):
            link = chain_of(pool, chain_g)
            link(pool.memset(ones[:], 1.0))
            pool.affine_select(out=K["ident"][:], in_=ones[:], compare_op=ALU.is_equal, fill=0.0,
                               base=0, pattern=[[-1, P]], channel_multiplier=1).then_inc(ident_ready, 1)

        @block.sync
        def _(sp):
            sp.wait_ge(pads_set, 1)
            for a, name in enumerate(["src", "dst"]):
                ids = A[name]
                sp.dma_start(ints[0:full_lines, a, :],
                             ids[0:full_lines * CHUNKS].rearrange("(p f) -> p f", f=CHUNKS)).then_inc(ids_loaded, 16)
                sp.dma_start(ints[full_lines:full_lines + 1, a, 0:tail_line],
                             ids[full_lines * CHUNKS:E].rearrange("(p f) -> p f", p=1)).then_inc(ids_loaded, 16)
            sp.dma_start(ew[0:full_lines, :],
                         A["edge_weight"][0:full_lines * CHUNKS].rearrange("(p f) -> p f", f=CHUNKS)).then_inc(ids_loaded, 16)
            sp.dma_start(ew[full_lines:full_lines + 1, 0:tail_line],
                         A["edge_weight"][full_lines * CHUNKS:E].rearrange("(p f) -> p f", p=1)).then_inc(ids_loaded, 16)
            flat3 = A["edge_attr_3"].rearrange("e c -> (e c)")
            sp.dma_start(vec[0:full_rows].rearrange("p a c -> p (a c)"),
                         flat3[0:full_rows * 12 * P].rearrange("(p f) -> p f", f=12 * P)).then_inc(vec_loaded, 16)
            sp.dma_start(vec[full_rows:full_rows + 1, 0:tail, :].rearrange("p a c -> p (a c)"),
                         flat3[full_rows * 12 * P:3 * E].rearrange("(p f) -> p f", p=1)).then_inc(vec_loaded, 16)
            sp.wait_ge(ids_float, 2)
            for a in range(2):
                sp.dma_start(T["ids"][a, 0:EP].rearrange("(p f) -> p f", f=CHUNKS), flts[:, a, :]).then_inc(ids_stored, 16)
            sp.dma_start(T["ids"][1:2, EP:EP + P], flts[P - 1:P, 1, CHUNKS - P:CHUNKS]).then_inc(ids_stored, 16)
            sp.dma_start(T["ew"][0:1, :].rearrange("a (p f) -> (a p) f", f=CHUNKS), ew[:]).then_inc(ids_stored, 16)
            sp.wait_ge(ids_stored, 64)
            for tile, a, off in [(cur, 1, 0), (nxt, 1, 1), (srow, 0, 0)]:
                sp.dma_start(tile[0:rows].rearrange("p b i -> p (b i)"),
                             T["ids"][a, off:off + EP].rearrange("(p f) -> p f", f=4 * P)).then_inc(rows_loaded, 16)

        @block.scalar
        def _(act):
            names = ["L0_gnn_W", "L1_gnn_Wq", "L1_gnn_Wk", "L1_gnn_Wv", "L1_gnn_Wo"]
            for i, name in enumerate(names):
                act.dma_start(wts[:, i, :], A[name]).then_inc(w_loaded, 16)
            act.dma_start(K["w0"][:], A["L2_gnn_W0"]).then_inc(w_loaded, 16)
            act.dma_start(K["w1"][:], A["L2_gnn_W1"]).then_inc(w_loaded, 16)
            act.dma_start(K["wh"][:], A["L0_gnn_W"]).then_inc(w_loaded, 16)
            for tile, name in [(K["bias0"], "L0_gnn_bias"), (K["b0"], "L2_gnn_b0"), (K["b1"], "L2_gnn_b1"), (K["mb2"], "L3_gnn_mlp_b2")]:
                act.dma_start(tile[:], A[name].rearrange("(a d) -> a d", a=1).broadcast_to([P, D])).then_inc(w_loaded, 16)
            act.wait_ge(zeros_set, 1)
            att = A["L0_gnn_att"]
            for h in range(HEADS):
                for s in range(2):
                    act.dma_start(att8[h * HC:(h + 1) * HC, 4 * s + h:4 * s + h + 1],
                                  att[0, h, s * HC:(s + 1) * HC].rearrange("(c a) -> c a", a=1)).then_inc(small_loaded, 16)
            act.dma_start(K["m0"][0:NB, 0:64], A["L3_gnn_mlp_w0"]).then_inc(small_loaded, 16)
            act.dma_start(K["m1"][0:64, 0:64], A["L3_gnn_mlp_w1"]).then_inc(small_loaded, 16)
            act.dma_start(K["m2"][0:64, :], A["L3_gnn_mlp_w2"]).then_inc(small_loaded, 16)
            act.dma_start(K["mb0"][0:64, :], A["L3_gnn_mlp_b0"].rearrange("(c a) -> c a", a=1)).then_inc(small_loaded, 16)
            act.dma_start(K["mb1"][0:64, :], A["L3_gnn_mlp_b1"].rearrange("(c a) -> c a", a=1)).then_inc(small_loaded, 16)
            act.dma_start(T["up"], zeros[:, 0:D]).then_inc(up_built, 16)
            act.wait_ge(up_built, 16)
            act.dma_start(T["up"][0:MUL, 0:MUL], A["L3_gnn_W_up0"]).then_inc(up_built, 16)
            for c in range(3):
                act.dma_start(T["up"][MUL + c:D:3, MUL * (c + 1):MUL * (c + 2)], A["L3_gnn_W_up1"]).then_inc(up_built, 16)
            act.wait_ge(up_built, 80)
            act.dma_start(wts[:, 5, :], T["up"]).then_inc(small_loaded, 16)
            for q, (part, row) in enumerate([(0, 0), (0, MUL), (1, 0), (1, 0)]):
                name = ["L3_gnn_W_out0", "L3_gnn_W_out1"][part]
                act.dma_start(wo0[q * MUL:(q + 1) * MUL, 0, :], A[name][row:row + MUL, :]).then_inc(small_loaded, 16)
            for q, row in enumerate([0, MUL, MUL, MUL]):
                act.dma_start(wo0[q * MUL:(q + 1) * MUL, 1, :], A["L3_gnn_W_out1"][row:row + MUL, :]).then_inc(small_loaded, 16)
            agg = T["agg"]
            for s in range(NSUPER):
                b = min(s * SUPER, LAST)
                if s == NSUPER - 1:
                    act.wait_ge(agg_zeroed, 16 * s)
                act.dma_start(agg[b:b + SUPER, :].rearrange("(p g) d -> p (g d)", g=G), zeros[:]).then_inc(agg_zeroed, 16)
            act.wait_ge(sumsq_ready, 1)
            nc.scalar.activation(rnorm[:], sq[:, :, 0], ACT.Sqrt).then_inc(norm_ready, 1)
            act.wait_ge(agg_zeroed, 16 * NSUPER)

        N_SMALL = 2 * HEADS + 5 + 1 + 8

        @block.vector
        def _(dve):
            link = chain_of(dve, chain_v)
            dve.memset(ints[:, 0, :], PAD_ID)
            link(dve.memset(ints[:, 1, :], PAD_ID))
            dve.memset(ew[:], 0.0)
            link(dve.memset(vec[:], 0.0))
            dve.memset(att8[:], 0.0).then_inc(pads_set, 1)
            link(dve.memset(zeros[:], 0.0))
            dve.memset(K["m0"][:], 0.0)
            dve.memset(K["m1"][:], 0.0)
            dve.memset(K["m2"][:], 0.0)
            dve.memset(K["mb0"][:], 0.0)
            link(dve.memset(K["mb1"][:], 0.0))
            dve.memset(K["eps"][:], EPS).then_inc(zeros_set, 1)
            dve.wait_ge(ids_loaded, 96)
            dve.tensor_copy(flts[:, 0, :], ints[:, 0, :]).then_inc(ids_float, 1)
            dve.tensor_copy(flts[:, 1, :], ints[:, 1, :]).then_inc(ids_float, 1)
            dve.wait_ge(vec_loaded, 32)
            link(dve.tensor_tensor(sq[:], vec[:], vec[:], ALU.mult))
            link(dve.tensor_tensor(sq[:, :, 0], sq[:, :, 0], sq[:, :, 1], ALU.add))
            dve.tensor_tensor(sq[:, :, 0], sq[:, :, 0], sq[:, :, 2], ALU.add).then_inc(sumsq_ready, 1)
            dve.wait_ge(norm_ready, 1)
            link(dve.tensor_scalar(rnorm[:], rnorm[:], 1e-12, None, ALU.add))
            link(dve.reciprocal(rinv[:], rnorm[:]))
            for c in range(3):
                link(dve.tensor_tensor(rhatR[:, c].rearrange("p b i -> p (b i)"), vec[:, :, c], rinv[:], ALU.mult))
            dve.wait_ge(rows_loaded, 48)
            link(dve.memset(scat[:], 0.0))
            link(dve.tensor_tensor(scat[0:rows], cur[0:rows], nxt[0:rows], ALU.is_equal))
            link(dve.scalar_tensor_tensor(out=scat[0:rows], in0=scat[0:rows], scalar=float(NO_ROW), in1=cur[0:rows],
                                          op0=ALU.mult, op1=ALU.max))
            dve.sem_inc(chunkify, 1)
            blocks = [(cur, K["dstB"][:]), (scat, scatB[:]), (srow, srcB[:])] + \
                     [(rhatR[:, c], K["rhatB"][:, c, :]) for c in range(3)]
            for n, (_, out) in enumerate(blocks):
                dve.wait_ge(pe_done, n + 1)
                dve.tensor_copy(out.rearrange("p (r b) -> p b r", b=4), pt[:, :, 0:rows]).then_inc(pe_used, 1)
            dve.wait_ge(pe_used, len(blocks))
            for tile in (K["scat_idx"], K["src_idx"], K["dst_idx"]):
                link(dve.memset(tile[:], 0))
            dve.tensor_copy(K["scat_idx"][:, 0:CHUNKS], scatB[:])
            dve.tensor_scalar(K["src_idx"][:, 0:CHUNKS], srcB[:], float(N - 1), None, ALU.min)
            dve.tensor_scalar(K["dst_idx"][:, 0:CHUNKS], K["dstB"][:], float(N - 1), None, ALU.min)
            link(dve.memset(dshift[:], 0.0))
            dve.wait_ge(ident_ready, 1)
            link(dve.tensor_scalar(dshift[:, 1:CHUNKS], K["dstB"][:, 0:CHUNKS - 1], 1.0, K["ident"][:, P - 1:P], ALU.add, ALU.mult))
            link(dve.tensor_scalar(K["carry_key"][:], dshift[:], -1.0, None, ALU.add))
            dve.wait_ge(w_loaded, 16 * 12)
            dve.wait_ge(small_loaded, 16 * N_SMALL)
            dve.tensor_scalar(K["wup"][:], wts[:, 5, :], MUL ** -0.5, None, ALU.mult).then_inc(chunkify, 1)
            base = len(blocks)
            dve.wait_ge(pe_done, base + 1)
            dve.tensor_copy(wT[:, 0:4, :], pw[:]).then_inc(pe_used, 1)
            dve.wait_ge(pe_done, base + 2)
            dve.tensor_copy(K["wa"][:], pw2[:, 1, 0:8])
            dve.tensor_scalar(K["wqk"][:], pw2[:, 2, :], D ** -0.5, None, ALU.mult)
            dve.tensor_copy(K["wvo"][:], pw2[:, 3, :])
            s0 = (2 * MUL) ** -0.5 / AVG
            sv = s0 * 3.0 ** 0.5
            link(dve.memset(K["wout"][:], 0.0))
            vcols = K["wout"][:, :, MUL:].rearrange("p a (k c) -> p a k c", c=3)
            link(dve.tensor_scalar(K["wout"][0:64, 0, 0:MUL], wo0[0:64, 0, :], s0, None, ALU.mult))
            link(dve.tensor_scalar(vcols[64:96, 0, :, 0], wo0[64:96, 0, :], sv, None, ALU.mult))
            link(dve.tensor_scalar(vcols[96:128, 0, :, 1], wo0[96:128, 0, :], sv, None, ALU.mult))
            link(dve.tensor_scalar(vcols[0:32, 1, :, 2], wo0[0:32, 1, :], sv, None, ALU.mult))
            for c in range(3):
                q = 32 * (c + 1)
                link(dve.tensor_scalar(vcols[q:q + 32, 1, :, c], wo0[q:q + 32, 1, :], s0, None, ALU.mult))

        @block.tensor
        def _(pe):
            pe.wait_ge(ident_ready, 1)
            pe.wait_ge(chunkify, 1)
            n = 0
            for src in [cur, scat, srow, rhatR[:, 0], rhatR[:, 1], rhatR[:, 2]]:
                if n:
                    pe.wait_ge(pe_used, n)
                for b in range(4):
                    tr = nc.tensor.transpose(pt[:, b, :], src[:, b, :], K["ident"][:])
                tr.then_inc(pe_done, 1)
                n += 1
            pe.wait_ge(chunkify, 2)
            pe.wait_ge(w_loaded, 16 * 12)
            for i in range(4):
                tr = nc.tensor.transpose(pw[:, i, :], wts[:, i, :], K["ident"][:])
            tr.then_inc(pe_done, 1)
            pe.wait_ge(pe_used, n + 1)
            nc.tensor.matmul(pw2[:, 1, 0:8], wT[:, 0, :], att8[:], start=True, stop=True)
            nc.tensor.matmul(pw2[:, 2, :], wT[:, 1, :], wT[:, 2, :], start=True, stop=True)
            nc.tensor.matmul(pw2[:, 3, :], wT[:, 3, :], wts[:, 4, :], start=True, stop=True).then_inc(pe_done, 1)
    end_stage(nc, owned)




def sort_by_src(nc, A, T, K):
    with ExitStack() as ctx:
        sb, ps, sem, sems, owned = stage_makers(nc, ctx, "sort")
        rec = [sb(f"rec{i}", [P, 3, SORTF]) for i in range(2)]
        ints = sb("ints", [P, 2, SORTF], I32)
        place = sb("place", [P, SORTF], I32)
        gray = sb("gray", [P, SORTF], I32)
        bit = sb("bit", [P, SORTF], I32)
        sign = sb("sign", [P, SORTF])
        swap = sb("swap", [P, SORTF // 2])
        diff = sb("diff", [P, 2, SORTF // 2])
        turn = ps("turn", [P, 3, SORTF])
        chain_v = sem("chain_v")
        padded = sem("padded")
        loaded = sem("loaded")
        place_ready = sem("place_ready")
        records_ready = sem("records_ready")
        turned = sem("turned")
        sorted_ready = sem("sorted_ready")
        stored = sem("stored")
        full, tail = E // SORTF, E % SORTF
        block = ctx.enter_context(nc.Block())
        turns = []

        @block.gpsimd
        def _(pool):
            pool.iota(place[:], pattern=[[1, SORTF]], base=0, channel_multiplier=SORTF).then_inc(place_ready, 1)

        @block.vector
        def _(dve):
            link = chain_of(dve, chain_v)
            dve.memset(ints[:], PAD_ID).then_inc(padded, 1)
            dve.wait_ge(place_ready, 1)
            link(dve.tensor_scalar(gray[:], place[:], 1, None, ALU.logical_shift_right))
            dve.wait_ge(loaded, 64)
            dve.tensor_copy(rec[0][:, 0, :], ints[:, 0, :])
            dve.tensor_copy(rec[0][:, 1, :], place[:])
            link(dve.tensor_copy(rec[0][:, 2, :], ints[:, 1, :]))
            now = 0

            def flip_signs(bits, i):
                link(dve.tensor_scalar(bit[:], bits[:], i, 1, ALU.logical_shift_right, ALU.bitwise_and))
                link(dve.tensor_scalar(sign[:], bit[:], -2.0, 1.0, ALU.mult, ALU.add))
                link(dve.tensor_tensor(rec[now][:, 0, :], rec[now][:, 0, :], sign[:], ALU.mult))

            def exchange(now, step):
                a = rec[now][:].rearrange("p r (b two j) -> p r b two j", two=2, j=step)
                o = rec[1 - now][:].rearrange("p r (b two j) -> p r b two j", two=2, j=step)
                s = swap[:].rearrange("p (b j) -> p b j", j=step)
                d = diff[:].rearrange("p r (b j) -> p r b j", j=step)
                dve.tensor_tensor(s, a[:, 0, :, 0], a[:, 0, :, 1], ALU.is_gt)
                for r in (1, 2):
                    link(dve.tensor_tensor(d[:, r - 1], a[:, r, :, 1], a[:, r, :, 0], ALU.subtract))
                dve.tensor_tensor(o[:, 0, :, 0], a[:, 0, :, 0], a[:, 0, :, 1], ALU.min)
                dve.tensor_tensor(o[:, 0, :, 1], a[:, 0, :, 0], a[:, 0, :, 1], ALU.max)
                for r in (1, 2):
                    link(dve.tensor_tensor(d[:, r - 1], d[:, r - 1], s, ALU.mult))
                for r in (1, 2):
                    dve.tensor_tensor(o[:, r, :, 0], a[:, r, :, 0], d[:, r - 1], ALU.add)
                    link(dve.tensor_tensor(o[:, r, :, 1], a[:, r, :, 1], d[:, r - 1], ALU.subtract))

            def turn_blocks(now):
                turns.append(now)
                dve.sem_inc(records_ready, 1)
                dve.wait_ge(turned, len(turns))
                link(dve.tensor_copy(rec[1 - now][:], turn[:]))

            flip_signs(place, 1)
            link(dve.tensor_tensor(gray[:], gray[:], place[:], ALU.bitwise_xor))
            top = SORTN.bit_length() - 1
            inner = SORTF.bit_length() - 1
            for i in range(1, top + 1):
                if i > inner:
                    turn_blocks(now)
                    now = 1 - now
                    for j in range(i - 1, inner - 1, -1):
                        exchange(now, 1 << (j - inner))
                        now = 1 - now
                    turn_blocks(now)
                    now = 1 - now
                for j in range(min(i, inner) - 1, -1, -1):
                    exchange(now, 1 << j)
                    now = 1 - now
                if i < top:
                    flip_signs(gray, i)
            dve.sem_inc(sorted_ready, 1 + now)

        @block.tensor
        def _(pe):
            for n, now in enumerate(turns):
                pe.wait_ge(records_ready, n + 1)
                for r in range(3):
                    for b in range(SORTF // P):
                        tr = nc.tensor.transpose(turn[:, r, b * P:(b + 1) * P], rec[now][:, r, b * P:(b + 1) * P], K["ident"][:])
                tr.then_inc(turned, 1)

        @block.sync
        def _(sp):
            sp.wait_ge(padded, 1)
            for a, name in enumerate(["src", "dst"]):
                sp.dma_start(ints[0:full, a, :], A[name][0:full * SORTF].rearrange("(p f) -> p f", f=SORTF)).then_inc(loaded, 16)
                sp.dma_start(ints[full:full + 1, a, 0:tail],
                             A[name][full * SORTF:E].rearrange("(p f) -> p f", p=1)).then_inc(loaded, 16)
            exchanges = 136
            now = (exchanges + len(turns)) % 2
            sp.wait_ge(sorted_ready, 1 + now)
            for r in range(3):
                sp.dma_start(T["sorted"][r].rearrange("(p f) -> p f", f=SORTF), rec[now][:, r, :]).then_inc(stored, 16)
            sp.wait_ge(stored, 48)
    end_stage(nc, owned)




def segment_tiles(sb, name, heads):
    seg = {"heads": heads}
    for tile in ("cont", "negcont", "nxt", "pre", "negpre", "suf", "last", "work"):
        seg[tile] = sb(f"{name}_{tile}", [P, CHUNKS])
    for row in ("first", "end", "full", "link", "neglink", "a", "nega", "arev", "linkn", "b", "c"):
        seg["r_" + row] = sb(f"{name}_r_{row}", [heads, P])
    seg["ccol"] = sb(f"{name}_ccol", [P, heads])
    seg["fullcol"] = sb(f"{name}_fullcol", [P, 1])
    return seg


def turner_of(sb, ps, sem):
    return {"scr": sb("turn_scr", [P, P]), "out": ps("turn_out", [P, P]), "ready": sem("turn_ready"),
            "done": sem("turn_done"), "turns": []}


def turn_by_vector(dve, turner, write):
    write(turner["scr"]).then_inc(turner["ready"], 1)
    turner["turns"].append(1)
    dve.wait_ge(turner["done"], len(turner["turns"]))


def turn_by_tensor(pe, turner, ident):
    for n in range(len(turner["turns"])):
        pe.wait_ge(turner["ready"], n + 1)
        pe.transpose(turner["out"][:], turner["scr"][:], ident[:]).then_inc(turner["done"], 1)


def find_segments(dve, link, turner, seg, ids):
    F, H, R = CHUNKS, seg["heads"], P
    link(dve.memset(seg["cont"][:, 0:1], 0.0))
    link(dve.tensor_tensor(seg["cont"][:, 1:F], ids[:, 1:F], ids[:, 0:F - 1], ALU.is_equal))
    link(dve.memset(seg["nxt"][:, F - 1:F], 0.0))
    link(dve.tensor_copy(seg["nxt"][:, 0:F - 1], seg["cont"][:, 1:F]))
    link(dve.tensor_scalar(seg["negcont"][:], seg["cont"][:], -1.0, BIG, ALU.add, ALU.mult))
    link(dve.tensor_scalar(seg["pre"][:], ids, ids[:, 0:1], None, ALU.is_equal))
    link(dve.tensor_scalar(seg["negpre"][:], seg["pre"][:], -1.0, BIG, ALU.add, ALU.mult))
    link(dve.tensor_scalar(seg["suf"][:], ids, ids[:, F - 1:F], None, ALU.is_equal))
    link(dve.tensor_tensor(seg["fullcol"][:], ids[:, 0:1], ids[:, F - 1:F], ALU.is_equal))
    for col, row in [(ids[:, 0:1], seg["r_first"]), (ids[:, F - 1:F], seg["r_end"]), (seg["fullcol"][:], seg["r_full"])]:
        turn_by_vector(dve, turner, lambda scr: dve.tensor_copy(scr[:, 0:H], col.broadcast_to([P, H])))
        link(dve.tensor_copy(row[:], turner["out"][0:H, :]))
    link(dve.memset(seg["r_link"][:], 0.0))
    link(dve.tensor_tensor(seg["r_link"][:, 1:R], seg["r_first"][:, 1:R], seg["r_end"][:, 0:R - 1], ALU.is_equal))
    link(dve.tensor_scalar(seg["r_neglink"][:], seg["r_link"][:], -1.0, BIG, ALU.add, ALU.mult))
    link(dve.memset(seg["r_a"][:], 0.0))
    link(dve.tensor_tensor(seg["r_a"][:, 1:R], seg["r_link"][:, 1:R], seg["r_full"][:, 0:R - 1], ALU.mult))
    link(dve.tensor_scalar(seg["r_nega"][:], seg["r_a"][:], -1.0, BIG, ALU.add, ALU.mult))
    link(dve.memset(seg["r_linkn"][:], 0.0))
    link(dve.tensor_copy(seg["r_linkn"][:, 0:R - 1], seg["r_link"][:, 1:R]))
    link(dve.memset(seg["r_arev"][:], 0.0))
    link(dve.tensor_tensor(seg["r_arev"][:, 0:R - 1], seg["r_linkn"][:, 0:R - 1], seg["r_full"][:, 1:R], ALU.mult))
    turn_by_vector(dve, turner, lambda scr: dve.tensor_copy(scr[0:H, :], seg["r_linkn"][:]))
    link(dve.tensor_copy(seg["last"][:], seg["nxt"][:]))
    link(dve.tensor_copy(seg["last"][:, F - 1:F], turner["out"][:, 0:1]))
    link(dve.tensor_scalar(seg["last"][:], seg["last"][:], -1.0, 1.0, ALU.mult, ALU.add))


def segment_scan(dve, link, turner, seg, kind, outs, ins):
    F, H, R = CHUNKS, len(outs), P
    for out, v in zip(outs, ins):
        if kind == "sum":
            link(dve.tensor_tensor_scan(out, seg["cont"][:], v, 0.0, ALU.mult, ALU.add))
        elif kind == "max":
            link(dve.tensor_tensor_scan(out, seg["negcont"][:], v, -BIG, ALU.add, ALU.max))
        else:
            link(dve.tensor_tensor(seg["work"][:], seg["last"][:], v, ALU.mult))
            link(dve.tensor_tensor_scan(out[:, ::-1], seg["nxt"][:, ::-1], seg["work"][:, ::-1], 0.0, ALU.mult, ALU.add))
    end = 0 if kind == "fill" else F - 1
    for h, out in enumerate(outs):
        link(dve.tensor_copy(turner["scr"][:, h:h + 1], out[:, end:end + 1]))
    turn_by_vector(dve, turner, lambda scr: dve.tensor_copy(scr[:, H - 1:H], outs[H - 1][:, end:end + 1]))
    ends, b, c = turner["out"][0:H, :], seg["r_b"][0:H, :], seg["r_c"][0:H, :]
    if kind == "sum":
        link(dve.memset(b[:, 0:1], 0.0))
        link(dve.tensor_tensor(b[:, 1:R], seg["r_link"][0:H, 1:R], ends[:, 0:R - 1], ALU.mult))
        link(dve.tensor_tensor_scan(c, seg["r_a"][0:H, :], b, 0.0, ALU.mult, ALU.add))
    elif kind == "max":
        link(dve.memset(b[:, 0:1], -BIG))
        link(dve.tensor_tensor(b[:, 1:R], seg["r_neglink"][0:H, 1:R], ends[:, 0:R - 1], ALU.add))
        link(dve.tensor_tensor_scan(c, seg["r_nega"][0:H, :], b, -BIG, ALU.add, ALU.max))
    else:
        link(dve.memset(b[:, R - 1:R], 0.0))
        link(dve.tensor_tensor(b[:, 0:R - 1], seg["r_linkn"][0:H, 0:R - 1], ends[:, 1:R], ALU.mult))
        link(dve.tensor_tensor_scan(c[:, ::-1], seg["r_arev"][0:H, ::-1], b[:, ::-1], 0.0, ALU.mult, ALU.add))
    turn_by_vector(dve, turner, lambda scr: dve.tensor_copy(scr[0:H, :], c))
    link(dve.tensor_copy(seg["ccol"][:, 0:H], turner["out"][:, 0:H]))
    for h, out in enumerate(outs):
        carried = seg["ccol"][:, h:h + 1]
        if kind == "sum":
            link(dve.scalar_tensor_tensor(out=out, in0=seg["pre"][:], scalar=carried, in1=out, op0=ALU.mult, op1=ALU.add))
        elif kind == "max":
            link(dve.scalar_tensor_tensor(out=out, in0=seg["negpre"][:], scalar=carried, in1=out, op0=ALU.add, op1=ALU.max))
        else:
            link(dve.scalar_tensor_tensor(out=out, in0=seg["suf"][:], scalar=carried, in1=out, op0=ALU.mult, op1=ALU.add))




def node_scores(nc, A, T, K):
    with ExitStack() as ctx:
        sb, ps, sem, sems, owned = stage_makers(nc, ctx, "nsc")
        x = [sb(f"x{h}", [P, G, D]) for h in range(2)]
        xT = [sb(f"xT{h}", [P, G, P]) for h in range(2)]
        s = [sb(f"s{h}", [P, G, 8]) for h in range(2)]
        tp = [ps(f"tp{h}", [P, G, P]) for h in range(2)]
        sp_ = [ps(f"sp{h}", [P, G, 64]) for h in range(2)]
        loaded, turned, copied = sems("loaded"), sems("turned"), sems("copied")
        scored, taken, stored = sems("scored"), sems("taken"), sems("stored")
        block = ctx.enter_context(nc.Block())

        @block.sync
        def _(sp):
            def load(t, h):
                wait_for(sp, turned[h], t)
                sp.dma_start(x[h][:], node_rows(A["x"], t, h)).then_inc(loaded[h], 16)
            node_loop(sp, load)

        @block.tensor
        def _(pe):
            def turn(t, h):
                pe.wait_ge(loaded[h], 16 * t + 16)
                wait_for(pe, copied[h], t)
                for g in range(G):
                    tr = pe.transpose(tp[h][:, g, :], x[h][:, g, :], K["ident"][:])
                tr.then_inc(turned[h], 1)

            def score(t, h):
                pe.wait_ge(copied[h], t + 1)
                wait_for(pe, taken[h], t)
                for g in range(G):
                    mm = pe.matmul(sp_[h][:, g, 0:8], xT[h][:, g, :], K["wa"][:], start=True, stop=True)
                mm.then_inc(scored[h], 1)

            def step(t, h):
                turn(t, h)
                if h == 1:
                    score(t, 0)
                    score(t, 1)
            node_loop(pe, step)

        @block.scalar
        def _(act):
            def copy(t, h):
                act.wait_ge(turned[h], t + 1)
                wait_for(act, scored[h], t)
                nc.scalar.copy(xT[h][:], tp[h][:]).then_inc(copied[h], 1)
            node_loop(act, copy)

        @block.vector
        def _(dve):
            def take(t, h):
                dve.wait_ge(scored[h], t + 1)
                wait_for(dve, stored[h], 16 * t)
                dve.tensor_copy(s[h][:], sp_[h][:, :, 0:8]).then_inc(taken[h], 1)
            node_loop(dve, take)

        @block.gpsimd
        def _(pool):
            def store(t, h):
                pool.wait_ge(taken[h], t + 1)
                if isinstance(t, int) and t == NLOOPS - 1 and h == 1:
                    pool.wait_ge(stored[0], 16 * t + 16)
                pool.nop(nofuse=True)
                pool.dma_start(node_rows(T["scores"], t, h), s[h][:]).then_inc(stored[h], 16)
            node_loop(pool, store)
            for h in range(2):
                pool.wait_ge(stored[h], 16 * NLOOPS)
    end_stage(nc, owned)


def edge_loop(engine, body):
    for h in range(2):
        body(0, h)
    with engine.Fori(1, LOOPS) as t:
        for h in range(2):
            body(t, h)


def four(tile, t, h):
    return tile[:, bass.ds(8 * t + 4 * h, 4)]


def gat_softmax(nc, A, T, K):
    with ExitStack() as ctx:
        sb, ps, sem, sems, owned = stage_makers(nc, ctx, "gsm")
        rec = sb("rec", [P, 3, CHUNKS])
        src_idx = sb("src_idx", [P, CHUNKS + 8], I32)
        dst_idx = sb("dst_idx", [P, CHUNKS + 8], I32)
        edge_idx = sb("edge_idx", [P, CHUNKS + 8], I32)
        ring = [sb(f"ring{h}", [P, 3, 4], I32) for h in range(2)]
        row_s = [sb(f"row_s{h}", [P, 4, 8]) for h in range(2)]
        row_d = [sb(f"row_d{h}", [P, 4, 8]) for h in range(2)]
        row_o = [sb(f"row_o{h}", [P, 4, HEADS]) for h in range(2)]
        al = sb("al", [P, HEADS, CHUNKS])
        mx = sb("mx", [P, HEADS, CHUNKS])
        tot = sb("tot", [P, HEADS + 1, CHUNKS])
        run = sb("run", [P, HEADS + 1, CHUNKS])
        seg = segment_tiles(sb, "src", HEADS + 1)
        turner = turner_of(sb, ps, sem)
        loaded, ring_ready, gathered = sem("loaded"), sems("ring_ready"), sems("gathered")
        rows_used, chain_v = sems("rows_used"), sem("chain_v")
        shifted, ex_ready = sem("shifted"), sem("ex_ready")
        out_ready, scattered = sems("out_ready"), sems("scattered")
        block = ctx.enter_context(nc.Block())

        @block.sync
        def _(sp):
            for r in range(3):
                sp.dma_start(rec[:, r, :], T["sorted"][r, 0:EP].rearrange("(p f) -> p f", f=CHUNKS)).then_inc(loaded, 16)

        @block.vector
        def _(dve):
            link = chain_of(dve, chain_v)
            for tile in (src_idx, dst_idx, edge_idx):
                link(dve.memset(tile[:], 0))
            link(dve.memset(turner["scr"][:], 0.0))
            dve.wait_ge(loaded, 48)
            dve.tensor_scalar(src_idx[:, 0:CHUNKS], rec[:, 0, :], float(N - 1), None, ALU.min)
            dve.tensor_copy(edge_idx[:, 0:CHUNKS], rec[:, 1, :])
            link(dve.tensor_scalar(dst_idx[:, 0:CHUNKS], rec[:, 2, :], float(N - 1), None, ALU.min))

            def fill_ring(t, h):
                dve.tensor_copy(ring[h][:, 0, :], four(src_idx, t, h))
                dve.tensor_copy(ring[h][:, 1, :], four(dst_idx, t, h)).then_inc(ring_ready[h], 1)

            def take_rows(t, h):
                dve.wait_ge(gathered[h], 128 * t + 128)
                dve.tensor_tensor(al[:, :, bass.ds(8 * t + 4 * h, 4)], row_s[h][:, :, 0:HEADS].rearrange("p j h -> p h j"),
                                  row_d[h][:, :, HEADS:8].rearrange("p j h -> p h j"), ALU.add).then_inc(rows_used[h], 1)
                fill_ring(t + 1, h)

            fill_ring(0, 0)
            fill_ring(0, 1)
            edge_loop(dve, take_rows)
            for h in range(2):
                dve.wait_ge(rows_used[h], LOOPS)
            link(dve.scalar_tensor_tensor(out=al[:], in0=al[:], scalar=0.2, in1=al[:], op0=ALU.mult, op1=ALU.max))
            find_segments(dve, link, turner, seg, rec[:, 0, :])
            heads = range(HEADS)
            segment_scan(dve, link, turner, seg, "max", [run[:, h, :] for h in heads], [al[:, h, :] for h in heads])
            segment_scan(dve, link, turner, seg, "fill", [mx[:, h, :] for h in heads], [run[:, h, :] for h in heads])
            link(dve.tensor_scalar(mx[:], mx[:], 0.0, None, ALU.max))
            dve.tensor_tensor(al[:], al[:], mx[:], ALU.subtract).then_inc(shifted, 1)
            dve.wait_ge(ex_ready, 2)
            link(dve.memset(tot[:, HEADS, :], 1.0))
            each = range(HEADS + 1)
            segment_scan(dve, link, turner, seg, "sum", [run[:, h, :] for h in each],
                         [al[:, h, :] for h in heads] + [tot[:, HEADS, :]])
            segment_scan(dve, link, turner, seg, "fill", [tot[:, h, :] for h in each], [run[:, h, :] for h in each])
            link(dve.tensor_scalar(seg["work"][:], tot[:, HEADS, :], -1.0, float(E), ALU.mult, ALU.add))
            for h in heads:
                link(dve.tensor_tensor(mx[:, h, :], mx[:, h, :], seg["work"][:], ALU.mult))
            link(dve.tensor_tensor(tot[:, 0:HEADS, :], tot[:, 0:HEADS, :], mx[:], ALU.add))
            link(dve.reciprocal(mx[:], tot[:, 0:HEADS, :]))
            link(dve.tensor_tensor(al[:], al[:], mx[:], ALU.mult))

            def give_rows(t, h):
                wait_for(dve, scattered[h], 64 * t)
                dve.tensor_copy(row_o[h][:], al[:, :, bass.ds(8 * t + 4 * h, 4)].rearrange("p h j -> p j h"))
                dve.tensor_copy(ring[h][:, 2, :], four(edge_idx, t, h)).then_inc(out_ready[h], 1)
            edge_loop(dve, give_rows)

        @block.scalar
        def _(act):
            act.wait_ge(shifted, 1)
            nc.scalar.activation(al[:], al[:], ACT.Exp).then_inc(ex_ready, 1)
            nc.scalar.activation(mx[:], mx[:], ACT.Exp, scale=-1.0).then_inc(ex_ready, 1)

        @block.tensor
        def _(pe):
            turn_by_tensor(pe, turner, K["ident"])

        @block.gpsimd
        def _(pool):
            def gather(t, h):
                pool.wait_ge(ring_ready[h], t + 1)
                wait_for(pool, rows_used[h], t)
                pool.nop(nofuse=True)
                for j in range(4):
                    pool.indirect_dma_start(row_s[h][:, j, :], None, T["scores"],
                                            bass.IndirectOffsetOnAxis(ring[h][:, 0, j:j + 1], 0)).then_inc(gathered[h], 16)
                    pool.indirect_dma_start(row_d[h][:, j, :], None, T["scores"],
                                            bass.IndirectOffsetOnAxis(ring[h][:, 1, j:j + 1], 0)).then_inc(gathered[h], 16)

            def scatter(t, h):
                pool.wait_ge(out_ready[h], t + 1)
                pool.nop(nofuse=True)
                for j in range(4):
                    pool.indirect_dma_start(T["alpha"], bass.IndirectOffsetOnAxis(ring[h][:, 2, j:j + 1], 0),
                                            row_o[h][:, j, :], None).then_inc(scattered[h], 16)
            edge_loop(pool, gather)
            edge_loop(pool, scatter)
            for h in range(2):
                pool.wait_ge(scattered[h], 64 * LOOPS)
    end_stage(nc, owned)


def gat_sums(nc, A, T, K):
    with ExitStack() as ctx:
        sb, ps, sem, sems, owned = stage_makers(nc, ctx, "gsu")
        ids = K["ids"]
        raw = sb("raw", [P, CHUNKS, HEADS])
        v = sb("v", [P, HEADS + 1, CHUNKS])
        run = sb("run", [P, HEADS + 1, CHUNKS])
        idx = sb("idx", [P, CHUNKS], I32)
        fidx = sb("fidx", [P, CHUNKS])
        ring = [sb(f"ring{h}", [P, 4], I32) for h in range(2)]
        row_o = [sb(f"row_o{h}", [P, 4, 8]) for h in range(2)]
        zero = sb("zero", [P, SUPER])
        turner = turner_of(sb, ps, sem)
        loaded, chain_v, zeroed, zero_set = sem("loaded"), sem("chain_v"), sem("zeroed"), sem("zero_set")
        out_ready, scattered = sems("out_ready"), sems("scattered")
        raw_zero = sem("raw_zero")
        block = ctx.enter_context(nc.Block())
        width = N * 8 // P
        cuts = list(range(0, width, SUPER)) + [width]

        @block.sync
        def _(sp):
            sp.dma_start(ids[:], T["ids"][1, 0:EP].rearrange("(p f) -> p f", f=CHUNKS)).then_inc(loaded, 16)
            full, tail = E // CHUNKS, E % CHUNKS
            sp.wait_ge(raw_zero, 1)
            sp.dma_start(raw[0:full].rearrange("p f h -> p (f h)"),
                         T["alpha"][0:full * CHUNKS, :].rearrange("(p f) h -> p (f h)", f=CHUNKS)).then_inc(loaded, 16)
            sp.dma_start(raw[full:full + 1, 0:tail].rearrange("p f h -> p (f h)"),
                         T["alpha"][full * CHUNKS:E, :].rearrange("(p f) h -> p (f h)", p=1)).then_inc(loaded, 16)
            sp.wait_ge(zero_set, 1)
            flat = T["nodes"].rearrange("n w -> (n w)").rearrange("(p f) -> p f", p=P)
            for a, b in zip(cuts, cuts[1:]):
                sp.dma_start(flat[:, a:b], zero[:, 0:b - a]).then_inc(zeroed, 16)

        @block.vector
        def _(dve):
            link = chain_of(dve, chain_v)
            dve.memset(zero[:], 0.0).then_inc(zero_set, 1)
            dve.memset(raw[:], 0.0).then_inc(raw_zero, 1)
            link(dve.memset(turner["scr"][:], 0.0))
            link(dve.memset(v[:, HEADS, :], 1.0))
            for h in range(2):
                link(dve.memset(row_o[h][:], 0.0))
            dve.wait_ge(loaded, 48)
            link(dve.tensor_copy(v[:, 0:HEADS, :], raw[:].rearrange("p f h -> p h f")))
            find_segments(dve, link, turner, K["seg"], ids[:])
            each = range(HEADS + 1)
            segment_scan(dve, link, turner, K["seg"], "sum", [run[:, h, :] for h in each], [v[:, h, :] for h in each])
            link(dve.tensor_scalar(fidx[:], K["seg"]["last"][:], -float(NO_ROW), float(NO_ROW), ALU.mult, ALU.add))
            link(dve.tensor_tensor(fidx[:], fidx[:], ids[:], ALU.max))
            link(dve.tensor_copy(idx[:], fidx[:]))

            def give_rows(t, h):
                wait_for(dve, scattered[h], 64 * t)
                dve.tensor_copy(row_o[h][:, :, 0:HEADS + 1], run[:, :, bass.ds(8 * t + 4 * h, 4)].rearrange("p h j -> p j h"))
                dve.tensor_copy(ring[h][:], four(idx, t, h)).then_inc(out_ready[h], 1)
            edge_loop(dve, give_rows)

        @block.tensor
        def _(pe):
            turn_by_tensor(pe, turner, K["ident"])

        @block.gpsimd
        def _(pool):
            pool.wait_ge(zeroed, 16 * (len(cuts) - 1))

            def scatter(t, h):
                pool.wait_ge(out_ready[h], t + 1)
                pool.nop(nofuse=True)
                for j in range(4):
                    pool.indirect_dma_start(T["nodes"], bass.IndirectOffsetOnAxis(ring[h][:, j:j + 1], 0), row_o[h][:, j, :],
                                            None, bounds_check=N - 1, oob_is_err=False).then_inc(scattered[h], 16)
            edge_loop(pool, scatter)
            for h in range(2):
                pool.wait_ge(scattered[h], 64 * LOOPS)
    end_stage(nc, owned)




def over_rows(vector):
    return vector[:].unsqueeze(1).broadcast_to([P, G, D])


def over_columns(scalars):
    return scalars.unsqueeze(2).broadcast_to([P, G, D])


def norm_of(sb, sems, eps, y, o, weight=None):
    norm = {"y": y, "o": o, "eps": eps, "weight": weight}
    for name, shape in [("stats", [P, G, 6]), ("diff", [P, G]), ("mv", [P, G, 2]), ("sd", [P, G]), ("rs", [P, G]), ("nb", [P, G])]:
        norm[name] = [sb(f"{name}{h}", shape) for h in range(2)]
    for name in ("stats_ready", "root_ready", "scale_ready", "normed", "chain", "weighted"):
        norm[name] = sems(f"norm_{name}")
    return norm


def norm_measure(norm, dve, t, h):
    for g in range(G):
        bn = dve.bn_stats(norm["stats"][h][:, g, :], norm["y"][h][:, g, :])
    bn.then_inc(norm["chain"][h], 1)
    dve.wait_ge(norm["chain"][h], 4 * t + 1)
    even, odd = norm["stats"][h][:, :, 0:3], norm["stats"][h][:, :, 3:6]
    dve.tensor_tensor(norm["diff"][h][:], even[:, :, 1], odd[:, :, 1], ALU.subtract)
    dve.tensor_tensor(norm["mv"][h][:, :, 0], even[:, :, 1], odd[:, :, 1], ALU.add)
    dve.tensor_tensor(norm["mv"][h][:, :, 1], even[:, :, 2], odd[:, :, 2], ALU.add).then_inc(norm["chain"][h], 1)
    dve.wait_ge(norm["chain"][h], 4 * t + 2)
    dve.scalar_tensor_tensor(out=norm["diff"][h][:], in0=norm["diff"][h][:], scalar=D / 4.0, in1=norm["diff"][h][:],
                             op0=ALU.mult, op1=ALU.mult).then_inc(norm["chain"][h], 1)
    dve.wait_ge(norm["chain"][h], 4 * t + 3)
    dve.tensor_tensor(norm["mv"][h][:, :, 1], norm["mv"][h][:, :, 1], norm["diff"][h][:], ALU.add).then_inc(norm["stats_ready"][h], 1)


def norm_root(norm, act, t, h):
    act.wait_ge(norm["stats_ready"][h], t + 1)
    act.activation(norm["sd"][h][:], norm["mv"][h][:, :, 1], ACT.Sqrt, bias=norm["eps"][:, 0:1], scale=1.0 / D).then_inc(norm["root_ready"][h], 1)


def norm_scale(norm, dve, t, h):
    dve.wait_ge(norm["root_ready"][h], t + 1)
    wait_for(dve, norm["normed"][h], t)
    dve.reciprocal(norm["rs"][h][:], norm["sd"][h][:]).then_inc(norm["chain"][h], 1)
    dve.wait_ge(norm["chain"][h], 4 * t + 4)
    if norm["weight"] is not None:
        w = norm["weight"][:, bass.ds(2 * t + h, 1), :].rearrange("p a g -> p (a g)")
        dve.tensor_tensor(norm["rs"][h][:], norm["rs"][h][:], w, ALU.mult).then_inc(norm["weighted"][h], 1)
        dve.wait_ge(norm["weighted"][h], t + 1)
    dve.scalar_tensor_tensor(out=norm["nb"][h][:], in0=norm["mv"][h][:, :, 0], scalar=-0.5, in1=norm["rs"][h][:],
                             op0=ALU.mult, op1=ALU.mult).then_inc(norm["scale_ready"][h], 1)


def norm_apply(norm, act, t, h, stored):
    act.wait_ge(norm["scale_ready"][h], t + 1)
    wait_for(act, stored[h], 16 * t)
    for g in range(G):
        ac = act.activation(norm["o"][h][:, g, :], norm["y"][h][:, g, :], ACT.Identity,
                            bias=norm["nb"][h][:, g:g + 1], scale=norm["rs"][h][:, g:g + 1])
    ac.then_inc(norm["normed"][h], 1)


def store_nodes(pool, table, tiles, ready, stored):
    def store(t, h):
        pool.wait_ge(ready[h], t + 1)
        if isinstance(t, int) and t == NLOOPS - 1 and h == 1:
            pool.wait_ge(stored[0], 16 * t + 16)
        pool.nop(nofuse=True)
        pool.dma_start(node_rows(table, t, h), tiles[h][:]).then_inc(stored[h], 16)
    node_loop(pool, store)
    for h in range(2):
        pool.wait_ge(stored[h], 16 * NLOOPS)


def load_nodes(sp, pairs, used, loaded):
    def load(t, h):
        wait_for(sp, used[h], t)
        for tiles, table in pairs:
            sp.dma_start(tiles[h][:], node_rows(table, t, h)).then_inc(loaded[h], 16)
    node_loop(sp, load)


def both_halves(*parts):
    def step(t, h):
        if h == 1:
            for part in parts:
                part(t, 0)
                part(t, 1)
    return step


def first_layer(nc, A, T, K):
    with ExitStack() as ctx:
        sb, ps, sem, sems, owned = stage_makers(nc, ctx, "l0")
        x = [sb(f"x{h}", [P, G, D]) for h in range(2)]
        nodes = [sb(f"nodes{h}", [P, G, 8]) for h in range(2)]
        xT = [sb(f"xT{h}", [P, G, P]) for h in range(2)]
        y = [sb(f"y{h}", [P, G, D]) for h in range(2)]
        o = [sb(f"o{h}", [P, G, D]) for h in range(2)]
        tp = [ps(f"tp{h}", [P, G, P]) for h in range(2)]
        hp = [ps(f"hp{h}", [P, G, D]) for h in range(2)]
        loaded, turned, copied, multiplied = sems("loaded"), sems("turned"), sems("copied"), sems("multiplied")
        used, stored, chain = sems("used"), sems("stored"), sems("chain")
        degrees, roots = sem("degrees"), sem("roots")
        norm = norm_of(sb, sems, K["eps"], y, o)
        block = ctx.enter_context(nc.Block())

        @block.sync
        def _(sp):
            load_nodes(sp, [(x, A["x"]), (nodes, T["nodes"])], used, loaded)

        @block.tensor
        def _(pe):
            def turn(t, h):
                pe.wait_ge(loaded[h], 32 * t + 32)
                wait_for(pe, copied[h], t)
                for g in range(G):
                    tr = pe.transpose(tp[h][:, g, :], x[h][:, g, :], K["ident"][:])
                tr.then_inc(turned[h], 1)

            def multiply(t, h):
                pe.wait_ge(copied[h], t + 1)
                wait_for(pe, used[h], t)
                for g in range(G):
                    mm = pe.matmul(hp[h][:, g, :], xT[h][:, g, :], K["wh"][:], start=True, stop=True)
                mm.then_inc(multiplied[h], 1)
            node_loop(pe, both_halves(turn, multiply))

        @block.scalar
        def _(act):
            def copy(t, h):
                act.wait_ge(turned[h], t + 1)
                wait_for(act, multiplied[h], t)
                act.copy(xT[h][:], tp[h][:]).then_inc(copied[h], 1)
            node_loop(act, both_halves(copy, lambda t, h: norm_root(norm, act, t, h), lambda t, h: norm_apply(norm, act, t, h, stored)))
            act.wait_ge(degrees, NSUPER)
            act.activation(K["dsqrt"][:], K["deg"][:], ACT.Sqrt).then_inc(roots, 1)

        @block.vector
        def _(dve):
            def add(t, h):
                link = loop_chain_of(dve, chain[h], t, 3)
                dve.wait_ge(multiplied[h], t + 1)
                wait_for(dve, norm["normed"][h], t)
                link(dve.tensor_tensor(y[h][:].rearrange("p g (a c) -> p g a c", a=HEADS),
                                       hp[h][:].rearrange("p g (a c) -> p g a c", a=HEADS),
                                       nodes[h][:, :, 0:HEADS].unsqueeze(3).broadcast_to([P, G, HEADS, HC]), ALU.mult))
                dve.tensor_scalar(K["deg"][:, bass.ds(2 * t + h, 1), :], nodes[h][:, :, HEADS:HEADS + 1].rearrange("p g a -> p a g"),
                                  1.0, None, ALU.add).then_inc(degrees, 1)
                link(dve.tensor_tensor(y[h][:], y[h][:], x[h][:], ALU.add))
                dve.sem_inc(used[h], 1)
                link(dve.tensor_tensor(y[h][:], y[h][:], over_rows(K["bias0"]), ALU.add))
                norm_measure(norm, dve, t, h)
            node_loop(dve, both_halves(add, lambda t, h: norm_scale(norm, dve, t, h)))
            dve.wait_ge(roots, 1)
            dve.reciprocal(K["dinv"][:], K["dsqrt"][:])

        @block.gpsimd
        def _(pool):
            store_nodes(pool, T["x1"], o, norm["normed"], stored)
    end_stage(nc, owned)


def residual_norm(nc, K, name, x_table, factor, agg_table, out_table, weight=None):
    with ExitStack() as ctx:
        sb, ps, sem, sems, owned = stage_makers(nc, ctx, name)
        x = [sb(f"x{h}", [P, G, D]) for h in range(2)]
        agg = [sb(f"agg{h}", [P, G, D]) for h in range(2)]
        y = [sb(f"y{h}", [P, G, D]) for h in range(2)]
        o = [sb(f"o{h}", [P, G, D]) for h in range(2)]
        loaded, used, stored = sems("loaded"), sems("used"), sems("stored")
        norm = norm_of(sb, sems, K["eps"], y, o, weight)
        block = ctx.enter_context(nc.Block())

        @block.sync
        def _(sp):
            load_nodes(sp, [(x, x_table), (agg, agg_table)], used, loaded)

        @block.vector
        def _(dve):
            def add(t, h):
                dve.wait_ge(loaded[h], 32 * t + 32)
                wait_for(dve, norm["normed"][h], t)
                dve.scalar_tensor_tensor(out=y[h][:], in0=x[h][:], scalar=factor, in1=agg[h][:],
                                         op0=ALU.mult, op1=ALU.add).then_inc(used[h], 1)
                dve.wait_ge(used[h], t + 1)
                norm_measure(norm, dve, t, h)
            node_loop(dve, both_halves(add, lambda t, h: norm_scale(norm, dve, t, h)))

        @block.scalar
        def _(act):
            node_loop(act, both_halves(lambda t, h: norm_root(norm, act, t, h), lambda t, h: norm_apply(norm, act, t, h, stored)))

        @block.gpsimd
        def _(pool):
            store_nodes(pool, out_table, o, norm["normed"], stored)
    end_stage(nc, owned)


def second_norm(nc, A, T, K):
    residual_norm(nc, K, "n1", T["x1"], 2.0, T["agg"], T["z2"], K["dinv"])


def final_layer(nc, A, T, K, out):
    residual_norm(nc, K, "n3", T["x3"], 1.0, T["agg"], out)


def gcn_nodes(nc, K, name, z_table, weight, bias, agg_table, out_table, x_table=None):
    normed = x_table is not None
    with ExitStack() as ctx:
        sb, ps, sem, sems, owned = stage_makers(nc, ctx, name)
        z = [sb(f"z{h}", [P, G, D]) for h in range(2)]
        agg = [sb(f"agg{h}", [P, G, D]) for h in range(2)]
        uT = [sb(f"uT{h}", [P, G, P]) for h in range(2)]
        y = [sb(f"y{h}", [P, G, D]) for h in range(2)]
        x = [sb(f"x{h}", [P, G, D]) for h in range(2)] if normed else None
        o = [sb(f"o{h}", [P, G, D]) for h in range(2)] if normed else y
        tp = [ps(f"tp{h}", [P, G, P]) for h in range(2)]
        hp = [ps(f"hp{h}", [P, G, D]) for h in range(2)]
        loaded, summed, turned, copied = sems("loaded"), sems("summed"), sems("turned"), sems("copied")
        multiplied, taken, ready = sems("multiplied"), sems("taken"), sems("ready")
        stored, chain = sems("stored"), sems("chain")
        norm = norm_of(sb, sems, K["eps"], y, o) if normed else None
        block = ctx.enter_context(nc.Block())

        @block.sync
        def _(sp):
            pairs = [(z, z_table), (agg, agg_table)] + ([(x, x_table)] if normed else [])
            def load(t, h):
                wait_for(sp, turned[h], t)
                if normed:
                    wait_for(sp, taken[h], t)
                for tiles, table in pairs:
                    sp.dma_start(tiles[h][:], node_rows(table, t, h)).then_inc(loaded[h], 16)
            node_loop(sp, load)

        @block.tensor
        def _(pe):
            def turn(t, h):
                pe.wait_ge(summed[h], t + 1)
                wait_for(pe, copied[h], t)
                for g in range(G):
                    tr = pe.transpose(tp[h][:, g, :], z[h][:, g, :], K["ident"][:])
                tr.then_inc(turned[h], 1)

            def multiply(t, h):
                pe.wait_ge(copied[h], t + 1)
                wait_for(pe, taken[h], t)
                for g in range(G):
                    mm = pe.matmul(hp[h][:, g, :], uT[h][:, g, :], weight[:], start=True, stop=True)
                mm.then_inc(multiplied[h], 1)
            node_loop(pe, both_halves(turn, multiply))

        @block.scalar
        def _(act):
            def copy(t, h):
                act.wait_ge(turned[h], t + 1)
                wait_for(act, multiplied[h], t)
                act.copy(uT[h][:], tp[h][:]).then_inc(copied[h], 1)
            parts = [copy]
            if normed:
                parts += [lambda t, h: norm_root(norm, act, t, h), lambda t, h: norm_apply(norm, act, t, h, stored)]
            node_loop(act, both_halves(*parts))

        @block.vector
        def _(dve):
            per = 4 if normed else 2
            n_load = 48 if normed else 32

            def add(t, h):
                link = loop_chain_of(dve, chain[h], 2 * t, per // 2)
                dve.wait_ge(loaded[h], n_load * t + n_load)
                link(dve.tensor_tensor(z[h][:], z[h][:], agg[h][:], ALU.add))
                dinv = K["dinv"][:, bass.ds(2 * t + h, 1), :].rearrange("p a g -> p (a g)")
                dve.tensor_tensor(z[h][:], z[h][:], over_columns(dinv), ALU.mult).then_inc(summed[h], 1)
                if normed:
                    dsqrt = K["dsqrt"][:, bass.ds(2 * t + h, 1), :].rearrange("p a g -> p (a g)")
                    link(dve.tensor_tensor(x[h][:], x[h][:], over_columns(dsqrt), ALU.mult))

            def activate(t, h):
                link = loop_chain_of(dve, chain[h], 2 * t + 1, per // 2)
                dve.wait_ge(multiplied[h], t + 1)
                wait_for(dve, norm["normed"][h] if normed else stored[h], t if normed else 16 * t)
                link(dve.tensor_tensor(y[h][:], hp[h][:], over_rows(bias), ALU.add))
                if normed:
                    link(dve.scalar_tensor_tensor(out=y[h][:], in0=y[h][:], scalar=0.0, in1=x[h][:], op0=ALU.max, op1=ALU.add))
                    dve.sem_inc(taken[h], 1)
                    norm_measure(norm, dve, t, h)
                else:
                    dve.sem_inc(taken[h], 1)
                    dinv = K["dinv"][:, bass.ds(2 * t + h, 1), :].rearrange("p a g -> p (a g)")
                    dve.scalar_tensor_tensor(out=y[h][:], in0=y[h][:], scalar=0.0, in1=over_columns(dinv),
                                             op0=ALU.max, op1=ALU.mult).then_inc(ready[h], 1)
            parts = [add, activate] + ([lambda t, h: norm_scale(norm, dve, t, h)] if normed else [])
            node_loop(dve, both_halves(*parts))

        @block.gpsimd
        def _(pool):
            store_nodes(pool, out_table, o, norm["normed"] if normed else ready, stored)
    end_stage(nc, owned)


def gcn_first(nc, A, T, K):
    gcn_nodes(nc, K, "g0", T["z2"], K["w0"], K["b0"], T["agg"], T["z1"])


def gcn_second(nc, A, T, K):
    gcn_nodes(nc, K, "g1", T["z1"], K["w1"], K["b1"], T["agg"], T["x3"], T["z2"])




def skewed_edge_loop(engine, front, back):
    front(0, 0)
    front(0, 1)
    back(0, 0)
    front(1, 0)
    back(0, 1)
    front(1, 1)
    back(1, 0)
    with engine.Fori(2, LOOPS) as t:
        front(t, 0)
        back(t - 1, 1)
        front(t, 1)
        back(t, 0)
    back(LOOPS - 1, 1)


def edge_rows(table, t, h):
    return table[bass.ds(t * (8 * P) + h * 4 * P, 4 * P), :].rearrange("(j p) d -> p j d", p=P)


def attention_scores(nc, A, T, K):
    with ExitStack() as ctx:
        sb, ps, sem, sems, owned = stage_makers(nc, ctx, "asc")
        xs = [sb(f"xs{h}", [P, 4, D]) for h in range(2)]
        xd = [sb(f"xd{h}", [P, 4, D]) for h in range(2)]
        xdT = [sb(f"xdT{h}", [P, 4, P]) for h in range(2)]
        prod = [sb(f"prod{h}", [P, 4, D]) for h in range(2)]
        four_scores = [sb(f"fs{h}", [P, 4]) for h in range(2)]
        ring = [sb(f"ring{h}", [P, 2, 4], I32) for h in range(2)]
        scores = sb("scores", [P, CHUNKS])
        rows = sb("rows", [P, 4, P])
        tp = [ps(f"tp{h}", [P, 4, P]) for h in range(2)]
        qp = [ps(f"qp{h}", [P, 4, D]) for h in range(2)]
        sT = ps("sT", [P, 4, P])
        ring_ready, gathered, turned, copied = sems("ring_ready"), sems("gathered"), sems("turned"), sems("copied")
        multiplied, dotted, kept, stored = sems("multiplied"), sems("dotted"), sems("kept"), sems("stored")
        all_scored, scores_turned, rows_ready, rows_stored = sem("all_scored"), sem("scores_turned"), sem("rows_ready"), sem("rows_stored")
        block = ctx.enter_context(nc.Block())

        @block.gpsimd
        def _(pool):
            def gather(t, h):
                pool.wait_ge(ring_ready[h], t + 1)
                wait_for(pool, dotted[h], t)
                wait_for(pool, stored[h], 16 * t)
                pool.nop(nofuse=True)
                for j in range(4):
                    pool.indirect_dma_start(xd[h][:, j, :], None, T["x1"],
                                            bass.IndirectOffsetOnAxis(ring[h][:, 1, j:j + 1], 0)).then_inc(gathered[h], 16)
                    pool.indirect_dma_start(xs[h][:, j, :], None, T["x1"],
                                            bass.IndirectOffsetOnAxis(ring[h][:, 0, j:j + 1], 0)).then_inc(gathered[h], 16)
            edge_loop(pool, gather)

        @block.sync
        def _(sp):
            def store(t, h):
                sp.wait_ge(gathered[h], 128 * t + 128)
                sp.dma_start(edge_rows(T["xsrc"], t, h), xs[h][:]).then_inc(stored[h], 16)
            edge_loop(sp, store)
            sp.wait_ge(rows_ready, 1)
            sp.dma_start(T["w"].rearrange("(r f) -> r f", f=4 * P), rows[0:CHUNKS // 4].rearrange("p b i -> p (b i)")).then_inc(rows_stored, 16)
            sp.wait_ge(rows_stored, 16)
            for h in range(2):
                sp.wait_ge(stored[h], 16 * LOOPS)

        @block.tensor
        def _(pe):
            def turn(t, h):
                pe.wait_ge(gathered[h], 128 * t + 128)
                wait_for(pe, copied[h], t)
                for j in range(4):
                    tr = pe.transpose(tp[h][:, j, :], xd[h][:, j, :], K["ident"][:])
                tr.then_inc(turned[h], 1)

            def multiply(t, h):
                pe.wait_ge(copied[h], t + 1)
                wait_for(pe, dotted[h], t)
                for j in range(4):
                    mm = pe.matmul(qp[h][:, j, :], xdT[h][:, j, :], K["wqk"][:], start=True, stop=True)
                mm.then_inc(multiplied[h], 1)

            skewed_edge_loop(pe, turn, multiply)
            pe.wait_ge(all_scored, 1)
            for b in range(4):
                tr = pe.transpose(sT[0:CHUNKS // 4, b, :], scores[:].rearrange("p (r b) -> p b r", b=4)[:, b, :], K["ident"][:])
            tr.then_inc(scores_turned, 1)

        @block.scalar
        def _(act):
            def copy(t, h):
                act.wait_ge(turned[h], t + 1)
                wait_for(act, multiplied[h], t)
                act.copy(xdT[h][:], tp[h][:]).then_inc(copied[h], 1)
            edge_loop(act, copy)

        @block.vector
        def _(dve):
            def fill_ring(t, h):
                dve.tensor_copy(ring[h][:, 0, :], four(K["src_idx"], t, h))
                dve.tensor_copy(ring[h][:, 1, :], four(K["dst_idx"], t, h)).then_inc(ring_ready[h], 1)

            def dot(t, h):
                dve.wait_ge(gathered[h], 128 * t + 128)
                fill_ring(t + 1, h)
                dve.wait_ge(multiplied[h], t + 1)
                for j in range(4):
                    dt = dve.tensor_tensor_reduce(prod[h][:, j, :], qp[h][:, j, :], xs[h][:, j, :], 1.0, 0.0, ALU.mult, ALU.add,
                                                  four_scores[h][:, j:j + 1])
                dt.then_inc(dotted[h], 1)
                dve.wait_ge(dotted[h], t + 1)
                dve.tensor_copy(four(scores, t, h), four_scores[h][:]).then_inc(kept[h], 1)
            fill_ring(0, 0)
            fill_ring(0, 1)
            edge_loop(dve, dot)
            for h in range(2):
                dve.wait_ge(kept[h], LOOPS)
            dve.sem_inc(all_scored, 1)
            dve.wait_ge(scores_turned, 1)
            dve.tensor_copy(rows[0:CHUNKS // 4], sT[0:CHUNKS // 4]).then_inc(rows_ready, 1)
    end_stage(nc, owned)


def attention_softmax(nc, A, T, K):
    with ExitStack() as ctx:
        sb, ps, sem, sems, owned = stage_makers(nc, ctx, "asm")
        e = sb("e", [P, CHUNKS])
        run = sb("run", [P, CHUNKS])
        top = sb("top", [P, CHUNKS])
        tot = sb("tot", [P, CHUNKS])
        rows = sb("rows", [P, 4, P])
        wp = ps("wp", [P, 4, P])
        turner = turner_of(sb, ps, sem)
        loaded, chain_v, shifted, ex_ready = sem("loaded"), sem("chain_v"), sem("shifted"), sem("ex_ready")
        w_ready, w_stored, rows_loaded, rows_turned = sem("w_ready"), sem("w_stored"), sem("rows_loaded"), sem("rows_turned")
        block = ctx.enter_context(nc.Block())
        quarter = CHUNKS // 4

        @block.sync
        def _(sp):
            sp.dma_start(e[:], T["w"].rearrange("(p f) -> p f", f=CHUNKS)).then_inc(loaded, 16)
            sp.wait_ge(w_ready, 1)
            sp.dma_start(T["w"].rearrange("(p f) -> p f", f=CHUNKS), e[:]).then_inc(w_stored, 16)
            sp.wait_ge(w_stored, 16)
            sp.dma_start(rows[0:quarter].rearrange("p b i -> p (b i)"), T["w"].rearrange("(r f) -> r f", f=4 * P)).then_inc(rows_loaded, 16)

        @block.scalar
        def _(act):
            act.wait_ge(shifted, 1)
            act.activation(e[:], e[:], ACT.Exp).then_inc(ex_ready, 1)

        @block.vector
        def _(dve):
            link = chain_of(dve, chain_v)
            link(dve.memset(turner["scr"][:], 0.0))
            link(dve.memset(rows[:], 0.0))
            dve.wait_ge(loaded, 16)
            segment_scan(dve, link, turner, K["seg"], "max", [run[:]], [e[:]])
            segment_scan(dve, link, turner, K["seg"], "fill", [top[:]], [run[:]])
            dve.tensor_tensor(e[:], e[:], top[:], ALU.subtract).then_inc(shifted, 1)
            dve.wait_ge(ex_ready, 1)
            segment_scan(dve, link, turner, K["seg"], "sum", [run[:]], [e[:]])
            segment_scan(dve, link, turner, K["seg"], "fill", [tot[:]], [run[:]])
            link(dve.reciprocal(top[:], tot[:]))
            dve.tensor_tensor(e[:], e[:], top[:], ALU.mult).then_inc(w_ready, 1)
            dve.wait_ge(rows_turned, 1)
            dve.tensor_copy(K["wB"][:].rearrange("p (r b) -> p b r", b=4), wp[:, :, 0:quarter])

        @block.tensor
        def _(pe):
            turn_by_tensor(pe, turner, K["ident"])
            pe.wait_ge(rows_loaded, 16)
            for b in range(4):
                tr = pe.transpose(wp[:, b, :], rows[:, b, :], K["ident"][:])
            tr.then_inc(rows_turned, 1)
    end_stage(nc, owned)


def edge_sums(nc, T, K, name, mode, source):
    mace, attn = mode == "messages", mode == "attention"
    with ExitStack() as ctx:
        sb, ps, sem, sems, owned = stage_makers(nc, ctx, name)
        xs = [sb(f"xs{h}", [P, 4, D]) for h in range(2)]
        drow = [sb(f"drow{h}", [P, 4, P]) for h in range(2)]
        same = [sb(f"same{h}", [P, 4, P]) for h in range(2)]
        carry = [sb(f"carry{h}", [P, 4, P]) for h in range(2)]
        out = [sb(f"out{h}", [P, 4, D]) for h in range(2)]
        gring = [sb(f"gring{h}", [P, 4], I32) for h in range(2)]
        sring = [sb(f"sring{h}", [P, 4], I32) for h in range(2)]
        op = [ps(f"op{j}", [P, 4, P]) for j in range(2)]
        parts = 2 if mace else 1
        if attn or mace:
            sumT = [sb(f"sumT{h}", [P, parts, 4, P]) for h in range(2)]
            tp = ps("tp", [P, parts, 4, P])
        if mace:
            msg = [sb(f"msg{h}", [P, 4, 2 * D]) for h in range(2)]
            xsT = [sb(f"xsT{h}", [P, 4, P]) for h in range(2)]
            h1 = [sb(f"h1{h}", [P, 4, P]) for h in range(2)]
            h2 = [sb(f"h2{h}", [P, 4, P]) for h in range(2)]
            wt = [sb(f"wt{h}", [P, 4, D]) for h in range(2)]
            tmp = [sb(f"tmp{h}", [P, 4, 3, MUL]) for h in range(2)]
            ws = [sb(f"ws{h}", [P, 4, MUL]) for h in range(2)]
            xtp, hid = ps("xtp", [P, 4, P]), ps("hid", [P, 4, P])
            up, wp = ps("up", [P, 4, D]), ps("wp", [P, 4, D])
        row_loaded, ring_ready, gathered = sems("row_loaded"), sems("ring_ready"), sems("gathered")
        masked, sums_turned, sums_copied = sems("masked"), sems("sums_turned"), sems("sums_copied")
        reduced, copied, scattered, sring_ready = sems("reduced"), sems("copied"), sems("scattered"), sems("sring_ready")
        zero_set = sem("zero_set")
        x_turned, x_copied, up_ready = sems("x_turned"), sems("x_copied"), sems("up_ready")
        h1_ready, h1_done, h2_ready, h2_done, w_ready = (sems("h1_ready"), sems("h1_done"), sems("h2_ready"),
                                                         sems("h2_done"), sems("w_ready"))
        msg_ready, msg_chain, wt_done = sems("msg_ready"), sems("msg_chain"), sems("wt_done")
        block = ctx.enter_context(nc.Block())

        @block.sync
        def _(sp):
            def load(t, h):
                wait_for(sp, masked[h], t)
                sp.dma_start(drow[h][:], T["ids"][1:2, bass.ds(t * (8 * P) + h * 4 * P, 4 * P)].broadcast_to([P, 4 * P])).then_inc(row_loaded[h], 16)
                if attn:
                    wait_for(sp, sums_turned[h], t)
                    sp.dma_start(xs[h][:], edge_rows(T["xsrc"], t, h)).then_inc(gathered[h], 16)
            edge_loop(sp, load)

        @block.gpsimd
        def _(pool):
            def gather(t, h):
                if attn:
                    return
                pool.wait_ge(ring_ready[h], t + 1)
                wait_for(pool, (x_turned if mace else reduced)[h], t if mace else 4 * t)
                pool.nop(nofuse=True)
                for j in range(4):
                    pool.indirect_dma_start(xs[h][:, j, :], None, source,
                                            bass.IndirectOffsetOnAxis(gring[h][:, j:j + 1], 0)).then_inc(gathered[h], 16)

            def scatter(t, h):
                pool.wait_ge(sring_ready[h], t + 1)
                pool.wait_ge(copied[h], 4 * t + 4)
                pool.nop(nofuse=True)
                for j in range(4):
                    pool.indirect_dma_start(T["agg"], bass.IndirectOffsetOnAxis(sring[h][:, j:j + 1], 0), out[h][:, j, :], None,
                                            bounds_check=N - 1, oob_is_err=False).then_inc(scattered[h], 16)
            skewed_edge_loop(pool, gather, scatter)
            for h in range(2):
                pool.wait_ge(scattered[h], 64 * LOOPS)

        @block.tensor
        def _(pe):
            def front(t, h):
                if not mace:
                    return
                pe.wait_ge(gathered[h], 64 * t + 64)
                if h == 0:
                    wait_for(pe, x_copied[1], t)
                else:
                    pe.wait_ge(x_copied[0], t + 1)
                for j in range(4):
                    mm = pe.transpose(xtp[:, j, :], xs[h][:, j, :], K["ident"][:])
                mm.then_inc(x_turned[h], 1)
                wait_for(pe, h2_done[1 - h], t + h)
                for j in range(4):
                    mm = pe.matmul(hid[:, j, :], K["m0g"][:, 4 * h + j, :], K["emb"][:, bass.ds(t * P, P)], start=True, stop=True)
                mm.then_inc(h1_ready[h], 1)
                pe.wait_ge(x_copied[h], t + 1)
                wait_for(pe, msg_ready[1 - h], t + h)
                for j in range(4):
                    mm = pe.matmul(up[:, j, :], xsT[h][:, j, :], K["wup"][:], start=True, stop=True)
                mm.then_inc(up_ready[h], 1)
                pe.wait_ge(h1_done[h], t + 1)
                pe.matmul(hid[:].rearrange("p j i -> p (j i)"), K["m1"][:], h1[h][:].rearrange("p j i -> p (j i)"),
                          start=True, stop=True).then_inc(h2_ready[h], 1)
                pe.wait_ge(h2_done[h], t + 1)
                wait_for(pe, wt_done[1 - h], t + h)
                for j in range(4):
                    mm = pe.matmul(wp[:, j, :], h2[h][:, j, :], K["m2"][:], start=True, stop=True)
                mm.then_inc(w_ready[h], 1)

            def back(t, h):
                pe.wait_ge(masked[h], t + 1)
                pe.wait_ge((msg_ready if mace else gathered)[h], t + 1 if mace else (16 if attn else 64) * (t + 1))
                if attn or mace:
                    wait_for(pe, sums_copied[1 - h], t + h)
                    for a in range(parts):
                        for j in range(4):
                            rows = msg[h][:, j, a * D:(a + 1) * D] if mace else xs[h][:, j, :]
                            mm = pe.matmul(tp[:, a, j, :], rows, same[h][:, j, :], start=True, stop=True)
                    mm.then_inc(sums_turned[h], 1)
                    pe.wait_ge(sums_copied[h], t + 1)
                for j in range(4):
                    if j >= 2:
                        pe.wait_ge(copied[h], 4 * t + j - 1)
                    else:
                        wait_for(pe, copied[1 - h], 4 * (t + h) - (1 - j) if h == 1 else 4 * t)
                    o = op[j % 2][:, 0, :]
                    if mace:
                        for a in range(parts):
                            pe.matmul(o, sumT[h][:, a, j, :], K["wout"][:, a, :], start=(a == 0), stop=False)
                    elif attn:
                        pe.matmul(o, sumT[h][:, 0, j, :], K["wvo"][:], start=True, stop=False)
                    else:
                        pe.matmul(o, same[h][:, j, :], xs[h][:, j, :], start=True, stop=False)
                    if j:
                        pe.wait_ge(copied[h], 4 * t + j)
                    else:
                        wait_for(pe, copied[1 - h], 4 * (t + h))
                    before = out[h][:, j - 1, :] if j else out[1 - h][:, 3, :]
                    pe.matmul(o, carry[h][:, j, :], before, start=False, stop=True).then_inc(reduced[h], 1)
                    if j == 3:
                        pass
            pe.wait_ge(zero_set, 1)
            skewed_edge_loop(pe, front, back)

        @block.scalar
        def _(act):
            def front(t, h):
                if not mace:
                    return
                act.wait_ge(x_turned[h], t + 1)
                wait_for(act, up_ready[h], t)
                act.copy(xsT[h][:], xtp[:]).then_inc(x_copied[h], 1)
                act.wait_ge(h1_ready[h], t + 1)
                act.activation(h1[h][:], hid[:], ACT.Silu, bias=K["mb0"][:, 0:1]).then_inc(h1_done[h], 1)
                act.wait_ge(h2_ready[h], t + 1)
                wait_for(act, w_ready[h], t)
                act.activation(h2[h][:], hid[:], ACT.Silu, bias=K["mb1"][:, 0:1]).then_inc(h2_done[h], 1)

            def back(t, h):
                if attn or mace:
                    act.wait_ge(sums_turned[h], t + 1)
                    wait_for(act, reduced[h], 4 * t)
                    act.copy(sumT[h][:], tp[:]).then_inc(sums_copied[h], 1)
                wait_for(act, scattered[h], 64 * t)
                for j in range(4):
                    act.wait_ge(reduced[h], 4 * t + j + 1)
                    act.copy(out[h][:, j, :], op[j % 2][:, 0, :]).then_inc(copied[h], 1)
            skewed_edge_loop(act, front, back)

        @block.vector
        def _(dve):
            def fill_rings(t, h):
                if not attn:
                    dve.tensor_copy(gring[h][:], four(K["src_idx"], t, h)).then_inc(ring_ready[h], 1)

            def masks(t, h):
                if not attn:
                    dve.wait_ge(gathered[h], 64 * t + 64)
                    fill_rings(t + 1, h)
                wait_for(dve, scattered[h], 64 * t)
                dve.tensor_copy(sring[h][:], four(K["scat_idx"], t, h)).then_inc(sring_ready[h], 1)
                dve.wait_ge(row_loaded[h], 16 * t + 16)
                wait_for(dve, reduced[h], 4 * t)
                if attn or mace:
                    wait_for(dve, sums_turned[h], t)
                for j in range(4):
                    key = K["dstB"][:, bass.ds(8 * t + 4 * h + j, 1)]
                    if attn:
                        dve.tensor_scalar(same[h][:, j, :], drow[h][:, j, :], key, K["wB"][:, bass.ds(8 * t + 4 * h + j, 1)],
                                          ALU.is_equal, ALU.mult)
                    else:
                        dve.tensor_scalar(same[h][:, j, :], drow[h][:, j, :], key, None, ALU.is_equal)
                    mk = dve.tensor_scalar(carry[h][:, j, :], drow[h][:, j, :], K["carry_key"][:, bass.ds(8 * t + 4 * h + j, 1)],
                                           None, ALU.is_equal)
                mk.then_inc(masked[h], 1)

            def messages(t, h):
                link = loop_chain_of(dve, msg_chain[h], t, 5)
                dve.wait_ge(w_ready[h], t + 1)
                link(dve.tensor_tensor(wt[h][:], wp[:], K["mb2"][:].unsqueeze(1).broadcast_to([P, 4, D]), ALU.add))
                dve.sem_inc(wt_done[h], 1)
                dve.wait_ge(up_ready[h], t + 1)
                wait_for(dve, sums_turned[h], t)
                w = wt[h][:].rearrange("p j (q k) -> p j q k", q=4)
                u = up[:].rearrange("p j (q k) -> p j q k", q=4)
                m = msg[h][:].rearrange("p j (q k) -> p j q k", q=8)
                axes = K["rhatB"][:, :, bass.ds(8 * t + 4 * h, 4)].rearrange("p c j -> p j c").unsqueeze(3).broadcast_to([P, 4, 3, MUL])
                dve.tensor_tensor(m[:, :, 0], w[:, :, 0], u[:, :, 0], ALU.mult)
                link(dve.tensor_tensor(ws[h][:], w[:, :, 1], u[:, :, 0], ALU.mult))
                dve.tensor_tensor(m[:, :, 2:5], ws[h][:].unsqueeze(2).broadcast_to([P, 4, 3, MUL]), axes, ALU.mult)
                dve.tensor_tensor(m[:, :, 5:8], w[:, :, 2].unsqueeze(2).broadcast_to([P, 4, 3, MUL]), u[:, :, 1:4], ALU.mult)
                link(dve.tensor_tensor(tmp[h][:], u[:, :, 1:4], axes, ALU.mult))
                link(dve.tensor_tensor(tmp[h][:, :, 0], tmp[h][:, :, 0], tmp[h][:, :, 1], ALU.add))
                link(dve.tensor_tensor(tmp[h][:, :, 0], tmp[h][:, :, 0], tmp[h][:, :, 2], ALU.add))
                dve.tensor_tensor(m[:, :, 1], w[:, :, 3], tmp[h][:, :, 0], ALU.mult).then_inc(msg_ready[h], 1)

            def step(t, h):
                masks(t, h)
                if mace:
                    messages(t, h)
            dve.memset(out[1][:, 3, :], 0.0).then_inc(zero_set, 1)
            fill_rings(0, 0)
            fill_rings(0, 1)
            edge_loop(dve, step)
    end_stage(nc, owned)


def attention_sums(nc, A, T, K):
    edge_sums(nc, T, K, "ats", "attention", None)


def gcn_sums_first(nc, A, T, K):
    edge_sums(nc, T, K, "gs0", "gcn", T["z2"])


def gcn_sums_second(nc, A, T, K):
    edge_sums(nc, T, K, "gs1", "gcn", T["z1"])


def message_sums(nc, A, T, K):
    edge_sums(nc, T, K, "mss", "messages", T["x3"])


def radial_basis(nc, A, T, K):
    with ExitStack() as ctx:
        sb, ps, sem, sems, owned = stage_makers(nc, ctx, "rad")
        rows = 8 * NB
        r = sb("r", [P, LOOPS, P])
        part = sb("part", [P, 1], I32)
        center = sb("center", [P, 1])
        inside = sb("inside", [P, LOOPS * P])
        chain_v, loaded, iota_ready, clipped, squared, expd = [sem(n) for n in ("chain_v", "loaded", "iota_ready", "clipped", "squared", "expd")]
        w_loaded, w_zero = sem("w_loaded"), sem("w_zero")
        block = ctx.enter_context(nc.Block())

        @block.gpsimd
        def _(pool):
            pool.iota(part[:], pattern=[[0, 1]], base=0, channel_multiplier=1).then_inc(iota_ready, 1)

        @block.sync
        def _(sp):
            for g in range(8):
                chunks = T["ew"].rearrange("a (t g i) -> a g t i", g=8, i=P)[:, g]
                sp.dma_start(r[NB * g:NB * (g + 1)], chunks.broadcast_to([NB, LOOPS, P])).then_inc(loaded, 16)
            sp.wait_ge(w_zero, 1)
            for g in range(8):
                sp.dma_start(K["m0g"][NB * g:NB * (g + 1), g, 0:64], A["L3_gnn_mlp_w0"]).then_inc(w_loaded, 16)
            sp.wait_ge(w_loaded, 128)

        @block.vector
        def _(dve):
            link = chain_of(dve, chain_v)
            dve.memset(K["m0g"][:], 0.0).then_inc(w_zero, 1)
            link(dve.memset(K["emb"][:], 0.0))
            dve.wait_ge(iota_ready, 1)
            link(dve.tensor_scalar(part[:], part[:], NB - 1, None, ALU.bitwise_and))
            link(dve.tensor_scalar(center[:], part[:], -1.0, None, ALU.mult))
            dve.wait_ge(loaded, 128)
            flat = r[0:rows].rearrange("p t i -> p (t i)")
            link(dve.tensor_scalar(inside[0:rows], flat, 1.0, float(NB) ** 0.5, ALU.is_le, ALU.mult))
            dve.tensor_scalar(flat, flat, 0.0, 1.0, ALU.max, ALU.min).then_inc(clipped, 1)
            dve.wait_ge(expd, 1)
            dve.tensor_tensor(K["emb"][0:rows], flat, inside[0:rows], ALU.mult)

        @block.scalar
        def _(act):
            flat = r[0:rows].rearrange("p t i -> p (t i)")
            act.wait_ge(clipped, 1)
            act.activation(flat, flat, ACT.Square, bias=center[0:rows, 0:1], scale=float(NB - 1)).then_inc(squared, 1)
            act.wait_ge(squared, 1)
            act.activation(flat, flat, ACT.Exp, scale=-0.5).then_inc(expd, 1)
    end_stage(nc, owned)




def tables(nc, shown=()):
    T = {}
    def dram(name, shape, dtype=F32):
        return nc.dram_tensor(name, shape, dtype, kind="ExternalOutput" if name in shown else "Internal").ap()
    T["ids"] = dram("t_ids", (2, EP + P))
    T["ew"] = dram("t_ew", (1, EP))
    T["up"] = dram("t_up", (D, D))
    T["sorted"] = dram("t_sorted", (3, SORTN))
    T["scores"] = dram("t_scores", (N, 8))
    T["alpha"] = dram("t_alpha", (SORTN, HEADS))
    T["nodes"] = dram("t_nodes", (N, 8))
    T["agg"] = dram("t_agg", (N, D))
    T["xsrc"] = dram("t_xsrc", (EP, D))
    T["w"] = dram("t_w", (EP,))
    T["x1"] = dram("t_x1", (N, D))
    T["z2"] = dram("t_z2", (N, D))
    T["z1"] = dram("t_z1", (N, D))
    T["x3"] = dram("t_x3", (N, D))
    return T


def kept(sb):
    K = {}
    K["ident"] = sb("ident", [P, P])
    for_weights = [P, D]
    K["w0"], K["w1"], K["wh"] = sb("w0", for_weights), sb("w1", for_weights), sb("wh", for_weights)
    K["wqk"], K["wvo"], K["wup"] = sb("wqk", for_weights), sb("wvo", for_weights), sb("wup", for_weights)
    K["wout"] = sb("wout", [P, 2, D])
    K["wa"] = sb("wa", [P, 8])
    K["bias0"], K["b0"], K["b1"], K["mb2"] = [sb(n, for_weights) for n in ("bias0", "b0", "b1", "mb2")]
    K["m0"], K["m1"], K["m2"] = [sb(n, for_weights) for n in ("m0", "m1", "m2")]
    K["mb0"], K["mb1"], K["eps"] = [sb(n, [P, 1]) for n in ("mb0", "mb1", "eps")]
    K["dstB"], K["carry_key"] = sb("dstB", [P, CHUNKS]), sb("carry_key", [P, CHUNKS])
    K["rhatB"] = sb("rhatB", [P, 3, CHUNKS])
    K["src_idx"], K["dst_idx"], K["scat_idx"] = [sb(n, [P, CHUNKS + 8], I32) for n in ("src_idx", "dst_idx", "scat_idx")]
    K["ids"] = sb("ids", [P, CHUNKS])
    K["seg"] = segment_tiles(sb, "dst", HEADS + 1)
    K["deg"] = sb("deg", [P, NSUPER, G])
    K["dinv"] = sb("dinv", [P, NSUPER, G])
    K["wB"] = sb("wB", [P, CHUNKS])
    K["m0g"] = sb("m0g", [P, 8, P])
    K["emb"] = sb("emb", [P, LOOPS * P])
    K["dsqrt"] = sb("dsqrt", [P, NSUPER, G])
    return K


def build(nc, A, out, stop=99, shown=()):
    T = tables(nc, shown)
    with ExitStack() as ctx:
        K = kept(stage_makers(nc, ctx, "kept")[0])
        for stage in STAGES[:stop]:
            stage(nc, A, T, K) if stage is not final_layer else stage(nc, A, T, K, out)


STAGES = [prepare, sort_by_src, node_scores, gat_softmax, gat_sums, first_layer, attention_scores, attention_softmax,
          attention_sums, second_norm, gcn_sums_first, gcn_first, gcn_sums_second, gcn_second, radial_basis, message_sums,
          final_layer]


_INS = ["x", "src", "dst", "edge_attr_3", "edge_weight", "L0_gnn_W", "L0_gnn_att", "L0_gnn_bias", "L1_gnn_Wq", "L1_gnn_Wk",
        "L1_gnn_Wv", "L1_gnn_Wo", "L2_gnn_W0", "L2_gnn_b0", "L2_gnn_W1", "L2_gnn_b1", "L3_gnn_W_up0", "L3_gnn_W_up1",
        "L3_gnn_mlp_w0", "L3_gnn_mlp_b0", "L3_gnn_mlp_w1", "L3_gnn_mlp_b1", "L3_gnn_mlp_w2", "L3_gnn_mlp_b2",
        "L3_gnn_W_out0", "L3_gnn_W_out1"]


def kernel(**inputs):
    import numpy as _np
    import concourse.bacc as _bacc
    from concourse import mybir as _mybir
    from concourse.bass_utils import run_bass_kernel_spmd as _run

    nc = _bacc.Bacc("TRN2", target_bir_lowering=False, num_devices=1)
    arrays, args = {}, {}
    for name in _INS:
        a = _np.ascontiguousarray(inputs[name])
        arrays[f"in_{name}_dram"] = a
        args[name] = nc.dram_tensor(f"in_{name}_dram", a.shape, _mybir.dt.from_np(a.dtype), kind="ExternalInput").ap()
    out = nc.dram_tensor("out_0_dram", (N, D), F32, kind="ExternalOutput").ap()
    build(nc, args, out)
    r = _run(nc, [arrays], core_ids=[0])
    return r.results[0]["out_0_dram"]
```

```python
from contextlib import ExitStack

import concourse.bass as bass
from concourse import mybir

ALU = mybir.AluOpType
ACT = mybir.ActivationFunctionType
F32 = mybir.dt.float32
I32 = mybir.dt.int32

P = 128
N = 100000
E = 50000
D = 128
HEADS = 4
HC = D // HEADS
CHUNKS = 392
EP = CHUNKS * P
SORTN = 65536
SORTF = SORTN // P
G = 8
SUPER = P * G
NSUPER = -(-N // SUPER)
LAST = N - SUPER
BUFS = 4
ITEMS = NSUPER
EIGHTS = CHUNKS // 8
PER_BUF = [-(-(ITEMS - u) // BUFS) for u in range(BUFS)]
PAD_ID = 1 << 17
NO_ROW = 1 << 20
BIG = 1.0e30
EPS = 1e-5
NB = 8
MUL = 32
AVG = 16.0
assert CHUNKS == 4 * ITEMS and EP >= E and N < PAD_ID


def stage_makers(nc, ctx, stage):
    owned = []

    def sb(name, shape, dtype=F32):
        return ctx.enter_context(nc.sbuf_tensor(f"{stage}_{name}", shape, dtype))

    def ps(name, shape, dtype=F32):
        return ctx.enter_context(nc.psum_tensor(f"{stage}_{name}", shape, dtype))

    def sem(name):
        owned.append(nc.alloc_semaphore(f"{stage}_{name}"))
        return owned[-1]

    def sems(name):
        return [sem(f"{name}{i}") for i in range(BUFS)]

    return sb, ps, sem, sems, owned


def end_stage(nc, owned):
    nc.clear_and_free_semaphores(owned)
    nc.all_engine_barrier()


def chain_of(engine, sem):
    count = [0]

    def link(instruction):
        count[0] += 1
        instruction.then_inc(sem, 1)
        engine.wait_ge(sem, count[0])
    return link


def loop_chain_of(engine, sem, t, per):
    count = [0]

    def link(instruction):
        count[0] += 1
        assert count[0] <= per
        instruction.then_inc(sem, 1)
        engine.wait_ge(sem, t * per + count[0])
    return link


def wait_for(engine, sem, value):
    if not isinstance(value, int) or value > 0:
        engine.wait_ge(sem, value)


def of_item(sems, t, u, back, by=1):
    return sems[(u - back) % BUFS], (t + (u - back) // BUFS) * by + by


def wait_item(engine, sems, t, u, back, by=1):
    if not isinstance(t, int) or BUFS * t + u - back >= 0:
        engine.wait_ge(*of_item(sems, t, u, back, by))


def pipeline(engine, *parts):
    latest = max(lag for _, lag in parts)
    start = 1 + -(-latest // BUFS) + 1
    end = ITEMS // BUFS

    def slot(t, u):
        for f, lag in parts:
            v = u - lag
            if not isinstance(t, int) or 0 <= BUFS * t + v < ITEMS:
                f(t + v // BUFS, v % BUFS)
    for q in range(start * BUFS):
        slot(q // BUFS, q % BUFS)
    with engine.Fori(start, end) as t:
        for u in range(BUFS):
            slot(t, u)
    for q in range(end * BUFS, ITEMS + latest):
        slot(q // BUFS, q % BUFS)


def is_item(t, u, item):
    return isinstance(t, int) and BUFS * t + u == item


def node_rows(table, t, u):
    base = LAST if is_item(t, u, ITEMS - 1) else t * (BUFS * SUPER) + u * SUPER
    return table[bass.ds(base, SUPER), :].rearrange("(p g) d -> p g d", g=G)


def node_scalars(table, t, u):
    return table[:, bass.ds(BUFS * t + u, 1), :].rearrange("p a g -> p (a g)")


def four(tile, t, u):
    return tile[:, bass.ds(4 * BUFS * t + 4 * u, 4)]


def four_each(tile, t, u):
    return tile[:, :, bass.ds(4 * BUFS * t + 4 * u, 4)]


def edge_rows(table, t, u):
    return table[bass.ds(t * (4 * BUFS * P) + u * 4 * P, 4 * P), :].rearrange("(j p) d -> p j d", p=P)




def prepare(nc, A, T, K):
    with ExitStack() as ctx:
        sb, ps, sem, sems, owned = stage_makers(nc, ctx, "prep")
        ints = sb("ints", [P, 2, CHUNKS], I32)
        flts = sb("flts", [P, 2, CHUNKS])
        wts = sb("wts", [P, 6, D])
        wT = sb("wT", [P, 5, D])
        att8 = sb("att8", [P, 8])
        zeros = sb("zeros", [P, SUPER])
        ew = sb("ew", [P, CHUNKS])
        ones = sb("ones", [P, P])
        rows = CHUNKS // 4
        cur = sb("cur", [P, 4, P])
        nxt = sb("nxt", [P, 4, P])
        srow = sb("srow", [P, 4, P])
        vec = sb("vec", [P, 4 * P, 3])
        scat = sb("scat", [P, 4, P])
        rnorm = sb("rnorm", [P, 4 * P])
        sq = sb("sq", [P, 4 * P, 3])
        rinv = sb("rinv", [P, 4 * P])
        rhatR = sb("rhatR", [P, 3, 4, P])
        scatB = sb("scatB", [P, CHUNKS])
        dshift = sb("dshift", [P, CHUNKS])
        srcB = sb("srcB", [P, CHUNKS])
        wo0 = sb("wo0", [P, 2, MUL])
        pw = ps("pw", [P, 4, P])
        pw2 = ps("pw2", [P, 4, P])
        pt = ps("pt", [P, 4, P])
        chain_v = sem("chain_v")
        chain_g = sem("chain_g")
        pads_set = sem("pads_set")
        ids_loaded = sem("ids_loaded")
        ids_float = sem("ids_float")
        ids_stored = sem("ids_stored")
        small_loaded = sem("small_loaded")
        vec_loaded = sem("vec_loaded")
        rows_loaded = sem("rows_loaded")
        ident_ready = sem("ident_ready")
        w_loaded = sem("w_loaded")
        zeros_set = sem("zeros_set")
        up_built = sem("up_built")
        pe_done = sem("pe_done")
        pe_used = sem("pe_used")
        sumsq_ready = sem("sumsq_ready")
        norm_ready = sem("norm_ready")
        chunkify = sem("chunkify")
        full_rows, tail = E // (4 * P), E % (4 * P)
        full_lines, tail_line = E // CHUNKS, E % CHUNKS
        block = ctx.enter_context(nc.Block())

        @block.gpsimd
        def _(pool):
            link = chain_of(pool, chain_g)
            link(pool.memset(ones[:], 1.0))
            pool.affine_select(out=K["ident"][:], in_=ones[:], compare_op=ALU.is_equal, fill=0.0,
                               base=0, pattern=[[-1, P]], channel_multiplier=1).then_inc(ident_ready, 1)

        @block.sync
        def _(sp):
            sp.wait_ge(pads_set, 1)
            for a, name in enumerate(["src", "dst"]):
                ids = A[name]
                sp.dma_start(ints[0:full_lines, a, :],
                             ids[0:full_lines * CHUNKS].rearrange("(p f) -> p f", f=CHUNKS)).then_inc(ids_loaded, 16)
                sp.dma_start(ints[full_lines:full_lines + 1, a, 0:tail_line],
                             ids[full_lines * CHUNKS:E].rearrange("(p f) -> p f", p=1)).then_inc(ids_loaded, 16)
            sp.dma_start(ew[0:full_lines, :],
                         A["edge_weight"][0:full_lines * CHUNKS].rearrange("(p f) -> p f", f=CHUNKS)).then_inc(ids_loaded, 16)
            sp.dma_start(ew[full_lines:full_lines + 1, 0:tail_line],
                         A["edge_weight"][full_lines * CHUNKS:E].rearrange("(p f) -> p f", p=1)).then_inc(ids_loaded, 16)
            flat3 = A["edge_attr_3"].rearrange("e c -> (e c)")
            sp.dma_start(vec[0:full_rows].rearrange("p a c -> p (a c)"),
                         flat3[0:full_rows * 12 * P].rearrange("(p f) -> p f", f=12 * P)).then_inc(vec_loaded, 16)
            sp.dma_start(vec[full_rows:full_rows + 1, 0:tail, :].rearrange("p a c -> p (a c)"),
                         flat3[full_rows * 12 * P:3 * E].rearrange("(p f) -> p f", p=1)).then_inc(vec_loaded, 16)
            sp.wait_ge(ids_float, 2)
            for a in range(2):
                sp.dma_start(T["ids"][a, 0:EP].rearrange("(p f) -> p f", f=CHUNKS), flts[:, a, :]).then_inc(ids_stored, 16)
            sp.dma_start(T["ids"][1:2, EP:EP + P], flts[P - 1:P, 1, CHUNKS - P:CHUNKS]).then_inc(ids_stored, 16)
            sp.dma_start(T["ew"][0:1, :].rearrange("a (p f) -> (a p) f", f=CHUNKS), ew[:]).then_inc(ids_stored, 16)
            sp.wait_ge(ids_stored, 64)
            for tile, a, off in [(cur, 1, 0), (nxt, 1, 1), (srow, 0, 0)]:
                sp.dma_start(tile[0:rows].rearrange("p b i -> p (b i)"),
                             T["ids"][a, off:off + EP].rearrange("(p f) -> p f", f=4 * P)).then_inc(rows_loaded, 16)

        @block.scalar
        def _(act):
            names = ["L0_gnn_W", "L1_gnn_Wq", "L1_gnn_Wk", "L1_gnn_Wv", "L1_gnn_Wo"]
            for i, name in enumerate(names):
                act.dma_start(wts[:, i, :], A[name]).then_inc(w_loaded, 16)
            act.dma_start(K["w0"][:], A["L2_gnn_W0"]).then_inc(w_loaded, 16)
            act.dma_start(K["w1"][:], A["L2_gnn_W1"]).then_inc(w_loaded, 16)
            act.dma_start(K["wh"][:], A["L0_gnn_W"]).then_inc(w_loaded, 16)
            for tile, name in [(K["bias0"], "L0_gnn_bias"), (K["b0"], "L2_gnn_b0"), (K["b1"], "L2_gnn_b1"), (K["mb2"], "L3_gnn_mlp_b2")]:
                act.dma_start(tile[:], A[name].rearrange("(a d) -> a d", a=1).broadcast_to([P, D])).then_inc(w_loaded, 16)
            act.wait_ge(zeros_set, 1)
            att = A["L0_gnn_att"]
            for h in range(HEADS):
                for s in range(2):
                    act.dma_start(att8[h * HC:(h + 1) * HC, 4 * s + h:4 * s + h + 1],
                                  att[0, h, s * HC:(s + 1) * HC].rearrange("(c a) -> c a", a=1)).then_inc(small_loaded, 16)
            act.dma_start(K["m0"][0:NB, 0:64], A["L3_gnn_mlp_w0"]).then_inc(small_loaded, 16)
            act.dma_start(K["m1"][0:64, 0:64], A["L3_gnn_mlp_w1"]).then_inc(small_loaded, 16)
            act.dma_start(K["m2"][0:64, :], A["L3_gnn_mlp_w2"]).then_inc(small_loaded, 16)
            act.dma_start(K["mb0"][0:64, :], A["L3_gnn_mlp_b0"].rearrange("(c a) -> c a", a=1)).then_inc(small_loaded, 16)
            act.dma_start(K["mb1"][0:64, :], A["L3_gnn_mlp_b1"].rearrange("(c a) -> c a", a=1)).then_inc(small_loaded, 16)
            act.dma_start(T["up"], zeros[:, 0:D]).then_inc(up_built, 16)
            act.wait_ge(up_built, 16)
            act.dma_start(T["up"][0:MUL, 0:MUL], A["L3_gnn_W_up0"]).then_inc(up_built, 16)
            for c in range(3):
                act.dma_start(T["up"][MUL + c:D:3, MUL * (c + 1):MUL * (c + 2)], A["L3_gnn_W_up1"]).then_inc(up_built, 16)
            act.wait_ge(up_built, 80)
            act.dma_start(wts[:, 5, :], T["up"]).then_inc(small_loaded, 16)
            for q, (part, row) in enumerate([(0, 0), (0, MUL), (1, 0), (1, 0)]):
                name = ["L3_gnn_W_out0", "L3_gnn_W_out1"][part]
                act.dma_start(wo0[q * MUL:(q + 1) * MUL, 0, :], A[name][row:row + MUL, :]).then_inc(small_loaded, 16)
            for q, row in enumerate([0, MUL, MUL, MUL]):
                act.dma_start(wo0[q * MUL:(q + 1) * MUL, 1, :], A["L3_gnn_W_out1"][row:row + MUL, :]).then_inc(small_loaded, 16)
            act.wait_ge(sumsq_ready, 1)
            nc.scalar.activation(rnorm[:], sq[:, :, 0], ACT.Sqrt).then_inc(norm_ready, 1)

        N_SMALL = 2 * HEADS + 5 + 1 + 8

        @block.vector
        def _(dve):
            link = chain_of(dve, chain_v)
            dve.memset(ints[:, 0, :], PAD_ID)
            link(dve.memset(ints[:, 1, :], PAD_ID))
            dve.memset(ew[:], 0.0)
            link(dve.memset(vec[:], 0.0))
            dve.memset(att8[:], 0.0).then_inc(pads_set, 1)
            link(dve.memset(zeros[:], 0.0))
            dve.memset(K["m0"][:], 0.0)
            dve.memset(K["m1"][:], 0.0)
            dve.memset(K["m2"][:], 0.0)
            dve.memset(K["mb0"][:], 0.0)
            link(dve.memset(K["mb1"][:], 0.0))
            dve.memset(K["eps"][:], EPS).then_inc(zeros_set, 1)
            dve.wait_ge(ids_loaded, 96)
            dve.tensor_copy(flts[:, 0, :], ints[:, 0, :]).then_inc(ids_float, 1)
            dve.tensor_copy(flts[:, 1, :], ints[:, 1, :]).then_inc(ids_float, 1)
            dve.wait_ge(vec_loaded, 32)
            link(dve.tensor_tensor(sq[:], vec[:], vec[:], ALU.mult))
            link(dve.tensor_tensor(sq[:, :, 0], sq[:, :, 0], sq[:, :, 1], ALU.add))
            dve.tensor_tensor(sq[:, :, 0], sq[:, :, 0], sq[:, :, 2], ALU.add).then_inc(sumsq_ready, 1)
            dve.wait_ge(norm_ready, 1)
            link(dve.tensor_scalar(rnorm[:], rnorm[:], 1e-12, None, ALU.add))
            link(dve.reciprocal(rinv[:], rnorm[:]))
            for c in range(3):
                link(dve.tensor_tensor(rhatR[:, c].rearrange("p b i -> p (b i)"), vec[:, :, c], rinv[:], ALU.mult))
            dve.wait_ge(rows_loaded, 48)
            link(dve.memset(scat[:], 0.0))
            link(dve.tensor_tensor(scat[0:rows], cur[0:rows], nxt[0:rows], ALU.is_equal))
            link(dve.scalar_tensor_tensor(out=scat[0:rows], in0=scat[0:rows], scalar=float(NO_ROW), in1=cur[0:rows],
                                          op0=ALU.mult, op1=ALU.max))
            dve.sem_inc(chunkify, 1)
            blocks = [(cur, K["dstB"][:]), (scat, scatB[:]), (srow, srcB[:])] + \
                     [(rhatR[:, c], K["rhatB"][:, c, :]) for c in range(3)]
            for n, (_, out) in enumerate(blocks):
                dve.wait_ge(pe_done, n + 1)
                dve.tensor_copy(out.rearrange("p (r b) -> p b r", b=4), pt[:, :, 0:rows]).then_inc(pe_used, 1)
            dve.wait_ge(pe_used, len(blocks))
            for tile in (K["scat_idx"], K["src_idx"], K["dst_idx"]):
                link(dve.memset(tile[:], 0))
            dve.tensor_copy(K["scat_idx"][:, 0:CHUNKS], scatB[:])
            dve.tensor_scalar(K["src_idx"][:, 0:CHUNKS], srcB[:], float(N - 1), None, ALU.min)
            dve.tensor_scalar(K["dst_idx"][:, 0:CHUNKS], K["dstB"][:], float(N - 1), None, ALU.min)
            link(dve.memset(dshift[:], 0.0))
            dve.wait_ge(ident_ready, 1)
            link(dve.tensor_scalar(dshift[:, 1:CHUNKS], K["dstB"][:, 0:CHUNKS - 1], 1.0, K["ident"][:, P - 1:P], ALU.add, ALU.mult))
            link(dve.tensor_scalar(K["carry_key"][:], dshift[:], -1.0, None, ALU.add))
            dve.wait_ge(w_loaded, 16 * 12)
            dve.wait_ge(small_loaded, 16 * N_SMALL)
            dve.tensor_scalar(K["wup"][:], wts[:, 5, :], MUL ** -0.5, None, ALU.mult).then_inc(chunkify, 1)
            base = len(blocks)
            dve.wait_ge(pe_done, base + 1)
            dve.tensor_copy(wT[:, 0:4, :], pw[:]).then_inc(pe_used, 1)
            dve.wait_ge(pe_done, base + 2)
            dve.tensor_copy(K["wa"][:], pw2[:, 1, 0:8])
            dve.tensor_scalar(K["wqk"][:], pw2[:, 2, :], D ** -0.5, None, ALU.mult)
            dve.tensor_copy(K["wvo"][:], pw2[:, 3, :])
            s0 = (2 * MUL) ** -0.5 / AVG
            sv = s0 * 3.0 ** 0.5
            link(dve.memset(K["wout"][:], 0.0))
            vcols = K["wout"][:, :, MUL:].rearrange("p a (k c) -> p a k c", c=3)
            link(dve.tensor_scalar(K["wout"][0:64, 0, 0:MUL], wo0[0:64, 0, :], s0, None, ALU.mult))
            link(dve.tensor_scalar(vcols[64:96, 0, :, 0], wo0[64:96, 0, :], sv, None, ALU.mult))
            link(dve.tensor_scalar(vcols[96:128, 0, :, 1], wo0[96:128, 0, :], sv, None, ALU.mult))
            link(dve.tensor_scalar(vcols[0:32, 1, :, 2], wo0[0:32, 1, :], sv, None, ALU.mult))
            for c in range(3):
                q = 32 * (c + 1)
                link(dve.tensor_scalar(vcols[q:q + 32, 1, :, c], wo0[q:q + 32, 1, :], s0, None, ALU.mult))

        @block.tensor
        def _(pe):
            pe.wait_ge(ident_ready, 1)
            pe.wait_ge(chunkify, 1)
            n = 0
            for src in [cur, scat, srow, rhatR[:, 0], rhatR[:, 1], rhatR[:, 2]]:
                if n:
                    pe.wait_ge(pe_used, n)
                for b in range(4):
                    tr = nc.tensor.transpose(pt[:, b, :], src[:, b, :], K["ident"][:])
                tr.then_inc(pe_done, 1)
                n += 1
            pe.wait_ge(chunkify, 2)
            pe.wait_ge(w_loaded, 16 * 12)
            for i in range(4):
                tr = nc.tensor.transpose(pw[:, i, :], wts[:, i, :], K["ident"][:])
            tr.then_inc(pe_done, 1)
            pe.wait_ge(pe_used, n + 1)
            nc.tensor.matmul(pw2[:, 1, 0:8], wT[:, 0, :], att8[:], start=True, stop=True)
            nc.tensor.matmul(pw2[:, 2, :], wT[:, 1, :], wT[:, 2, :], start=True, stop=True)
            nc.tensor.matmul(pw2[:, 3, :], wT[:, 3, :], wts[:, 4, :], start=True, stop=True).then_inc(pe_done, 1)
    end_stage(nc, owned)




def sort_and_scores(nc, A, T, K):
    with ExitStack() as ctx:
        sb, ps, sem, sems, owned = stage_makers(nc, ctx, "sort")
        x = [sb(f"x{u}", [P, G, D]) for u in range(BUFS)]
        xT = [sb(f"xT{u}", [P, G, P]) for u in range(2)]
        s = [sb(f"s{u}", [P, G, 8]) for u in range(BUFS)]
        zeros = sb("zeros", [P, SUPER])
        tp = ps("tp", [P, G, P])
        sps = [ps(f"sps{v}", [P, G, 64]) for v in range(2)]
        x_loaded, x_turned, x_copied = sems("x_loaded"), sems("x_turned"), sems("x_copied")
        scored, s_ready, s_stored = sems("scored"), sems("s_ready"), sems("s_stored")
        agg_zeroed, zeros_set = sem("agg_zeroed"), sem("zeros_set")
        rec = [sb(f"rec{i}", [P, 3, SORTF]) for i in range(2)]
        ints = sb("ints", [P, 2, SORTF], I32)
        place = sb("place", [P, SORTF], I32)
        gray = sb("gray", [P, SORTF], I32)
        bit = sb("bit", [P, SORTF], I32)
        sign = sb("sign", [P, SORTF])
        swap = sb("swap", [P, SORTF // 2])
        diff = sb("diff", [P, 2, SORTF // 2])
        flip = ps("flip", [P, 3, SORTF])
        chain_v = sem("chain_v")
        padded = sem("padded")
        loaded = sem("loaded")
        place_ready = sem("place_ready")
        records_ready = sem("records_ready")
        turned = sem("turned")
        sorted_ready = sem("sorted_ready")
        stored = sem("stored")
        full, tail = E // SORTF, E % SORTF
        block = ctx.enter_context(nc.Block())
        turns = []

        @block.gpsimd
        def _(pool):
            pool.iota(place[:], pattern=[[1, SORTF]], base=0, channel_multiplier=SORTF).then_inc(place_ready, 1)

        @block.vector
        def _(dve):
            link = chain_of(dve, chain_v)
            dve.memset(ints[:], PAD_ID).then_inc(padded, 1)
            dve.memset(zeros[:], 0.0).then_inc(zeros_set, 1)
            dve.wait_ge(place_ready, 1)
            link(dve.tensor_scalar(gray[:], place[:], 1, None, ALU.logical_shift_right))
            dve.wait_ge(loaded, 64)
            dve.tensor_copy(rec[0][:, 0, :], ints[:, 0, :])
            dve.tensor_copy(rec[0][:, 1, :], place[:])
            link(dve.tensor_copy(rec[0][:, 2, :], ints[:, 1, :]))
            now = 0

            def flip_signs(bits, i):
                link(dve.tensor_scalar(bit[:], bits[:], i, 1, ALU.logical_shift_right, ALU.bitwise_and))
                link(dve.tensor_scalar(sign[:], bit[:], -2.0, 1.0, ALU.mult, ALU.add))
                link(dve.tensor_tensor(rec[now][:, 0, :], rec[now][:, 0, :], sign[:], ALU.mult))

            def exchange(now, step):
                a = rec[now][:].rearrange("p r (b two j) -> p r b two j", two=2, j=step)
                o = rec[1 - now][:].rearrange("p r (b two j) -> p r b two j", two=2, j=step)
                s = swap[:].rearrange("p (b j) -> p b j", j=step)
                d = diff[:].rearrange("p r (b j) -> p r b j", j=step)
                dve.tensor_tensor(s, a[:, 0, :, 0], a[:, 0, :, 1], ALU.is_gt)
                for r in (1, 2):
                    link(dve.tensor_tensor(d[:, r - 1], a[:, r, :, 1], a[:, r, :, 0], ALU.subtract))
                dve.tensor_tensor(o[:, 0, :, 0], a[:, 0, :, 0], a[:, 0, :, 1], ALU.min)
                dve.tensor_tensor(o[:, 0, :, 1], a[:, 0, :, 0], a[:, 0, :, 1], ALU.max)
                for r in (1, 2):
                    link(dve.tensor_tensor(d[:, r - 1], d[:, r - 1], s, ALU.mult))
                for r in (1, 2):
                    dve.tensor_tensor(o[:, r, :, 0], a[:, r, :, 0], d[:, r - 1], ALU.add)
                    link(dve.tensor_tensor(o[:, r, :, 1], a[:, r, :, 1], d[:, r - 1], ALU.subtract))

            def turn_blocks(now):
                turns.append(now)
                dve.sem_inc(records_ready, 1)
                dve.wait_ge(turned, len(turns))
                link(dve.tensor_copy(rec[1 - now][:], flip[:]))

            flip_signs(place, 1)
            link(dve.tensor_tensor(gray[:], gray[:], place[:], ALU.bitwise_xor))
            top = SORTN.bit_length() - 1
            inner = SORTF.bit_length() - 1
            for i in range(1, top + 1):
                if i > inner:
                    turn_blocks(now)
                    now = 1 - now
                    for j in range(i - 1, inner - 1, -1):
                        exchange(now, 1 << (j - inner))
                        now = 1 - now
                    turn_blocks(now)
                    now = 1 - now
                for j in range(min(i, inner) - 1, -1, -1):
                    exchange(now, 1 << j)
                    now = 1 - now
                if i < top:
                    flip_signs(gray, i)
            dve.sem_inc(sorted_ready, 1 + now)

        @block.tensor
        def _(pe):
            def turn(t, u):
                pe.wait_ge(x_loaded[u], 16 * t + 16)
                wait_item(pe, x_copied, t, u, 1)
                for g in range(G):
                    tr = pe.transpose(tp[:, g, :], x[u][:, g, :], K["ident"][:])
                tr.then_inc(x_turned[u], 1)

            def score(t, u):
                pe.wait_ge(x_copied[u], t + 1)
                wait_item(pe, s_ready, t, u, 2)
                for g in range(G):
                    mm = pe.matmul(sps[u % 2][:, g, 0:8], xT[u % 2][:, g, :], K["wa"][:], start=True, stop=True)
                mm.then_inc(scored[u], 1)
            pipeline(pe, (turn, 0), (score, 1))
            for n, now in enumerate(turns):
                pe.wait_ge(records_ready, n + 1)
                for r in range(3):
                    for b in range(SORTF // P):
                        tr = nc.tensor.transpose(flip[:, r, b * P:(b + 1) * P], rec[now][:, r, b * P:(b + 1) * P], K["ident"][:])
                tr.then_inc(turned, 1)

        @block.scalar
        def _(act):
            def copy(t, u):
                act.wait_ge(x_turned[u], t + 1)
                wait_item(act, scored, t, u, 2)
                act.copy(xT[u % 2][:], tp[:]).then_inc(x_copied[u], 1)

            def take(t, u):
                act.wait_ge(scored[u], t + 1)
                wait_item(act, s_stored, t, u, 4, 16)
                act.copy(s[u][:], sps[u % 2][:, :, 0:8]).then_inc(s_ready[u], 1)
            pipeline(act, (copy, 0), (take, 2))

        @block.sync
        def _(sp):
            sp.wait_ge(padded, 1)
            for a, name in enumerate(["src", "dst"]):
                sp.dma_start(ints[0:full, a, :], A[name][0:full * SORTF].rearrange("(p f) -> p f", f=SORTF)).then_inc(loaded, 16)
                sp.dma_start(ints[full:full + 1, a, 0:tail],
                             A[name][full * SORTF:E].rearrange("(p f) -> p f", p=1)).then_inc(loaded, 16)
            def load_x(t, u):
                wait_item(sp, x_turned, t, u, 4)
                sp.dma_start(x[u][:], node_rows(A["x"], t, u)).then_inc(x_loaded[u], 16)

            def store_s(t, u):
                sp.wait_ge(s_ready[u], t + 1)
                if is_item(t, u, ITEMS - 1):
                    wait_item(sp, s_stored, t, u, 1, 16)
                sp.dma_start(node_rows(T["scores"], t, u), s[u][:]).then_inc(s_stored[u], 16)
            pipeline(sp, (load_x, 0), (store_s, 6))
            sp.wait_ge(zeros_set, 1)
            for n in range(NSUPER):
                b = min(n * SUPER, LAST)
                if n == NSUPER - 1:
                    sp.wait_ge(agg_zeroed, 16 * n)
                sp.dma_start(T["agg"][b:b + SUPER, :].rearrange("(p g) d -> p (g d)", g=G), zeros[:]).then_inc(agg_zeroed, 16)
            for u in range(BUFS):
                sp.wait_ge(s_stored[u], 16 * PER_BUF[u])
            sp.wait_ge(agg_zeroed, 16 * NSUPER)
            phases = SORTN.bit_length() - 1
            exchanges = phases * (phases + 1) // 2
            now = (exchanges + len(turns)) % 2
            sp.wait_ge(sorted_ready, 1 + now)
            for r in range(3):
                sp.dma_start(T["sorted"][r].rearrange("(p f) -> p f", f=SORTF), rec[now][:, r, :]).then_inc(stored, 16)
            sp.wait_ge(stored, 48)
    end_stage(nc, owned)




def segment_tiles(sb, name, heads):
    seg = {"heads": heads}
    for tile in ("cont", "negcont", "nxt", "pre", "negpre", "suf", "last", "work"):
        seg[tile] = sb(f"{name}_{tile}", [P, CHUNKS])
    for row in ("first", "end", "full", "link", "neglink", "a", "nega", "arev", "linkn", "b", "c"):
        seg["r_" + row] = sb(f"{name}_r_{row}", [heads, P])
    seg["ccol"] = sb(f"{name}_ccol", [P, heads])
    seg["fullcol"] = sb(f"{name}_fullcol", [P, 1])
    return seg


def turner_of(sb, ps, sem):
    return {"scr": sb("turn_scr", [P, P]), "out": ps("turn_out", [P, P]), "ready": sem("turn_ready"),
            "done": sem("turn_done"), "turns": []}


def turn_by_vector(dve, turner, write):
    write(turner["scr"]).then_inc(turner["ready"], 1)
    turner["turns"].append(1)
    dve.wait_ge(turner["done"], len(turner["turns"]))


def turn_by_tensor(pe, turner, ident):
    for n in range(len(turner["turns"])):
        pe.wait_ge(turner["ready"], n + 1)
        pe.transpose(turner["out"][:], turner["scr"][:], ident[:]).then_inc(turner["done"], 1)


def find_segments(dve, link, turner, seg, ids):
    F, H, R = CHUNKS, seg["heads"], P
    link(dve.memset(seg["cont"][:, 0:1], 0.0))
    link(dve.tensor_tensor(seg["cont"][:, 1:F], ids[:, 1:F], ids[:, 0:F - 1], ALU.is_equal))
    link(dve.memset(seg["nxt"][:, F - 1:F], 0.0))
    link(dve.tensor_copy(seg["nxt"][:, 0:F - 1], seg["cont"][:, 1:F]))
    link(dve.tensor_scalar(seg["negcont"][:], seg["cont"][:], -1.0, BIG, ALU.add, ALU.mult))
    link(dve.tensor_scalar(seg["pre"][:], ids, ids[:, 0:1], None, ALU.is_equal))
    link(dve.tensor_scalar(seg["negpre"][:], seg["pre"][:], -1.0, BIG, ALU.add, ALU.mult))
    link(dve.tensor_scalar(seg["suf"][:], ids, ids[:, F - 1:F], None, ALU.is_equal))
    link(dve.tensor_tensor(seg["fullcol"][:], ids[:, 0:1], ids[:, F - 1:F], ALU.is_equal))
    for col, row in [(ids[:, 0:1], seg["r_first"]), (ids[:, F - 1:F], seg["r_end"]), (seg["fullcol"][:], seg["r_full"])]:
        turn_by_vector(dve, turner, lambda scr: dve.tensor_copy(scr[:, 0:H], col.broadcast_to([P, H])))
        link(dve.tensor_copy(row[:], turner["out"][0:H, :]))
    link(dve.memset(seg["r_link"][:], 0.0))
    link(dve.tensor_tensor(seg["r_link"][:, 1:R], seg["r_first"][:, 1:R], seg["r_end"][:, 0:R - 1], ALU.is_equal))
    link(dve.tensor_scalar(seg["r_neglink"][:], seg["r_link"][:], -1.0, BIG, ALU.add, ALU.mult))
    link(dve.memset(seg["r_a"][:], 0.0))
    link(dve.tensor_tensor(seg["r_a"][:, 1:R], seg["r_link"][:, 1:R], seg["r_full"][:, 0:R - 1], ALU.mult))
    link(dve.tensor_scalar(seg["r_nega"][:], seg["r_a"][:], -1.0, BIG, ALU.add, ALU.mult))
    link(dve.memset(seg["r_linkn"][:], 0.0))
    link(dve.tensor_copy(seg["r_linkn"][:, 0:R - 1], seg["r_link"][:, 1:R]))
    link(dve.memset(seg["r_arev"][:], 0.0))
    link(dve.tensor_tensor(seg["r_arev"][:, 0:R - 1], seg["r_linkn"][:, 0:R - 1], seg["r_full"][:, 1:R], ALU.mult))
    turn_by_vector(dve, turner, lambda scr: dve.tensor_copy(scr[0:H, :], seg["r_linkn"][:]))
    link(dve.tensor_copy(seg["last"][:], seg["nxt"][:]))
    link(dve.tensor_copy(seg["last"][:, F - 1:F], turner["out"][:, 0:1]))
    link(dve.tensor_scalar(seg["last"][:], seg["last"][:], -1.0, 1.0, ALU.mult, ALU.add))


def segment_scan(dve, link, turner, seg, kind, outs, ins):
    F, H, R = CHUNKS, len(outs), P
    for out, v in zip(outs, ins):
        if kind == "sum":
            link(dve.tensor_tensor_scan(out, seg["cont"][:], v, 0.0, ALU.mult, ALU.add))
        elif kind == "max":
            link(dve.tensor_tensor_scan(out, seg["negcont"][:], v, -BIG, ALU.add, ALU.max))
        else:
            link(dve.tensor_tensor(seg["work"][:], seg["last"][:], v, ALU.mult))
            link(dve.tensor_tensor_scan(out[:, ::-1], seg["nxt"][:, ::-1], seg["work"][:, ::-1], 0.0, ALU.mult, ALU.add))
    end = 0 if kind == "fill" else F - 1
    for h, out in enumerate(outs):
        link(dve.tensor_copy(turner["scr"][:, h:h + 1], out[:, end:end + 1]))
    turn_by_vector(dve, turner, lambda scr: dve.tensor_copy(scr[:, H - 1:H], outs[H - 1][:, end:end + 1]))
    ends, b, c = turner["out"][0:H, :], seg["r_b"][0:H, :], seg["r_c"][0:H, :]
    if kind == "sum":
        link(dve.memset(b[:, 0:1], 0.0))
        link(dve.tensor_tensor(b[:, 1:R], seg["r_link"][0:H, 1:R], ends[:, 0:R - 1], ALU.mult))
        link(dve.tensor_tensor_scan(c, seg["r_a"][0:H, :], b, 0.0, ALU.mult, ALU.add))
    elif kind == "max":
        link(dve.memset(b[:, 0:1], -BIG))
        link(dve.tensor_tensor(b[:, 1:R], seg["r_neglink"][0:H, 1:R], ends[:, 0:R - 1], ALU.add))
        link(dve.tensor_tensor_scan(c, seg["r_nega"][0:H, :], b, -BIG, ALU.add, ALU.max))
    else:
        link(dve.memset(b[:, R - 1:R], 0.0))
        link(dve.tensor_tensor(b[:, 0:R - 1], seg["r_linkn"][0:H, 0:R - 1], ends[:, 1:R], ALU.mult))
        link(dve.tensor_tensor_scan(c[:, ::-1], seg["r_arev"][0:H, ::-1], b[:, ::-1], 0.0, ALU.mult, ALU.add))
    turn_by_vector(dve, turner, lambda scr: dve.tensor_copy(scr[0:H, :], c))
    link(dve.tensor_copy(seg["ccol"][:, 0:H], turner["out"][:, 0:H]))
    for h, out in enumerate(outs):
        carried = seg["ccol"][:, h:h + 1]
        if kind == "sum":
            link(dve.scalar_tensor_tensor(out=out, in0=seg["pre"][:], scalar=carried, in1=out, op0=ALU.mult, op1=ALU.add))
        elif kind == "max":
            link(dve.scalar_tensor_tensor(out=out, in0=seg["negpre"][:], scalar=carried, in1=out, op0=ALU.add, op1=ALU.max))
        else:
            link(dve.scalar_tensor_tensor(out=out, in0=seg["suf"][:], scalar=carried, in1=out, op0=ALU.mult, op1=ALU.add))




def gat_softmax(nc, A, T, K):
    with ExitStack() as ctx:
        sb, ps, sem, sems, owned = stage_makers(nc, ctx, "gsm")
        rec = sb("rec", [P, 3, CHUNKS])
        src_idx = sb("src_idx", [P, CHUNKS], I32)
        dst_idx = sb("dst_idx", [P, CHUNKS], I32)
        edge_idx = sb("edge_idx", [P, CHUNKS], I32)
        ring = [sb(f"ring{u}", [P, 2, 4], I32) for u in range(BUFS)]
        out_ring = [sb(f"out_ring{u}", [P, 4], I32) for u in range(BUFS)]
        row_s = [sb(f"row_s{u}", [P, 4, 8]) for u in range(BUFS)]
        row_d = [sb(f"row_d{u}", [P, 4, 8]) for u in range(BUFS)]
        row_o = [sb(f"row_o{u}", [P, 4, HEADS]) for u in range(BUFS)]
        al = sb("al", [P, HEADS, CHUNKS])
        mx = sb("mx", [P, HEADS, CHUNKS])
        tot = sb("tot", [P, HEADS + 1, CHUNKS])
        run = sb("run", [P, HEADS + 1, CHUNKS])
        seg = segment_tiles(sb, "src", HEADS + 1)
        turner = turner_of(sb, ps, sem)
        h1 = [sb(f"h1{v}", [P, 4, P]) for v in range(2)]
        h2 = [sb(f"h2{v}", [P, 4, P]) for v in range(2)]
        w = [sb(f"w{u}", [P, 4, D]) for u in range(BUFS)]
        hp1, hp2, wp = ps("hp1", [P, 4, P]), ps("hp2", [P, 4, P]), ps("wp", [P, 4, D])
        loaded, ring_ready, gathered = sem("loaded"), sems("ring_ready"), sems("gathered")
        rows_used, chain_v = sems("rows_used"), sem("chain_v")
        shifted, ex_ready = sem("shifted"), sem("ex_ready")
        out_ready, scattered = sems("out_ready"), sems("scattered")
        h1_ready, h1_done, h2_ready, h2_done = sems("h1_ready"), sems("h1_done"), sems("h2_ready"), sems("h2_done")
        wp_ready, w_ready, w_stored = sems("wp_ready"), sems("w_ready"), sems("w_stored")
        block = ctx.enter_context(nc.Block())

        @block.sync
        def _(sp):
            for r in range(3):
                sp.dma_start(rec[:, r, :], T["sorted"][r, 0:EP].rearrange("(p f) -> p f", f=CHUNKS)).then_inc(loaded, 16)

            def store_w(t, u):
                sp.wait_ge(w_ready[u], t + 1)
                sp.dma_start(edge_rows(T["radial"], t, u), w[u][:]).then_inc(w_stored[u], 16)
            pipeline(sp, (store_w, 0))
            for u in range(BUFS):
                sp.wait_ge(w_stored[u], 16 * PER_BUF[u])

        @block.vector
        def _(dve):
            link = chain_of(dve, chain_v)
            link(dve.memset(turner["scr"][:], 0.0))
            dve.wait_ge(loaded, 48)
            dve.tensor_scalar(src_idx[:], rec[:, 0, :], float(N - 1), None, ALU.min)
            dve.tensor_copy(edge_idx[:], rec[:, 1, :])
            link(dve.tensor_scalar(dst_idx[:], rec[:, 2, :], float(N - 1), None, ALU.min))

            def fill_ring(t, u):
                wait_item(dve, gathered, t, u, 4, 128)
                dve.tensor_copy(ring[u][:, 0, :], four(src_idx, t, u))
                dve.tensor_copy(ring[u][:, 1, :], four(dst_idx, t, u)).then_inc(ring_ready[u], 1)

            def take_rows(t, u):
                dve.wait_ge(gathered[u], 128 * t + 128)
                dve.tensor_tensor(four_each(al, t, u), row_s[u][:, :, 0:HEADS].rearrange("p j h -> p h j"),
                                  row_d[u][:, :, HEADS:8].rearrange("p j h -> p h j"), ALU.add).then_inc(rows_used[u], 1)

            def add_bias(t, u):
                dve.wait_ge(wp_ready[u], t + 1)
                wait_item(dve, w_stored, t, u, 4, 16)
                dve.tensor_tensor(w[u][:], wp[:], K["mb2"][:].unsqueeze(1).broadcast_to([P, 4, D]), ALU.add).then_inc(w_ready[u], 1)
            pipeline(dve, (fill_ring, 0), (add_bias, 2), (take_rows, 4))
            for u in range(BUFS):
                dve.wait_ge(rows_used[u], PER_BUF[u])
            link(dve.scalar_tensor_tensor(out=al[:], in0=al[:], scalar=0.2, in1=al[:], op0=ALU.mult, op1=ALU.max))
            find_segments(dve, link, turner, seg, rec[:, 0, :])
            heads = range(HEADS)
            segment_scan(dve, link, turner, seg, "max", [run[:, h, :] for h in heads], [al[:, h, :] for h in heads])
            segment_scan(dve, link, turner, seg, "fill", [mx[:, h, :] for h in heads], [run[:, h, :] for h in heads])
            link(dve.tensor_scalar(mx[:], mx[:], 0.0, None, ALU.max))
            dve.tensor_tensor(al[:], al[:], mx[:], ALU.subtract).then_inc(shifted, 1)
            dve.wait_ge(ex_ready, 2)
            link(dve.memset(tot[:, HEADS, :], 1.0))
            each = range(HEADS + 1)
            segment_scan(dve, link, turner, seg, "sum", [run[:, h, :] for h in each],
                         [al[:, h, :] for h in heads] + [tot[:, HEADS, :]])
            segment_scan(dve, link, turner, seg, "fill", [tot[:, h, :] for h in each], [run[:, h, :] for h in each])
            link(dve.tensor_scalar(seg["work"][:], tot[:, HEADS, :], -1.0, float(E), ALU.mult, ALU.add))
            for h in heads:
                link(dve.tensor_tensor(mx[:, h, :], mx[:, h, :], seg["work"][:], ALU.mult))
            link(dve.tensor_tensor(tot[:, 0:HEADS, :], tot[:, 0:HEADS, :], mx[:], ALU.add))
            link(dve.reciprocal(mx[:], tot[:, 0:HEADS, :]))
            link(dve.tensor_tensor(al[:], al[:], mx[:], ALU.mult))

            def give_rows(t, u):
                wait_item(dve, scattered, t, u, 4, 64)
                dve.tensor_copy(row_o[u][:], four_each(al, t, u).rearrange("p h j -> p j h"))
                dve.tensor_copy(out_ring[u][:], four(edge_idx, t, u)).then_inc(out_ready[u], 1)
            pipeline(dve, (give_rows, 0))

        @block.scalar
        def _(act):
            def first(t, u):
                act.wait_ge(h1_ready[u], t + 1)
                wait_item(act, h2_ready, t, u, 2)
                act.activation(h1[u % 2][:], hp1[:], ACT.Silu, bias=K["mb0"][:, 0:1]).then_inc(h1_done[u], 1)

            def second(t, u):
                act.wait_ge(h2_ready[u], t + 1)
                wait_item(act, wp_ready, t, u, 2)
                act.activation(h2[u % 2][:], hp2[:], ACT.Silu, bias=K["mb1"][:, 0:1]).then_inc(h2_done[u], 1)
            pipeline(act, (first, 0), (second, 1))
            act.wait_ge(shifted, 1)
            nc.scalar.activation(al[:], al[:], ACT.Exp).then_inc(ex_ready, 1)
            nc.scalar.activation(mx[:], mx[:], ACT.Exp, scale=-1.0).then_inc(ex_ready, 1)

        @block.tensor
        def _(pe):
            def first(t, u):
                wait_item(pe, h1_done, t, u, 1)
                for j in range(4):
                    mm = pe.matmul(hp1[:, j, :], K["m0g"][:, (4 * u + j) % 8, :], radial_block(K, t, u), start=True, stop=True)
                mm.then_inc(h1_ready[u], 1)

            def second(t, u):
                pe.wait_ge(h1_done[u], t + 1)
                wait_item(pe, h2_done, t, u, 1)
                pe.matmul(hp2[:].rearrange("p j i -> p (j i)"), K["m1"][:], h1[u % 2][:].rearrange("p j i -> p (j i)"),
                          start=True, stop=True).then_inc(h2_ready[u], 1)

            def third(t, u):
                pe.wait_ge(h2_done[u], t + 1)
                wait_item(pe, w_ready, t, u, 1)
                for j in range(4):
                    mm = pe.matmul(wp[:, j, :], h2[u % 2][:, j, :], K["m2"][:], start=True, stop=True)
                mm.then_inc(wp_ready[u], 1)
            pipeline(pe, (first, 0), (second, 1), (third, 2))
            turn_by_tensor(pe, turner, K["ident"])

        @block.gpsimd
        def _(pool):
            def gather(t, u):
                pool.wait_ge(ring_ready[u], t + 1)
                wait_item(pool, rows_used, t, u, 4)
                pool.nop(nofuse=True)
                for j in range(4):
                    pool.indirect_dma_start(row_s[u][:, j, :], None, T["scores"],
                                            bass.IndirectOffsetOnAxis(ring[u][:, 0, j:j + 1], 0)).then_inc(gathered[u], 16)
                    pool.indirect_dma_start(row_d[u][:, j, :], None, T["scores"],
                                            bass.IndirectOffsetOnAxis(ring[u][:, 1, j:j + 1], 0)).then_inc(gathered[u], 16)

            def scatter(t, u):
                pool.wait_ge(out_ready[u], t + 1)
                pool.nop(nofuse=True)
                for j in range(4):
                    pool.indirect_dma_start(T["alpha"], bass.IndirectOffsetOnAxis(out_ring[u][:, j:j + 1], 0),
                                            row_o[u][:, j, :], None).then_inc(scattered[u], 16)
            pipeline(pool, (gather, 0))
            pipeline(pool, (scatter, 0))
            for u in range(BUFS):
                pool.wait_ge(scattered[u], 64 * PER_BUF[u])
    end_stage(nc, owned)


def gat_sums(nc, A, T, K):
    with ExitStack() as ctx:
        sb, ps, sem, sems, owned = stage_makers(nc, ctx, "gsu")
        ids = K["ids"]
        raw = sb("raw", [P, CHUNKS, HEADS])
        v = sb("v", [P, HEADS + 1, CHUNKS])
        run = sb("run", [P, HEADS + 1, CHUNKS])
        idx = sb("idx", [P, CHUNKS], I32)
        fidx = sb("fidx", [P, CHUNKS])
        ring = [sb(f"ring{u}", [P, 4], I32) for u in range(BUFS)]
        row_o = [sb(f"row_o{u}", [P, 4, 8]) for u in range(BUFS)]
        zero = sb("zero", [P, SUPER])
        turner = turner_of(sb, ps, sem)
        loaded, chain_v, zeroed, zero_set = sem("loaded"), sem("chain_v"), sem("zeroed"), sem("zero_set")
        out_ready, scattered = sems("out_ready"), sems("scattered")
        raw_zero = sem("raw_zero")
        block = ctx.enter_context(nc.Block())
        width = N * 8 // P
        cuts = list(range(0, width, SUPER)) + [width]

        @block.sync
        def _(sp):
            sp.dma_start(ids[:], T["ids"][1, 0:EP].rearrange("(p f) -> p f", f=CHUNKS)).then_inc(loaded, 16)
            full, tail = E // CHUNKS, E % CHUNKS
            sp.wait_ge(raw_zero, 1)
            sp.dma_start(raw[0:full].rearrange("p f h -> p (f h)"),
                         T["alpha"][0:full * CHUNKS, :].rearrange("(p f) h -> p (f h)", f=CHUNKS)).then_inc(loaded, 16)
            sp.dma_start(raw[full:full + 1, 0:tail].rearrange("p f h -> p (f h)"),
                         T["alpha"][full * CHUNKS:E, :].rearrange("(p f) h -> p (f h)", p=1)).then_inc(loaded, 16)
            sp.wait_ge(zero_set, 1)
            flat = T["nodes"].rearrange("n w -> (n w)").rearrange("(p f) -> p f", p=P)
            for a, b in zip(cuts, cuts[1:]):
                sp.dma_start(flat[:, a:b], zero[:, 0:b - a]).then_inc(zeroed, 16)

        @block.vector
        def _(dve):
            link = chain_of(dve, chain_v)
            dve.memset(zero[:], 0.0).then_inc(zero_set, 1)
            dve.memset(raw[:], 0.0).then_inc(raw_zero, 1)
            link(dve.memset(turner["scr"][:], 0.0))
            link(dve.memset(v[:, HEADS, :], 1.0))
            for u in range(BUFS):
                link(dve.memset(row_o[u][:], 0.0))
            dve.wait_ge(loaded, 48)
            link(dve.tensor_copy(v[:, 0:HEADS, :], raw[:].rearrange("p f h -> p h f")))
            find_segments(dve, link, turner, K["seg"], ids[:])
            each = range(HEADS + 1)
            segment_scan(dve, link, turner, K["seg"], "sum", [run[:, h, :] for h in each], [v[:, h, :] for h in each])
            link(dve.tensor_scalar(fidx[:], K["seg"]["last"][:], -float(NO_ROW), float(NO_ROW), ALU.mult, ALU.add))
            link(dve.tensor_tensor(fidx[:], fidx[:], ids[:], ALU.max))
            link(dve.tensor_copy(idx[:], fidx[:]))

            def give_rows(t, u):
                wait_item(dve, scattered, t, u, 4, 64)
                dve.tensor_copy(row_o[u][:, :, 0:HEADS + 1], four_each(run, t, u).rearrange("p h j -> p j h"))
                dve.tensor_copy(ring[u][:], four(idx, t, u)).then_inc(out_ready[u], 1)
            pipeline(dve, (give_rows, 0))

        @block.tensor
        def _(pe):
            turn_by_tensor(pe, turner, K["ident"])

        @block.gpsimd
        def _(pool):
            pool.wait_ge(zeroed, 16 * (len(cuts) - 1))

            def scatter(t, u):
                pool.wait_ge(out_ready[u], t + 1)
                pool.nop(nofuse=True)
                for j in range(4):
                    pool.indirect_dma_start(T["nodes"], bass.IndirectOffsetOnAxis(ring[u][:, j:j + 1], 0), row_o[u][:, j, :],
                                            None, bounds_check=N - 1, oob_is_err=False).then_inc(scattered[u], 16)
            pipeline(pool, (scatter, 0))
            for u in range(BUFS):
                pool.wait_ge(scattered[u], 64 * PER_BUF[u])
    end_stage(nc, owned)




def over_rows(vector):
    return vector[:].unsqueeze(1).broadcast_to([P, G, D])


def over_columns(scalars):
    return scalars.unsqueeze(2).broadcast_to([P, G, D])


def norm_of(sb, sems, eps, y, o, weight=None):
    norm = {"y": y, "o": o, "eps": eps, "weight": weight}
    for name, shape in [("stats", [P, G, 6]), ("diff", [P, G]), ("mv", [P, G, 2]), ("sd", [P, G]), ("rs", [P, G]), ("nb", [P, G])]:
        norm[name] = [sb(f"{name}{u}", shape) for u in range(BUFS)]
    for name in ("stats_ready", "root_ready", "scale_ready", "normed", "chain", "weighted"):
        norm[name] = sems(f"norm_{name}")
    return norm


def norm_measure(norm, dve, t, u):
    for g in range(G):
        bn = dve.bn_stats(norm["stats"][u][:, g, :], norm["y"][u][:, g, :])
    bn.then_inc(norm["chain"][u], 1)
    dve.wait_ge(norm["chain"][u], 4 * t + 1)
    even, odd = norm["stats"][u][:, :, 0:3], norm["stats"][u][:, :, 3:6]
    dve.tensor_tensor(norm["diff"][u][:], even[:, :, 1], odd[:, :, 1], ALU.subtract)
    dve.tensor_tensor(norm["mv"][u][:, :, 0], even[:, :, 1], odd[:, :, 1], ALU.add)
    dve.tensor_tensor(norm["mv"][u][:, :, 1], even[:, :, 2], odd[:, :, 2], ALU.add).then_inc(norm["chain"][u], 1)
    dve.wait_ge(norm["chain"][u], 4 * t + 2)
    dve.scalar_tensor_tensor(out=norm["diff"][u][:], in0=norm["diff"][u][:], scalar=D / 4.0, in1=norm["diff"][u][:],
                             op0=ALU.mult, op1=ALU.mult).then_inc(norm["chain"][u], 1)
    dve.wait_ge(norm["chain"][u], 4 * t + 3)
    dve.tensor_tensor(norm["mv"][u][:, :, 1], norm["mv"][u][:, :, 1], norm["diff"][u][:], ALU.add).then_inc(norm["stats_ready"][u], 1)


def norm_root(norm, act, t, u):
    act.wait_ge(norm["stats_ready"][u], t + 1)
    act.activation(norm["sd"][u][:], norm["mv"][u][:, :, 1], ACT.Sqrt, bias=norm["eps"][:, 0:1], scale=1.0 / D).then_inc(norm["root_ready"][u], 1)


def norm_scale(norm, dve, t, u):
    dve.wait_ge(norm["root_ready"][u], t + 1)
    wait_item(dve, norm["normed"], t, u, 4)
    dve.reciprocal(norm["rs"][u][:], norm["sd"][u][:]).then_inc(norm["chain"][u], 1)
    dve.wait_ge(norm["chain"][u], 4 * t + 4)
    if norm["weight"] is not None:
        dve.tensor_tensor(norm["rs"][u][:], norm["rs"][u][:], node_scalars(norm["weight"], t, u), ALU.mult).then_inc(norm["weighted"][u], 1)
        dve.wait_ge(norm["weighted"][u], t + 1)
    dve.scalar_tensor_tensor(out=norm["nb"][u][:], in0=norm["mv"][u][:, :, 0], scalar=-0.5, in1=norm["rs"][u][:],
                             op0=ALU.mult, op1=ALU.mult).then_inc(norm["scale_ready"][u], 1)


def norm_apply(norm, act, t, u, stored):
    act.wait_ge(norm["scale_ready"][u], t + 1)
    wait_item(act, stored, t, u, 4, 16)
    for g in range(G):
        ac = act.activation(norm["o"][u][:, g, :], norm["y"][u][:, g, :], ACT.Identity,
                            bias=norm["nb"][u][:, g:g + 1], scale=norm["rs"][u][:, g:g + 1])
    ac.then_inc(norm["normed"][u], 1)


def move_nodes(sp, load, table, tiles, ready, stored):
    def store(t, u):
        sp.wait_ge(ready[u], t + 1)
        if is_item(t, u, ITEMS - 1):
            wait_item(sp, stored, t, u, 1, 16)
        sp.dma_start(node_rows(table, t, u), tiles[u][:]).then_inc(stored[u], 16)
    pipeline(sp, (load, 0), (store, 5))
    for u in range(BUFS):
        sp.wait_ge(stored[u], 16 * PER_BUF[u])


def first_layer(nc, A, T, K):
    with ExitStack() as ctx:
        sb, ps, sem, sems, owned = stage_makers(nc, ctx, "l0")
        x = [sb(f"x{u}", [P, G, D]) for u in range(BUFS)]
        nodes = [sb(f"nodes{u}", [P, G, 8]) for u in range(BUFS)]
        xT = [sb(f"xT{v}", [P, G, P]) for v in range(2)]
        y = [sb(f"y{u}", [P, G, D]) for u in range(BUFS)]
        o = [sb(f"o{u}", [P, G, D]) for u in range(BUFS)]
        xb = [sb(f"xb{v}", [P, G, D]) for v in range(2)]
        tp = [ps(f"tp{v}", [P, G, P]) for v in range(2)]
        hp = [ps(f"hp{v}", [P, G, D]) for v in range(2)]
        loaded, turned, copied, multiplied = sems("loaded"), sems("turned"), sems("copied"), sems("multiplied")
        biased, used, stored, chain = sems("biased"), sems("used"), sems("stored"), sems("chain")
        degrees, roots = sem("degrees"), sem("roots")
        norm = norm_of(sb, sems, K["eps"], y, o)
        block = ctx.enter_context(nc.Block())

        @block.sync
        def _(sp):
            def load(t, u):
                wait_item(sp, turned, t, u, 4)
                wait_item(sp, used, t, u, 4)
                sp.dma_start(x[u][:], node_rows(A["x"], t, u)).then_inc(loaded[u], 16)
                sp.dma_start(nodes[u][:], node_rows(T["nodes"], t, u)).then_inc(loaded[u], 16)
            move_nodes(sp, load, T["x1"], o, norm["normed"], stored)

        @block.gpsimd
        def _(pool):
            def add_bias(t, u):
                pool.wait_ge(loaded[u], 32 * t + 32)
                wait_item(pool, used, t, u, 2)
                pool.tensor_tensor(xb[u % 2][:], x[u][:], over_rows(K["bias0"]), ALU.add).then_inc(biased[u], 1)
            pipeline(pool, (add_bias, 0))

        @block.tensor
        def _(pe):
            def turn(t, u):
                pe.wait_ge(loaded[u], 32 * t + 32)
                wait_item(pe, copied, t, u, 2)
                for g in range(G):
                    tr = pe.transpose(tp[u % 2][:, g, :], x[u][:, g, :], K["ident"][:])
                tr.then_inc(turned[u], 1)

            def multiply(t, u):
                pe.wait_ge(copied[u], t + 1)
                wait_item(pe, used, t, u, 2)
                for g in range(G):
                    mm = pe.matmul(hp[u % 2][:, g, :], xT[u % 2][:, g, :], K["wh"][:], start=True, stop=True)
                mm.then_inc(multiplied[u], 1)
            pipeline(pe, (turn, 0), (multiply, 1))

        @block.scalar
        def _(act):
            def copy(t, u):
                act.wait_ge(turned[u], t + 1)
                wait_item(act, multiplied, t, u, 2)
                act.copy(xT[u % 2][:], tp[u % 2][:]).then_inc(copied[u], 1)
            pipeline(act, (copy, 0), (lambda t, u: norm_root(norm, act, t, u), 2),
                     (lambda t, u: norm_apply(norm, act, t, u, stored), 3))
            act.wait_ge(degrees, ITEMS)
            act.activation(K["dsqrt"][:], K["deg"][:], ACT.Sqrt).then_inc(roots, 1)

        @block.vector
        def _(dve):
            def add(t, u):
                link = loop_chain_of(dve, chain[u], t, 2)
                dve.wait_ge(multiplied[u], t + 1)
                dve.wait_ge(loaded[u], 32 * t + 32)
                wait_item(dve, norm["normed"], t, u, 4)
                link(dve.tensor_tensor(y[u][:].rearrange("p g (a c) -> p g a c", a=HEADS),
                                       hp[u % 2][:].rearrange("p g (a c) -> p g a c", a=HEADS),
                                       nodes[u][:, :, 0:HEADS].unsqueeze(3).broadcast_to([P, G, HEADS, HC]), ALU.mult))
                dve.tensor_scalar(K["deg"][:, bass.ds(BUFS * t + u, 1), :], nodes[u][:, :, HEADS:HEADS + 1].rearrange("p g a -> p a g"),
                                  1.0, None, ALU.add).then_inc(degrees, 1)
                dve.wait_ge(biased[u], t + 1)
                link(dve.tensor_tensor(y[u][:], y[u][:], xb[u % 2][:], ALU.add))
                dve.sem_inc(used[u], 1)
                norm_measure(norm, dve, t, u)
            pipeline(dve, (add, 0), (lambda t, u: norm_scale(norm, dve, t, u), 1))
            dve.wait_ge(roots, 1)
            dve.reciprocal(K["dinv"][:], K["dsqrt"][:])
    end_stage(nc, owned)


def residual_norm(nc, K, name, x_table, factor, agg_table, out_table, weight=None):
    with ExitStack() as ctx:
        sb, ps, sem, sems, owned = stage_makers(nc, ctx, name)
        x = [sb(f"x{u}", [P, G, D]) for u in range(BUFS)]
        agg = [sb(f"agg{u}", [P, G, D]) for u in range(BUFS)]
        y = [sb(f"y{u}", [P, G, D]) for u in range(BUFS)]
        o = [sb(f"o{u}", [P, G, D]) for u in range(BUFS)]
        loaded, used, stored = sems("loaded"), sems("used"), sems("stored")
        norm = norm_of(sb, sems, K["eps"], y, o, weight)
        block = ctx.enter_context(nc.Block())

        @block.sync
        def _(sp):
            def load(t, u):
                wait_item(sp, used, t, u, 4)
                sp.dma_start(x[u][:], node_rows(x_table, t, u)).then_inc(loaded[u], 16)
                sp.dma_start(agg[u][:], node_rows(agg_table, t, u)).then_inc(loaded[u], 16)
            move_nodes(sp, load, out_table, o, norm["normed"], stored)

        @block.vector
        def _(dve):
            def add(t, u):
                dve.wait_ge(loaded[u], 32 * t + 32)
                wait_item(dve, norm["normed"], t, u, 4)
                dve.scalar_tensor_tensor(out=y[u][:], in0=x[u][:], scalar=factor, in1=agg[u][:],
                                         op0=ALU.mult, op1=ALU.add).then_inc(used[u], 1)
                dve.wait_ge(used[u], t + 1)
                norm_measure(norm, dve, t, u)
            pipeline(dve, (add, 0), (lambda t, u: norm_scale(norm, dve, t, u), 1))

        @block.scalar
        def _(act):
            pipeline(act, (lambda t, u: norm_root(norm, act, t, u), 0), (lambda t, u: norm_apply(norm, act, t, u, stored), 1))
    end_stage(nc, owned)


def second_norm(nc, A, T, K):
    residual_norm(nc, K, "n1", T["x1"], 2.0, T["agg"], T["z2"], K["dinv"])


def final_layer(nc, A, T, K, out):
    residual_norm(nc, K, "n3", T["x3"], 1.0, T["agg"], out)


def gcn_nodes(nc, K, name, z_table, weight, bias, agg_table, out_table, x_table=None):
    normed = x_table is not None
    with ExitStack() as ctx:
        sb, ps, sem, sems, owned = stage_makers(nc, ctx, name)
        z = [sb(f"z{u}", [P, G, D]) for u in range(BUFS)]
        agg = [sb(f"agg{u}", [P, G, D]) for u in range(BUFS)]
        uT = [sb(f"uT{v}", [P, G, P]) for v in range(2)]
        y = [sb(f"y{u}", [P, G, D]) for u in range(BUFS)]
        o = [sb(f"o{u}", [P, G, D]) for u in range(BUFS)]
        x = [sb(f"x{u}", [P, G, D]) for u in range(BUFS)] if normed else None
        tp = [ps(f"tp{v}", [P, G, P]) for v in range(2)]
        hp = [ps(f"hp{v}", [P, G, D]) for v in range(2)]
        loaded, summed, turned, copied = sems("loaded"), sems("summed"), sems("turned"), sems("copied")
        multiplied, taken, ready, stored = sems("multiplied"), sems("taken"), sems("ready"), sems("stored")
        x_loaded, x_scaled, x_used, biased = sems("x_loaded"), sems("x_scaled"), sems("x_used"), sems("biased")
        norm = norm_of(sb, sems, K["eps"], y, o) if normed else None
        done = norm["normed"] if normed else ready
        block = ctx.enter_context(nc.Block())

        @block.sync
        def _(sp):
            def load(t, u):
                wait_item(sp, turned, t, u, 4)
                sp.dma_start(z[u][:], node_rows(z_table, t, u)).then_inc(loaded[u], 16)
                sp.dma_start(agg[u][:], node_rows(agg_table, t, u)).then_inc(loaded[u], 16)
                if normed:
                    wait_item(sp, x_used, t, u, 4)
                    sp.dma_start(x[u][:], node_rows(x_table, t, u)).then_inc(x_loaded[u], 16)
            move_nodes(sp, load, out_table, o, done, stored)

        def add(engine, t, u):
            engine.wait_ge(loaded[u], 32 * t + 32)
            engine.tensor_tensor(z[u][:], z[u][:], agg[u][:], ALU.add).then_inc(summed[u], 1)

        @block.tensor
        def _(pe):
            def turn(t, u):
                pe.wait_ge(summed[u], t + 1)
                wait_item(pe, copied, t, u, 2)
                for g in range(G):
                    tr = pe.transpose(tp[u % 2][:, g, :], z[u][:, g, :], K["ident"][:])
                tr.then_inc(turned[u], 1)

            def multiply(t, u):
                pe.wait_ge(copied[u], t + 1)
                wait_item(pe, taken, t, u, 2)
                for g in range(G):
                    mm = pe.matmul(hp[u % 2][:, g, :], uT[u % 2][:, g, :], weight[:], start=True, stop=True)
                mm.then_inc(multiplied[u], 1)
            pipeline(pe, (turn, 0), (multiply, 1))

        @block.scalar
        def _(act):
            def copy(t, u):
                act.wait_ge(turned[u], t + 1)
                wait_item(act, multiplied, t, u, 2)
                act.copy(uT[u % 2][:], tp[u % 2][:]).then_inc(copied[u], 1)

            def activate(t, u):
                act.wait_ge(taken[u], t + 1)
                wait_item(act, stored, t, u, 4, 16)
                for g in range(G):
                    ac = act.activation(o[u][:, g, :], y[u][:, g, :], ACT.Relu,
                                        scale=K["dinv"][:, bass.ds(BUFS * t + u, 1), g])
                ac.then_inc(ready[u], 1)
            if normed:
                pipeline(act, (copy, 0), (lambda t, u: norm_root(norm, act, t, u), 2),
                         (lambda t, u: norm_apply(norm, act, t, u, stored), 3))
            else:
                pipeline(act, (copy, 0), (activate, 2))

        @block.vector
        def _(dve):
            def take(t, u):
                dve.wait_ge(multiplied[u], t + 1)
                wait_item(dve, done, t, u, 4)
                for g in range(G):
                    st = dve.scalar_tensor_tensor(out=y[u][:, g, :], in0=hp[u % 2][:, g, :],
                                                  scalar=K["dinv"][:, bass.ds(BUFS * t + u, 1), g], in1=bias[:],
                                                  op0=ALU.mult, op1=ALU.add)
                st.then_inc(taken[u], 1)
                if normed:
                    dve.wait_ge(taken[u], t + 1)
                    dve.wait_ge(x_scaled[u], t + 1)
                    dve.scalar_tensor_tensor(out=y[u][:], in0=y[u][:], scalar=0.0, in1=x[u][:],
                                             op0=ALU.max, op1=ALU.add).then_inc(x_used[u], 1)
                    dve.wait_ge(x_used[u], t + 1)
                    norm_measure(norm, dve, t, u)
            if normed:
                pipeline(dve, (take, 0), (lambda t, u: norm_scale(norm, dve, t, u), 1))
            else:
                pipeline(dve, (lambda t, u: add(dve, t, u), 0), (take, 2))

        @block.gpsimd
        def _(pool):
            def scale(t, u):
                pool.wait_ge(x_loaded[u], 16 * t + 16)
                pool.tensor_tensor(x[u][:], x[u][:], over_columns(node_scalars(K["dsqrt"], t, u)), ALU.mult).then_inc(x_scaled[u], 1)
            if normed:
                pipeline(pool, (lambda t, u: add(pool, t, u), 0), (scale, 0))
    end_stage(nc, owned)


def gcn_first(nc, A, T, K):
    gcn_nodes(nc, K, "g0", T["z2"], K["w0"], K["b0"], T["agg"], T["z1"])


def gcn_second(nc, A, T, K):
    gcn_nodes(nc, K, "g1", T["z1"], K["w1"], K["b1"], T["agg"], T["x3"], T["z2"])




def attention_scores(nc, A, T, K):
    with ExitStack() as ctx:
        sb, ps, sem, sems, owned = stage_makers(nc, ctx, "asc")
        xs = [sb(f"xs{u}", [P, 4, D]) for u in range(BUFS)]
        xd = [sb(f"xd{u}", [P, 4, D]) for u in range(BUFS)]
        xdT = [sb(f"xdT{v}", [P, 4, P]) for v in range(2)]
        prod = [sb(f"prod{u}", [P, 4, D]) for u in range(BUFS)]
        four_scores = [sb(f"fs{u}", [P, 4]) for u in range(BUFS)]
        ring = [sb(f"ring{u}", [P, 2, 4], I32) for u in range(BUFS)]
        scores = sb("scores", [P, CHUNKS])
        rows = sb("rows", [P, 4, P])
        tp = [ps(f"tp{v}", [P, 4, P]) for v in range(2)]
        qp = [ps(f"qp{v}", [P, 4, D]) for v in range(2)]
        sT = ps("sT", [P, 4, P])
        ring_ready, gathered, turned, copied = sems("ring_ready"), sems("gathered"), sems("turned"), sems("copied")
        multiplied, dotted, kept, stored = sems("multiplied"), sems("dotted"), sems("kept"), sems("stored")
        all_scored, scores_turned, rows_ready, rows_stored = sem("all_scored"), sem("scores_turned"), sem("rows_ready"), sem("rows_stored")
        block = ctx.enter_context(nc.Block())

        @block.gpsimd
        def _(pool):
            def gather(t, u):
                pool.wait_ge(ring_ready[u], t + 1)
                wait_item(pool, dotted, t, u, 4)
                wait_item(pool, stored, t, u, 4, 16)
                pool.nop(nofuse=True)
                for j in range(4):
                    pool.indirect_dma_start(xd[u][:, j, :], None, T["x1"],
                                            bass.IndirectOffsetOnAxis(ring[u][:, 1, j:j + 1], 0)).then_inc(gathered[u], 16)
                    pool.indirect_dma_start(xs[u][:, j, :], None, T["x1"],
                                            bass.IndirectOffsetOnAxis(ring[u][:, 0, j:j + 1], 0)).then_inc(gathered[u], 16)
            pipeline(pool, (gather, 0))

        @block.sync
        def _(sp):
            def store(t, u):
                sp.wait_ge(gathered[u], 128 * t + 128)
                sp.dma_start(edge_rows(T["xsrc"], t, u), xs[u][:]).then_inc(stored[u], 16)
            pipeline(sp, (store, 0))
            sp.wait_ge(rows_ready, 1)
            sp.dma_start(T["w"].rearrange("(r f) -> r f", f=4 * P), rows[0:CHUNKS // 4].rearrange("p b i -> p (b i)")).then_inc(rows_stored, 16)
            sp.wait_ge(rows_stored, 16)
            for u in range(BUFS):
                sp.wait_ge(stored[u], 16 * PER_BUF[u])

        @block.tensor
        def _(pe):
            def turn(t, u):
                pe.wait_ge(gathered[u], 128 * t + 128)
                wait_item(pe, copied, t, u, 2)
                for j in range(4):
                    tr = pe.transpose(tp[u % 2][:, j, :], xd[u][:, j, :], K["ident"][:])
                tr.then_inc(turned[u], 1)

            def multiply(t, u):
                pe.wait_ge(copied[u], t + 1)
                wait_item(pe, dotted, t, u, 2)
                for j in range(4):
                    mm = pe.matmul(qp[u % 2][:, j, :], xdT[u % 2][:, j, :], K["wqk"][:], start=True, stop=True)
                mm.then_inc(multiplied[u], 1)
            pipeline(pe, (turn, 0), (multiply, 0))
            pe.wait_ge(all_scored, 1)
            for b in range(4):
                tr = pe.transpose(sT[0:CHUNKS // 4, b, :], scores[:].rearrange("p (r b) -> p b r", b=4)[:, b, :], K["ident"][:])
            tr.then_inc(scores_turned, 1)

        @block.scalar
        def _(act):
            def copy(t, u):
                act.wait_ge(turned[u], t + 1)
                wait_item(act, multiplied, t, u, 2)
                act.copy(xdT[u % 2][:], tp[u % 2][:]).then_inc(copied[u], 1)
            pipeline(act, (copy, 0))

        @block.vector
        def _(dve):
            def fill_ring(t, u):
                wait_item(dve, gathered, t, u, 4, 128)
                dve.tensor_copy(ring[u][:, 0, :], four(K["src_idx"], t, u))
                dve.tensor_copy(ring[u][:, 1, :], four(K["dst_idx"], t, u)).then_inc(ring_ready[u], 1)

            def dot(t, u):
                dve.wait_ge(multiplied[u], t + 1)
                wait_item(dve, kept, t, u, 4)
                for j in range(4):
                    dt = dve.tensor_tensor_reduce(prod[u][:, j, :], qp[u % 2][:, j, :], xs[u][:, j, :], 1.0, 0.0, ALU.mult, ALU.add,
                                                  four_scores[u][:, j:j + 1])
                dt.then_inc(dotted[u], 1)
                dve.wait_ge(dotted[u], t + 1)
                dve.tensor_copy(four(scores, t, u), four_scores[u][:]).then_inc(kept[u], 1)
            pipeline(dve, (fill_ring, 0), (dot, 4))
            for u in range(BUFS):
                dve.wait_ge(kept[u], PER_BUF[u])
            dve.sem_inc(all_scored, 1)
            dve.wait_ge(scores_turned, 1)
            dve.tensor_copy(rows[0:CHUNKS // 4], sT[0:CHUNKS // 4]).then_inc(rows_ready, 1)
    end_stage(nc, owned)


def attention_softmax(nc, A, T, K):
    with ExitStack() as ctx:
        sb, ps, sem, sems, owned = stage_makers(nc, ctx, "asm")
        e = sb("e", [P, CHUNKS])
        run = sb("run", [P, CHUNKS])
        top = sb("top", [P, CHUNKS])
        tot = sb("tot", [P, CHUNKS])
        rows = sb("rows", [P, 4, P])
        wp = ps("wp", [P, 4, P])
        turner = turner_of(sb, ps, sem)
        loaded, chain_v, shifted, ex_ready = sem("loaded"), sem("chain_v"), sem("shifted"), sem("ex_ready")
        w_ready, w_stored, rows_loaded, rows_turned = sem("w_ready"), sem("w_stored"), sem("rows_loaded"), sem("rows_turned")
        block = ctx.enter_context(nc.Block())
        quarter = CHUNKS // 4

        @block.sync
        def _(sp):
            sp.dma_start(e[:], T["w"].rearrange("(p f) -> p f", f=CHUNKS)).then_inc(loaded, 16)
            sp.wait_ge(w_ready, 1)
            sp.dma_start(T["w"].rearrange("(p f) -> p f", f=CHUNKS), e[:]).then_inc(w_stored, 16)
            sp.wait_ge(w_stored, 16)
            sp.dma_start(rows[0:quarter].rearrange("p b i -> p (b i)"), T["w"].rearrange("(r f) -> r f", f=4 * P)).then_inc(rows_loaded, 16)

        @block.scalar
        def _(act):
            act.wait_ge(shifted, 1)
            act.activation(e[:], e[:], ACT.Exp).then_inc(ex_ready, 1)

        @block.vector
        def _(dve):
            link = chain_of(dve, chain_v)
            link(dve.memset(turner["scr"][:], 0.0))
            link(dve.memset(rows[:], 0.0))
            dve.wait_ge(loaded, 16)
            segment_scan(dve, link, turner, K["seg"], "max", [run[:]], [e[:]])
            segment_scan(dve, link, turner, K["seg"], "fill", [top[:]], [run[:]])
            dve.tensor_tensor(e[:], e[:], top[:], ALU.subtract).then_inc(shifted, 1)
            dve.wait_ge(ex_ready, 1)
            segment_scan(dve, link, turner, K["seg"], "sum", [run[:]], [e[:]])
            segment_scan(dve, link, turner, K["seg"], "fill", [tot[:]], [run[:]])
            link(dve.reciprocal(top[:], tot[:]))
            dve.tensor_tensor(e[:], e[:], top[:], ALU.mult).then_inc(w_ready, 1)
            dve.wait_ge(rows_turned, 1)
            dve.tensor_copy(K["wB"][:].rearrange("p (r b) -> p b r", b=4), wp[:, :, 0:quarter])

        @block.tensor
        def _(pe):
            turn_by_tensor(pe, turner, K["ident"])
            pe.wait_ge(rows_loaded, 16)
            for b in range(4):
                tr = pe.transpose(wp[:, b, :], rows[:, b, :], K["ident"][:])
            tr.then_inc(rows_turned, 1)
    end_stage(nc, owned)


def edge_sums(nc, T, K, name, mode, source):
    mace, attn = mode == "messages", mode == "attention"
    turning = mace or attn
    with ExitStack() as ctx:
        sb, ps, sem, sems, owned = stage_makers(nc, ctx, name)
        xs = [sb(f"xs{u}", [P, 4, D]) for u in range(BUFS)]
        drow = [sb(f"drow{u}", [P, 4, P]) for u in range(BUFS)]
        same = [sb(f"same{u}", [P, 4, P]) for u in range(BUFS)]
        carry = [sb(f"carry{u}", [P, 4, P]) for u in range(BUFS)]
        out = [sb(f"out{u}", [P, 4, D]) for u in range(BUFS)]
        gring = [sb(f"gring{u}", [P, 4], I32) for u in range(BUFS)]
        sring = [sb(f"sring{u}", [P, 4], I32) for u in range(BUFS)]
        op = [ps(f"op{v}", [P, 4, P]) for v in range(2)]
        parts = 2 if mace else 1
        if turning:
            sumT = [sb(f"sumT{v}", [P, parts, 4, P]) for v in range(2)]
            tp = [ps(f"tp{v}", [P, parts, 4, P]) for v in range(2 // parts)]
        if mace:
            msg = [sb(f"msg{u}", [P, 4, 2 * D]) for u in range(BUFS)]
            xsT = [sb(f"xsT{v}", [P, 4, P]) for v in range(2)]
            wt = [sb(f"wt{u}", [P, 4, D]) for u in range(BUFS)]
            tmp = [sb(f"tmp{u}", [P, 4, 3, MUL]) for u in range(BUFS)]
            ws = [sb(f"ws{u}", [P, 4, MUL]) for u in range(BUFS)]
            xtp = ps("xtp", [P, 4, P])
            up = [ps(f"up{v}", [P, 4, D]) for v in range(2)]
        row_loaded, ring_ready, gathered = sems("row_loaded"), sems("ring_ready"), sems("gathered")
        masked, sums_turned, sums_copied = sems("masked"), sems("sums_turned"), sems("sums_copied")
        reduced, copied, scattered, sring_ready = sems("reduced"), sems("copied"), sems("scattered"), sems("sring_ready")
        zero_set = sem("zero_set")
        x_turned, x_copied, up_ready, wt_loaded = sems("x_turned"), sems("x_copied"), sems("up_ready"), sems("wt_loaded")
        msg_ready, msg_chain = sems("msg_ready"), sems("msg_chain")
        block = ctx.enter_context(nc.Block())

        @block.sync
        def _(sp):
            def load(t, u):
                wait_item(sp, masked, t, u, 4)
                sp.dma_start(drow[u][:], T["ids"][1:2, bass.ds(t * (4 * BUFS * P) + u * 4 * P, 4 * P)].broadcast_to([P, 4 * P])).then_inc(row_loaded[u], 16)
                if attn:
                    wait_item(sp, sums_turned, t, u, 4)
                    sp.dma_start(xs[u][:], edge_rows(T["xsrc"], t, u)).then_inc(gathered[u], 16)
                if mace:
                    wait_item(sp, msg_ready, t, u, 4)
                    sp.dma_start(wt[u][:], edge_rows(T["radial"], t, u)).then_inc(wt_loaded[u], 16)
            pipeline(sp, (load, 0))

        @block.gpsimd
        def _(pool):
            def gather(t, u):
                pool.wait_ge(ring_ready[u], t + 1)
                if mace:
                    wait_item(pool, x_turned, t, u, 4)
                else:
                    wait_item(pool, reduced, t, u, 4, 4)
                pool.nop(nofuse=True)
                for j in range(4):
                    pool.indirect_dma_start(xs[u][:, j, :], None, source,
                                            bass.IndirectOffsetOnAxis(gring[u][:, j:j + 1], 0)).then_inc(gathered[u], 16)

            def scatter(t, u):
                pool.wait_ge(sring_ready[u], t + 1)
                pool.wait_ge(copied[u], 4 * t + 4)
                pool.nop(nofuse=True)
                for j in range(4):
                    pool.indirect_dma_start(T["agg"], bass.IndirectOffsetOnAxis(sring[u][:, j:j + 1], 0), out[u][:, j, :], None,
                                            bounds_check=N - 1, oob_is_err=False).then_inc(scattered[u], 16)
            if attn:
                pipeline(pool, (scatter, 0))
            else:
                pipeline(pool, (gather, 0), (scatter, 3 if mace else 2))
            for u in range(BUFS):
                pool.wait_ge(scattered[u], 64 * PER_BUF[u])

        @block.tensor
        def _(pe):
            def turn_x(t, u):
                pe.wait_ge(gathered[u], 64 * t + 64)
                wait_item(pe, x_copied, t, u, 1)
                for j in range(4):
                    tr = pe.transpose(xtp[:, j, :], xs[u][:, j, :], K["ident"][:])
                tr.then_inc(x_turned[u], 1)

            def project(t, u):
                pe.wait_ge(x_copied[u], t + 1)
                wait_item(pe, msg_ready, t, u, 2)
                for j in range(4):
                    mm = pe.matmul(up[u % 2][:, j, :], xsT[u % 2][:, j, :], K["wup"][:], start=True, stop=True)
                mm.then_inc(up_ready[u], 1)

            def turn_sums(t, u):
                pe.wait_ge(masked[u], t + 1)
                if mace:
                    pe.wait_ge(msg_ready[u], t + 1)
                else:
                    pe.wait_ge(gathered[u], 16 * t + 16)
                wait_item(pe, sums_copied, t, u, len(tp))
                for a in range(parts):
                    for j in range(4):
                        rows = msg[u][:, j, a * D:(a + 1) * D] if mace else xs[u][:, j, :]
                        mm = pe.matmul(tp[u % len(tp)][:, a, j, :], rows, same[u][:, j, :], start=True, stop=True)
                mm.then_inc(sums_turned[u], 1)

            def reduce(t, u):
                pe.wait_ge(masked[u], t + 1)
                if turning:
                    pe.wait_ge(sums_copied[u], t + 1)
                else:
                    pe.wait_ge(gathered[u], 64 * t + 64)
                for j in range(4):
                    o = op[j % 2][:, 0, :]
                    if mace:
                        for a in range(parts):
                            pe.matmul(o, sumT[u % 2][:, a, j, :], K["wout"][:, a, :], start=(a == 0), stop=False)
                    elif attn:
                        pe.matmul(o, sumT[u % 2][:, 0, j, :], K["wvo"][:], start=True, stop=False)
                    else:
                        pe.matmul(o, same[u][:, j, :], xs[u][:, j, :], start=True, stop=False)
                    if j:
                        pe.wait_ge(copied[u], 4 * t + j)
                    else:
                        wait_item(pe, copied, t, u, 1, 4)
                    before = out[u][:, j - 1, :] if j else out[(u - 1) % BUFS][:, 3, :]
                    pe.matmul(o, carry[u][:, j, :], before, start=False, stop=True).then_inc(reduced[u], 1)
            pe.wait_ge(zero_set, 1)
            if mace:
                pipeline(pe, (turn_x, 0), (project, 0), (turn_sums, 1), (reduce, 2))
            elif attn:
                pipeline(pe, (turn_sums, 0), (reduce, 1))
            else:
                pipeline(pe, (reduce, 0))

        @block.scalar
        def _(act):
            def copy_x(t, u):
                act.wait_ge(x_turned[u], t + 1)
                wait_item(act, up_ready, t, u, 2)
                act.copy(xsT[u % 2][:], xtp[:]).then_inc(x_copied[u], 1)

            def copy_sums(t, u):
                act.wait_ge(sums_turned[u], t + 1)
                wait_item(act, reduced, t, u, 2, 4)
                act.copy(sumT[u % 2][:], tp[u % len(tp)][:]).then_inc(sums_copied[u], 1)

            def copy_out(t, u):
                wait_item(act, scattered, t, u, 4, 64)
                for j in range(4):
                    act.wait_ge(reduced[u], 4 * t + j + 1)
                    act.copy(out[u][:, j, :], op[j % 2][:, 0, :]).then_inc(copied[u], 1)
            if mace:
                pipeline(act, (copy_x, 0), (copy_sums, 1), (copy_out, 2))
            elif attn:
                pipeline(act, (copy_sums, 0), (copy_out, 1))
            else:
                pipeline(act, (copy_out, 0))

        @block.vector
        def _(dve):
            def fill_ring(t, u):
                wait_item(dve, gathered, t, u, 4, 64)
                dve.tensor_copy(gring[u][:], four(K["src_idx"], t, u)).then_inc(ring_ready[u], 1)

            def masks(t, u):
                wait_item(dve, scattered, t, u, 4, 64)
                dve.tensor_copy(sring[u][:], four(K["scat_idx"], t, u)).then_inc(sring_ready[u], 1)
                dve.wait_ge(row_loaded[u], 16 * t + 16)
                wait_item(dve, reduced, t, u, 4, 4)
                chunk = 4 * BUFS * t + 4 * u
                for j in range(4):
                    key = K["dstB"][:, bass.ds(chunk + j, 1)]
                    if attn:
                        dve.tensor_scalar(same[u][:, j, :], drow[u][:, j, :], key, K["wB"][:, bass.ds(chunk + j, 1)],
                                          ALU.is_equal, ALU.mult)
                    else:
                        dve.tensor_scalar(same[u][:, j, :], drow[u][:, j, :], key, None, ALU.is_equal)
                    mk = dve.tensor_scalar(carry[u][:, j, :], drow[u][:, j, :], K["carry_key"][:, bass.ds(chunk + j, 1)],
                                           None, ALU.is_equal)
                mk.then_inc(masked[u], 1)

            def messages(t, u):
                link = loop_chain_of(dve, msg_chain[u], t, 4)
                dve.wait_ge(wt_loaded[u], 16 * t + 16)
                dve.wait_ge(up_ready[u], t + 1)
                wait_item(dve, sums_turned, t, u, 4)
                w = wt[u][:].rearrange("p j (q k) -> p j q k", q=4)
                v = up[u % 2][:].rearrange("p j (q k) -> p j q k", q=4)
                m = msg[u][:].rearrange("p j (q k) -> p j q k", q=8)
                axes = K["rhatB"][:, :, bass.ds(4 * BUFS * t + 4 * u, 4)].rearrange("p c j -> p j c").unsqueeze(3).broadcast_to([P, 4, 3, MUL])
                dve.tensor_tensor(m[:, :, 0], w[:, :, 0], v[:, :, 0], ALU.mult)
                link(dve.tensor_tensor(ws[u][:], w[:, :, 1], v[:, :, 0], ALU.mult))
                dve.tensor_tensor(m[:, :, 2:5], ws[u][:].unsqueeze(2).broadcast_to([P, 4, 3, MUL]), axes, ALU.mult)
                dve.tensor_tensor(m[:, :, 5:8], w[:, :, 2].unsqueeze(2).broadcast_to([P, 4, 3, MUL]), v[:, :, 1:4], ALU.mult)
                link(dve.tensor_tensor(tmp[u][:], v[:, :, 1:4], axes, ALU.mult))
                link(dve.tensor_tensor(tmp[u][:, :, 0], tmp[u][:, :, 0], tmp[u][:, :, 1], ALU.add))
                link(dve.tensor_tensor(tmp[u][:, :, 0], tmp[u][:, :, 0], tmp[u][:, :, 2], ALU.add))
                dve.tensor_tensor(m[:, :, 1], w[:, :, 3], tmp[u][:, :, 0], ALU.mult).then_inc(msg_ready[u], 1)

            dve.memset(out[BUFS - 1][:, 3, :], 0.0).then_inc(zero_set, 1)
            if mace:
                pipeline(dve, (fill_ring, 0), (masks, 3), (messages, 4))
            elif attn:
                pipeline(dve, (masks, 0))
            else:
                pipeline(dve, (fill_ring, 0), (masks, 3))
    end_stage(nc, owned)


def attention_sums(nc, A, T, K):
    edge_sums(nc, T, K, "ats", "attention", None)


def gcn_sums_first(nc, A, T, K):
    edge_sums(nc, T, K, "gs0", "gcn", T["z2"])


def gcn_sums_second(nc, A, T, K):
    edge_sums(nc, T, K, "gs1", "gcn", T["z1"])


def message_sums(nc, A, T, K):
    edge_sums(nc, T, K, "mss", "messages", T["x3"])


def radial_basis(nc, A, T, K):
    with ExitStack() as ctx:
        sb, ps, sem, sems, owned = stage_makers(nc, ctx, "rad")
        rows = 8 * NB
        r = sb("r", [P, EIGHTS, P])
        part = sb("part", [P, 1], I32)
        center = sb("center", [P, 1])
        inside = sb("inside", [P, EIGHTS * P])
        chain_v, loaded, iota_ready, clipped, squared, expd = [sem(n) for n in ("chain_v", "loaded", "iota_ready", "clipped", "squared", "expd")]
        w_loaded, w_zero = sem("w_loaded"), sem("w_zero")
        block = ctx.enter_context(nc.Block())

        @block.gpsimd
        def _(pool):
            pool.iota(part[:], pattern=[[0, 1]], base=0, channel_multiplier=1).then_inc(iota_ready, 1)

        @block.sync
        def _(sp):
            for g in range(8):
                chunks = T["ew"].rearrange("a (t g i) -> a g t i", g=8, i=P)[:, g]
                sp.dma_start(r[NB * g:NB * (g + 1)], chunks.broadcast_to([NB, EIGHTS, P])).then_inc(loaded, 16)
            sp.wait_ge(w_zero, 1)
            for g in range(8):
                sp.dma_start(K["m0g"][NB * g:NB * (g + 1), g, 0:64], A["L3_gnn_mlp_w0"]).then_inc(w_loaded, 16)
            sp.wait_ge(w_loaded, 128)

        @block.vector
        def _(dve):
            link = chain_of(dve, chain_v)
            dve.memset(K["m0g"][:], 0.0).then_inc(w_zero, 1)
            link(dve.memset(K["emb"][:], 0.0))
            dve.wait_ge(iota_ready, 1)
            link(dve.tensor_scalar(part[:], part[:], NB - 1, None, ALU.bitwise_and))
            link(dve.tensor_scalar(center[:], part[:], -1.0, None, ALU.mult))
            dve.wait_ge(loaded, 128)
            flat = r[0:rows].rearrange("p t i -> p (t i)")
            link(dve.tensor_scalar(inside[0:rows], flat, 1.0, float(NB) ** 0.5, ALU.is_le, ALU.mult))
            dve.tensor_scalar(flat, flat, 0.0, 1.0, ALU.max, ALU.min).then_inc(clipped, 1)
            dve.wait_ge(expd, 1)
            dve.tensor_tensor(K["emb"][0:rows], flat, inside[0:rows], ALU.mult)

        @block.scalar
        def _(act):
            flat = r[0:rows].rearrange("p t i -> p (t i)")
            act.wait_ge(clipped, 1)
            act.activation(flat, flat, ACT.Square, bias=center[0:rows, 0:1], scale=float(NB - 1)).then_inc(squared, 1)
            act.wait_ge(squared, 1)
            act.activation(flat, flat, ACT.Exp, scale=-0.5).then_inc(expd, 1)
    end_stage(nc, owned)


def radial_block(K, t, u):
    return K["emb"][:, bass.ds(t * (BUFS // 2 * P) + u // 2 * P, P)]




def tables(nc, shown=()):
    T = {}
    def dram(name, shape, dtype=F32):
        return nc.dram_tensor(name, shape, dtype, kind="ExternalOutput" if name in shown else "Internal").ap()
    T["ids"] = dram("t_ids", (2, EP + P))
    T["ew"] = dram("t_ew", (1, EP))
    T["up"] = dram("t_up", (D, D))
    T["sorted"] = dram("t_sorted", (3, SORTN))
    T["scores"] = dram("t_scores", (N, 8))
    T["alpha"] = dram("t_alpha", (SORTN, HEADS))
    T["nodes"] = dram("t_nodes", (N, 8))
    T["agg"] = dram("t_agg", (N, D))
    T["xsrc"] = dram("t_xsrc", (EP, D))
    T["radial"] = dram("t_radial", (EP, D))
    T["w"] = dram("t_w", (EP,))
    T["x1"] = dram("t_x1", (N, D))
    T["z2"] = dram("t_z2", (N, D))
    T["z1"] = dram("t_z1", (N, D))
    T["x3"] = dram("t_x3", (N, D))
    return T


def kept(sb):
    K = {}
    K["ident"] = sb("ident", [P, P])
    for_weights = [P, D]
    K["w0"], K["w1"], K["wh"] = sb("w0", for_weights), sb("w1", for_weights), sb("wh", for_weights)
    K["wqk"], K["wvo"], K["wup"] = sb("wqk", for_weights), sb("wvo", for_weights), sb("wup", for_weights)
    K["wout"] = sb("wout", [P, 2, D])
    K["wa"] = sb("wa", [P, 8])
    K["bias0"], K["b0"], K["b1"], K["mb2"] = [sb(n, for_weights) for n in ("bias0", "b0", "b1", "mb2")]
    K["m0"], K["m1"], K["m2"] = [sb(n, for_weights) for n in ("m0", "m1", "m2")]
    K["mb0"], K["mb1"], K["eps"] = [sb(n, [P, 1]) for n in ("mb0", "mb1", "eps")]
    K["dstB"], K["carry_key"] = sb("dstB", [P, CHUNKS]), sb("carry_key", [P, CHUNKS])
    K["rhatB"] = sb("rhatB", [P, 3, CHUNKS])
    K["src_idx"], K["dst_idx"], K["scat_idx"] = [sb(n, [P, CHUNKS], I32) for n in ("src_idx", "dst_idx", "scat_idx")]
    K["ids"] = sb("ids", [P, CHUNKS])
    K["seg"] = segment_tiles(sb, "dst", HEADS + 1)
    K["deg"] = sb("deg", [P, NSUPER, G])
    K["dinv"] = sb("dinv", [P, NSUPER, G])
    K["wB"] = sb("wB", [P, CHUNKS])
    K["m0g"] = sb("m0g", [P, 8, P])
    K["emb"] = sb("emb", [P, EIGHTS * P])
    K["dsqrt"] = sb("dsqrt", [P, NSUPER, G])
    return K


def build(nc, A, out, stop=99, shown=()):
    T = tables(nc, shown)
    with ExitStack() as ctx:
        K = kept(stage_makers(nc, ctx, "kept")[0])
        for stage in STAGES[:stop]:
            stage(nc, A, T, K) if stage is not final_layer else stage(nc, A, T, K, out)


STAGES = [prepare, radial_basis, sort_and_scores, gat_softmax, gat_sums, first_layer, attention_scores, attention_softmax,
          attention_sums, second_norm, gcn_sums_first, gcn_first, gcn_sums_second, gcn_second, message_sums,
          final_layer]


_INS = ["x", "src", "dst", "edge_attr_3", "edge_weight", "L0_gnn_W", "L0_gnn_att", "L0_gnn_bias", "L1_gnn_Wq", "L1_gnn_Wk",
        "L1_gnn_Wv", "L1_gnn_Wo", "L2_gnn_W0", "L2_gnn_b0", "L2_gnn_W1", "L2_gnn_b1", "L3_gnn_W_up0", "L3_gnn_W_up1",
        "L3_gnn_mlp_w0", "L3_gnn_mlp_b0", "L3_gnn_mlp_w1", "L3_gnn_mlp_b1", "L3_gnn_mlp_w2", "L3_gnn_mlp_b2",
        "L3_gnn_W_out0", "L3_gnn_W_out1"]


def kernel(**inputs):
    import numpy as _np
    import concourse.bacc as _bacc
    from concourse import mybir as _mybir
    from concourse.bass_utils import run_bass_kernel_spmd as _run

    nc = _bacc.Bacc("TRN2", target_bir_lowering=False, num_devices=1)
    arrays, args = {}, {}
    for name in _INS:
        a = _np.ascontiguousarray(inputs[name])
        arrays[f"in_{name}_dram"] = a
        args[name] = nc.dram_tensor(f"in_{name}_dram", a.shape, _mybir.dt.from_np(a.dtype), kind="ExternalInput").ap()
    out = nc.dram_tensor("out_0_dram", (N, D), F32, kind="ExternalOutput").ap()
    build(nc, args, out)
    r = _run(nc, [arrays], core_ids=[0])
    return r.results[0]["out_0_dram"]
```

```python
from contextlib import ExitStack

import concourse.bass as bass
from concourse import mybir

ALU = mybir.AluOpType
ACT = mybir.ActivationFunctionType
F32 = mybir.dt.float32
I32 = mybir.dt.int32

P = 128
N = 100000
E = 50000
D = 128
HEADS = 4
HC = D // HEADS
CHUNKS = 392
EP = CHUNKS * P
SORTN = 65536
SORTF = SORTN // P
G = 8
SUPER = P * G
NSUPER = -(-N // SUPER)
LAST = N - SUPER
BUFS = 4
ITEMS = NSUPER
EIGHTS = CHUNKS // 8
PER_BUF = [-(-(ITEMS - u) // BUFS) for u in range(BUFS)]
PAD_ID = 1 << 17
NO_ROW = 1 << 20
BIG = 1.0e30
EPS = 1e-5
ROW1 = D + 4
NB = 8
MUL = 32
AVG = 16.0
assert CHUNKS == 4 * ITEMS and EP >= E and N < PAD_ID


def stage_makers(nc, ctx, stage):
    owned = []

    def sb(name, shape, dtype=F32):
        return ctx.enter_context(nc.sbuf_tensor(f"{stage}_{name}", shape, dtype))

    def ps(name, shape, dtype=F32):
        return ctx.enter_context(nc.psum_tensor(f"{stage}_{name}", shape, dtype))

    def sem(name):
        owned.append(nc.alloc_semaphore(f"{stage}_{name}"))
        return owned[-1]

    def sems(name):
        return [sem(f"{name}{i}") for i in range(BUFS)]

    return sb, ps, sem, sems, owned


def end_stage(nc, owned):
    nc.clear_and_free_semaphores(owned)
    nc.all_engine_barrier()


def chain_of(engine, sem):
    count = [0]

    def link(instruction):
        count[0] += 1
        instruction.then_inc(sem, 1)
        engine.wait_ge(sem, count[0])
    return link


def loop_chain_of(engine, sem, t, per):
    count = [0]

    def link(instruction):
        count[0] += 1
        assert count[0] <= per
        instruction.then_inc(sem, 1)
        engine.wait_ge(sem, t * per + count[0])
    return link


def of_item(sems, t, u, back, by=1):
    return sems[(u - back) % BUFS], (t + (u - back) // BUFS) * by + by


def wait_item(engine, sems, t, u, back, by=1):
    if not isinstance(t, int) or BUFS * t + u - back >= 0:
        engine.wait_ge(*of_item(sems, t, u, back, by))


def pipeline(engine, *parts, first=0, last=None):
    latest = max(lag for _, lag in parts)
    last = ITEMS + latest if last is None else last
    start = max(1 + -(-latest // BUFS) + 1, -(-first // BUFS))
    end = min(last, ITEMS) // BUFS

    def slot(t, u):
        for f, lag in parts:
            v = u - lag
            if not isinstance(t, int) or 0 <= BUFS * t + v < ITEMS:
                f(t + v // BUFS, v % BUFS)
    for q in range(first, start * BUFS):
        slot(q // BUFS, q % BUFS)
    with engine.Fori(start, end) as t:
        for u in range(BUFS):
            slot(t, u)
    for q in range(end * BUFS, last):
        slot(q // BUFS, q % BUFS)


def is_item(t, u, item):
    return isinstance(t, int) and BUFS * t + u == item


def node_rows(table, t, u):
    base = LAST if is_item(t, u, ITEMS - 1) else t * (BUFS * SUPER) + u * SUPER
    return table[bass.ds(base, SUPER), :].rearrange("(p g) d -> p g d", g=G)


def node_scalars(table, t, u):
    return table[:, bass.ds(BUFS * t + u, 1), :].rearrange("p a g -> p (a g)")


def four(tile, t, u):
    return tile[:, bass.ds(4 * BUFS * t + 4 * u, 4)]


def four_each(tile, t, u):
    return tile[:, :, bass.ds(4 * BUFS * t + 4 * u, 4)]


def edge_rows(table, t, u):
    return table[bass.ds(t * (4 * BUFS * P) + u * 4 * P, 4 * P), :].rearrange("(j p) d -> p j d", p=P)




def prepare(nc, A, T, K):
    with ExitStack() as ctx:
        sb, ps, sem, sems, owned = stage_makers(nc, ctx, "prep")
        ints = sb("ints", [P, 2, CHUNKS], I32)
        flts = sb("flts", [P, 2, CHUNKS])
        wts = sb("wts", [P, 6, D])
        wT = sb("wT", [P, 5, D])
        att8 = sb("att8", [P, 8])
        zeros = sb("zeros", [P, SUPER])
        ew = sb("ew", [P, CHUNKS])
        ones = sb("ones", [P, P])
        rows = CHUNKS // 4
        cur = sb("cur", [P, 4, P])
        nxt = sb("nxt", [P, 4, P])
        srow = sb("srow", [P, 4, P])
        vec = sb("vec", [P, 4 * P, 3])
        scat = sb("scat", [P, 4, P])
        rnorm = sb("rnorm", [P, 4 * P])
        sq = sb("sq", [P, 4 * P, 3])
        rinv = sb("rinv", [P, 4 * P])
        rhatR = sb("rhatR", [P, 3, 4, P])
        scatB = sb("scatB", [P, CHUNKS])
        dshift = sb("dshift", [P, CHUNKS])
        srcB = sb("srcB", [P, CHUNKS])
        wo0 = sb("wo0", [P, 2, MUL])
        pw = ps("pw", [P, 4, P])
        pw2 = ps("pw2", [P, 4, P])
        pt = ps("pt", [P, 4, P])
        chain_v = sem("chain_v")
        chain_g = sem("chain_g")
        pads_set = sem("pads_set")
        ids_loaded = sem("ids_loaded")
        ids_float = sem("ids_float")
        ids_stored = sem("ids_stored")
        small_loaded = sem("small_loaded")
        vec_loaded = sem("vec_loaded")
        rows_loaded = sem("rows_loaded")
        ident_ready = sem("ident_ready")
        w_loaded = sem("w_loaded")
        zeros_set = sem("zeros_set")
        up_built = sem("up_built")
        pe_done = sem("pe_done")
        pe_used = sem("pe_used")
        sumsq_ready = sem("sumsq_ready")
        norm_ready = sem("norm_ready")
        chunkify = sem("chunkify")
        full_rows, tail = E // (4 * P), E % (4 * P)
        full_lines, tail_line = E // CHUNKS, E % CHUNKS
        block = ctx.enter_context(nc.Block())

        @block.gpsimd
        def _(pool):
            link = chain_of(pool, chain_g)
            link(pool.memset(ones[:], 1.0))
            pool.affine_select(out=K["ident"][:], in_=ones[:], compare_op=ALU.is_equal, fill=0.0,
                               base=0, pattern=[[-1, P]], channel_multiplier=1).then_inc(ident_ready, 1)

        @block.sync
        def _(sp):
            sp.wait_ge(pads_set, 1)
            for a, name in enumerate(["src", "dst"]):
                ids = A[name]
                sp.dma_start(ints[0:full_lines, a, :],
                             ids[0:full_lines * CHUNKS].rearrange("(p f) -> p f", f=CHUNKS)).then_inc(ids_loaded, 16)
                sp.dma_start(ints[full_lines:full_lines + 1, a, 0:tail_line],
                             ids[full_lines * CHUNKS:E].rearrange("(p f) -> p f", p=1)).then_inc(ids_loaded, 16)
            sp.dma_start(ew[0:full_lines, :],
                         A["edge_weight"][0:full_lines * CHUNKS].rearrange("(p f) -> p f", f=CHUNKS)).then_inc(ids_loaded, 16)
            sp.dma_start(ew[full_lines:full_lines + 1, 0:tail_line],
                         A["edge_weight"][full_lines * CHUNKS:E].rearrange("(p f) -> p f", p=1)).then_inc(ids_loaded, 16)
            flat3 = A["edge_attr_3"].rearrange("e c -> (e c)")
            sp.dma_start(vec[0:full_rows].rearrange("p a c -> p (a c)"),
                         flat3[0:full_rows * 12 * P].rearrange("(p f) -> p f", f=12 * P)).then_inc(vec_loaded, 16)
            sp.dma_start(vec[full_rows:full_rows + 1, 0:tail, :].rearrange("p a c -> p (a c)"),
                         flat3[full_rows * 12 * P:3 * E].rearrange("(p f) -> p f", p=1)).then_inc(vec_loaded, 16)
            sp.wait_ge(ids_float, 2)
            for a in range(2):
                sp.dma_start(T["ids"][a, 0:EP].rearrange("(p f) -> p f", f=CHUNKS), flts[:, a, :]).then_inc(ids_stored, 16)
            sp.dma_start(T["ids"][1:2, EP:EP + P], flts[P - 1:P, 1, CHUNKS - P:CHUNKS]).then_inc(ids_stored, 16)
            sp.dma_start(T["ew"][0:1, :].rearrange("a (p f) -> (a p) f", f=CHUNKS), ew[:]).then_inc(ids_stored, 16)
            sp.wait_ge(ids_stored, 64)
            for tile, a, off in [(cur, 1, 0), (nxt, 1, 1), (srow, 0, 0)]:
                sp.dma_start(tile[0:rows].rearrange("p b i -> p (b i)"),
                             T["ids"][a, off:off + EP].rearrange("(p f) -> p f", f=4 * P)).then_inc(rows_loaded, 16)

        @block.scalar
        def _(act):
            names = ["L0_gnn_W", "L1_gnn_Wq", "L1_gnn_Wk", "L1_gnn_Wv", "L1_gnn_Wo"]
            for i, name in enumerate(names):
                act.dma_start(wts[:, i, :], A[name]).then_inc(w_loaded, 16)
            act.dma_start(K["w0"][:], A["L2_gnn_W0"]).then_inc(w_loaded, 16)
            act.dma_start(K["w1"][:], A["L2_gnn_W1"]).then_inc(w_loaded, 16)
            act.dma_start(K["wh"][:], A["L0_gnn_W"]).then_inc(w_loaded, 16)
            for tile, name in [(K["bias0"], "L0_gnn_bias"), (K["b0"], "L2_gnn_b0"), (K["b1"], "L2_gnn_b1"), (K["mb2"], "L3_gnn_mlp_b2")]:
                act.dma_start(tile[:], A[name].rearrange("(a d) -> a d", a=1).broadcast_to([P, D])).then_inc(w_loaded, 16)
            act.wait_ge(zeros_set, 1)
            att = A["L0_gnn_att"]
            for h in range(HEADS):
                for s in range(2):
                    act.dma_start(att8[h * HC:(h + 1) * HC, 4 * s + h:4 * s + h + 1],
                                  att[0, h, s * HC:(s + 1) * HC].rearrange("(c a) -> c a", a=1)).then_inc(small_loaded, 16)
            act.dma_start(K["m0"][0:NB, 0:64], A["L3_gnn_mlp_w0"]).then_inc(small_loaded, 16)
            act.dma_start(K["m1"][0:64, 0:64], A["L3_gnn_mlp_w1"]).then_inc(small_loaded, 16)
            act.dma_start(K["m2"][0:64, :], A["L3_gnn_mlp_w2"]).then_inc(small_loaded, 16)
            act.dma_start(K["mb0"][0:64, :], A["L3_gnn_mlp_b0"].rearrange("(c a) -> c a", a=1)).then_inc(small_loaded, 16)
            act.dma_start(K["mb1"][0:64, :], A["L3_gnn_mlp_b1"].rearrange("(c a) -> c a", a=1)).then_inc(small_loaded, 16)
            act.dma_start(T["up"], zeros[:, 0:D]).then_inc(up_built, 16)
            act.wait_ge(up_built, 16)
            act.dma_start(T["up"][0:MUL, 0:MUL], A["L3_gnn_W_up0"]).then_inc(up_built, 16)
            for c in range(3):
                act.dma_start(T["up"][MUL + c:D:3, MUL * (c + 1):MUL * (c + 2)], A["L3_gnn_W_up1"]).then_inc(up_built, 16)
            act.wait_ge(up_built, 80)
            act.dma_start(wts[:, 5, :], T["up"]).then_inc(small_loaded, 16)
            for q, (part, row) in enumerate([(0, 0), (0, MUL), (1, 0), (1, 0)]):
                name = ["L3_gnn_W_out0", "L3_gnn_W_out1"][part]
                act.dma_start(wo0[q * MUL:(q + 1) * MUL, 0, :], A[name][row:row + MUL, :]).then_inc(small_loaded, 16)
            for q, row in enumerate([0, MUL, MUL, MUL]):
                act.dma_start(wo0[q * MUL:(q + 1) * MUL, 1, :], A["L3_gnn_W_out1"][row:row + MUL, :]).then_inc(small_loaded, 16)
            act.wait_ge(sumsq_ready, 1)
            nc.scalar.activation(rnorm[:], sq[:, :, 0], ACT.Sqrt).then_inc(norm_ready, 1)

        N_SMALL = 2 * HEADS + 5 + 1 + 8

        @block.vector
        def _(dve):
            link = chain_of(dve, chain_v)
            dve.memset(ints[:, 0, :], PAD_ID)
            link(dve.memset(ints[:, 1, :], PAD_ID))
            dve.memset(ew[:], 0.0)
            link(dve.memset(vec[:], 0.0))
            dve.memset(att8[:], 0.0).then_inc(pads_set, 1)
            link(dve.memset(zeros[:], 0.0))
            dve.memset(K["m0"][:], 0.0)
            dve.memset(K["m1"][:], 0.0)
            dve.memset(K["m2"][:], 0.0)
            dve.memset(K["mb0"][:], 0.0)
            link(dve.memset(K["mb1"][:], 0.0))
            dve.memset(K["one"][:], 1.0)
            dve.memset(K["quarter_eps"][:], EPS / 4.0)
            dve.memset(K["eps"][:], EPS).then_inc(zeros_set, 1)
            dve.wait_ge(ids_loaded, 96)
            dve.tensor_copy(flts[:, 0, :], ints[:, 0, :]).then_inc(ids_float, 1)
            dve.tensor_copy(flts[:, 1, :], ints[:, 1, :]).then_inc(ids_float, 1)
            dve.wait_ge(vec_loaded, 32)
            link(dve.tensor_tensor(sq[:], vec[:], vec[:], ALU.mult))
            link(dve.tensor_tensor(sq[:, :, 0], sq[:, :, 0], sq[:, :, 1], ALU.add))
            dve.tensor_tensor(sq[:, :, 0], sq[:, :, 0], sq[:, :, 2], ALU.add).then_inc(sumsq_ready, 1)
            dve.wait_ge(norm_ready, 1)
            link(dve.tensor_scalar(rnorm[:], rnorm[:], 1e-12, None, ALU.add))
            link(dve.reciprocal(rinv[:], rnorm[:]))
            for c in range(3):
                link(dve.tensor_tensor(rhatR[:, c].rearrange("p b i -> p (b i)"), vec[:, :, c], rinv[:], ALU.mult))
            dve.wait_ge(rows_loaded, 48)
            link(dve.memset(scat[:], 0.0))
            link(dve.tensor_tensor(scat[0:rows], cur[0:rows], nxt[0:rows], ALU.is_equal))
            link(dve.scalar_tensor_tensor(out=scat[0:rows], in0=scat[0:rows], scalar=float(NO_ROW), in1=cur[0:rows],
                                          op0=ALU.mult, op1=ALU.max))
            dve.sem_inc(chunkify, 1)
            blocks = [(cur, K["dstB"][:]), (scat, scatB[:]), (srow, srcB[:])] + \
                     [(rhatR[:, c], K["rhatB"][:, c, :]) for c in range(3)]
            for n, (_, out) in enumerate(blocks):
                dve.wait_ge(pe_done, n + 1)
                dve.tensor_copy(out.rearrange("p (r b) -> p b r", b=4), pt[:, :, 0:rows]).then_inc(pe_used, 1)
            dve.wait_ge(pe_used, len(blocks))
            for tile in (K["scat_idx"], K["src_idx"], K["dst_idx"]):
                link(dve.memset(tile[:], 0))
            dve.tensor_copy(K["scat_idx"][:, 0:CHUNKS], scatB[:])
            dve.tensor_scalar(K["src_idx"][:, 0:CHUNKS], srcB[:], float(N - 1), None, ALU.min)
            dve.tensor_scalar(K["dst_idx"][:, 0:CHUNKS], K["dstB"][:], float(N - 1), None, ALU.min)
            link(dve.memset(dshift[:], 0.0))
            dve.wait_ge(ident_ready, 1)
            link(dve.tensor_scalar(dshift[:, 1:CHUNKS], K["dstB"][:, 0:CHUNKS - 1], 1.0, K["ident"][:, P - 1:P], ALU.add, ALU.mult))
            link(dve.tensor_scalar(K["carry_key"][:], dshift[:], -1.0, None, ALU.add))
            dve.wait_ge(w_loaded, 16 * 12)
            dve.wait_ge(small_loaded, 16 * N_SMALL)
            dve.tensor_scalar(K["wup"][:], wts[:, 5, :], MUL ** -0.5, None, ALU.mult).then_inc(chunkify, 1)
            base = len(blocks)
            dve.wait_ge(pe_done, base + 1)
            dve.tensor_copy(wT[:, 0:4, :], pw[:]).then_inc(pe_used, 1)
            dve.wait_ge(pe_done, base + 2)
            dve.tensor_copy(K["wa"][:], pw2[:, 1, 0:8])
            dve.tensor_scalar(K["wqk"][:], pw2[:, 2, :], D ** -0.5, None, ALU.mult)
            dve.tensor_copy(K["wvo"][:], pw2[:, 3, :])
            s0 = (2 * MUL) ** -0.5 / AVG
            sv = s0 * 3.0 ** 0.5
            link(dve.memset(K["wout"][:], 0.0))
            vcols = K["wout"][:, :, MUL:].rearrange("p a (k c) -> p a k c", c=3)
            link(dve.tensor_scalar(K["wout"][0:64, 0, 0:MUL], wo0[0:64, 0, :], s0, None, ALU.mult))
            link(dve.tensor_scalar(vcols[64:96, 0, :, 0], wo0[64:96, 0, :], sv, None, ALU.mult))
            link(dve.tensor_scalar(vcols[96:128, 0, :, 1], wo0[96:128, 0, :], sv, None, ALU.mult))
            link(dve.tensor_scalar(vcols[0:32, 1, :, 2], wo0[0:32, 1, :], sv, None, ALU.mult))
            for c in range(3):
                q = 32 * (c + 1)
                link(dve.tensor_scalar(vcols[q:q + 32, 1, :, c], wo0[q:q + 32, 1, :], s0, None, ALU.mult))

        @block.tensor
        def _(pe):
            pe.wait_ge(ident_ready, 1)
            pe.wait_ge(chunkify, 1)
            n = 0
            for src in [cur, scat, srow, rhatR[:, 0], rhatR[:, 1], rhatR[:, 2]]:
                if n:
                    pe.wait_ge(pe_used, n)
                for b in range(4):
                    tr = nc.tensor.transpose(pt[:, b, :], src[:, b, :], K["ident"][:])
                tr.then_inc(pe_done, 1)
                n += 1
            pe.wait_ge(chunkify, 2)
            pe.wait_ge(w_loaded, 16 * 12)
            for i in range(4):
                tr = nc.tensor.transpose(pw[:, i, :], wts[:, i, :], K["ident"][:])
            tr.then_inc(pe_done, 1)
            pe.wait_ge(pe_used, n + 1)
            nc.tensor.matmul(pw2[:, 1, 0:8], wT[:, 0, :], att8[:], start=True, stop=True)
            nc.tensor.matmul(pw2[:, 2, :], wT[:, 1, :], wT[:, 2, :], start=True, stop=True)
            nc.tensor.matmul(pw2[:, 3, :], wT[:, 3, :], wts[:, 4, :], start=True, stop=True).then_inc(pe_done, 1)
    end_stage(nc, owned)




def sort_and_scores(nc, A, T, K):
    with ExitStack() as ctx:
        sb, ps, sem, sems, owned = stage_makers(nc, ctx, "sort")
        x = [sb(f"x{u}", [P, G, D]) for u in range(BUFS)]
        xT = [sb(f"xT{u}", [P, G, P]) for u in range(2)]
        s = [sb(f"s{u}", [P, G, 8]) for u in range(BUFS)]
        tp = ps("tp", [P, G, P])
        sps = [ps(f"sps{v}", [P, G, 64]) for v in range(2)]
        x_loaded, x_turned, x_copied = sems("x_loaded"), sems("x_turned"), sems("x_copied")
        scored, s_ready, s_stored = sems("scored"), sems("s_ready"), sems("s_stored")
        xd = [sb(f"xd{u}", [P, 4, D]) for u in range(BUFS)]
        ring = [sb(f"ring{u}", [P, 4], I32) for u in range(BUFS)]
        ring_ready, gathered, xd_stored = sems("ring_ready"), sems("gathered"), sems("xd_stored")
        rec = [sb(f"rec{i}", [P, 3, SORTF]) for i in range(2)]
        ints = sb("ints", [P, 2, SORTF], I32)
        place = sb("place", [P, SORTF], I32)
        gray = sb("gray", [P, SORTF], I32)
        bit = sb("bit", [P, SORTF], I32)
        sign = sb("sign", [P, SORTF])
        swap = sb("swap", [P, SORTF // 2])
        diff = sb("diff", [P, 2, SORTF // 2])
        flip = ps("flip", [P, 3, SORTF])
        chain_v = sem("chain_v")
        padded = sem("padded")
        loaded = sem("loaded")
        place_ready = sem("place_ready")
        records_ready = sem("records_ready")
        turned = sem("turned")
        sorted_ready = sem("sorted_ready")
        stored = sem("stored")
        full, tail = E // SORTF, E % SORTF
        block = ctx.enter_context(nc.Block())
        turns = []

        @block.gpsimd
        def _(pool):
            pool.iota(place[:], pattern=[[1, SORTF]], base=0, channel_multiplier=SORTF).then_inc(place_ready, 1)

            def gather(t, u):
                wait_item(pool, gathered, t, u, 4, 64)
                wait_item(pool, xd_stored, t, u, 4, 16)
                pool.tensor_copy(ring[u][:], four(K["dst_idx"], t, u)).then_inc(ring_ready[u], 1)
                pool.wait_ge(ring_ready[u], t + 1)
                pool.nop(nofuse=True)
                for j in range(4):
                    pool.indirect_dma_start(xd[u][:, j, :], None, A["x"],
                                            bass.IndirectOffsetOnAxis(ring[u][:, j:j + 1], 0)).then_inc(gathered[u], 16)
            pipeline(pool, (gather, 0))

        @block.vector
        def _(dve):
            link = chain_of(dve, chain_v)
            dve.memset(ints[:], PAD_ID).then_inc(padded, 1)
            dve.wait_ge(place_ready, 1)
            link(dve.tensor_scalar(gray[:], place[:], 1, None, ALU.logical_shift_right))
            dve.wait_ge(loaded, 64)
            dve.tensor_copy(rec[0][:, 0, :], ints[:, 0, :])
            dve.tensor_copy(rec[0][:, 1, :], place[:])
            link(dve.tensor_copy(rec[0][:, 2, :], ints[:, 1, :]))
            now = 0

            def flip_signs(bits, i):
                link(dve.tensor_scalar(bit[:], bits[:], i, 1, ALU.logical_shift_right, ALU.bitwise_and))
                link(dve.tensor_scalar(sign[:], bit[:], -2.0, 1.0, ALU.mult, ALU.add))
                link(dve.tensor_tensor(rec[now][:, 0, :], rec[now][:, 0, :], sign[:], ALU.mult))

            def exchange(now, step):
                a = rec[now][:].rearrange("p r (b two j) -> p r b two j", two=2, j=step)
                o = rec[1 - now][:].rearrange("p r (b two j) -> p r b two j", two=2, j=step)
                s = swap[:].rearrange("p (b j) -> p b j", j=step)
                d = diff[:].rearrange("p r (b j) -> p r b j", j=step)
                both = s.unsqueeze(1).broadcast_to([P, 2, SORTF // 2 // step, step])
                dve.tensor_tensor(s, a[:, 0, :, 0], a[:, 0, :, 1], ALU.is_gt)
                dve.tensor_tensor(o[:, 0, :, 0], a[:, 0, :, 0], a[:, 0, :, 1], ALU.min)
                dve.tensor_tensor(o[:, 0, :, 1], a[:, 0, :, 0], a[:, 0, :, 1], ALU.max)
                link(dve.tensor_tensor(d, a[:, 1:3, :, 1], a[:, 1:3, :, 0], ALU.subtract))
                link(dve.tensor_tensor(d, d, both, ALU.mult))
                dve.tensor_tensor(o[:, 1:3, :, 0], a[:, 1:3, :, 0], d, ALU.add)
                link(dve.tensor_tensor(o[:, 1:3, :, 1], a[:, 1:3, :, 1], d, ALU.subtract))

            def turn_blocks(now):
                turns.append(now)
                dve.sem_inc(records_ready, 1)
                dve.wait_ge(turned, len(turns))
                link(dve.tensor_copy(rec[1 - now][:], flip[:]))

            flip_signs(place, 1)
            link(dve.tensor_tensor(gray[:], gray[:], place[:], ALU.bitwise_xor))
            top = SORTN.bit_length() - 1
            inner = SORTF.bit_length() - 1
            for i in range(1, top + 1):
                if i > inner:
                    turn_blocks(now)
                    now = 1 - now
                    for j in range(i - 1, inner - 1, -1):
                        exchange(now, 1 << (j - inner))
                        now = 1 - now
                    turn_blocks(now)
                    now = 1 - now
                for j in range(min(i, inner) - 1, -1, -1):
                    exchange(now, 1 << j)
                    now = 1 - now
                if i < top:
                    flip_signs(gray, i)
            dve.sem_inc(sorted_ready, 1 + now)

        @block.tensor
        def _(pe):
            def turn(t, u):
                pe.wait_ge(x_loaded[u], 16 * t + 16)
                wait_item(pe, x_copied, t, u, 1)
                for g in range(G):
                    tr = pe.transpose(tp[:, g, :], x[u][:, g, :], K["ident"][:])
                tr.then_inc(x_turned[u], 1)

            def score(t, u):
                pe.wait_ge(x_copied[u], t + 1)
                wait_item(pe, s_ready, t, u, 2)
                for g in range(G):
                    mm = pe.matmul(sps[u % 2][:, g, 0:8], xT[u % 2][:, g, :], K["wa"][:], start=True, stop=True)
                mm.then_inc(scored[u], 1)
            before, more, place_now = 44, 8, 0
            for n, now in enumerate(turns):
                if n % 2 == 0:
                    upto = before + more * (n // 2)
                    pipeline(pe, (turn, 0), (score, 1), first=place_now, last=upto)
                    place_now = upto
                pe.wait_ge(records_ready, n + 1)
                for r in range(3):
                    for b in range(SORTF // P):
                        tr = nc.tensor.transpose(flip[:, r, b * P:(b + 1) * P], rec[now][:, r, b * P:(b + 1) * P], K["ident"][:])
                tr.then_inc(turned, 1)
            pipeline(pe, (turn, 0), (score, 1), first=place_now)

        @block.scalar
        def _(act):
            def copy(t, u):
                act.wait_ge(x_turned[u], t + 1)
                wait_item(act, scored, t, u, 2)
                act.copy(xT[u % 2][:], tp[:]).then_inc(x_copied[u], 1)

            def take(t, u):
                act.wait_ge(scored[u], t + 1)
                wait_item(act, s_stored, t, u, 4, 16)
                act.copy(s[u][:], sps[u % 2][:, :, 0:8]).then_inc(s_ready[u], 1)
            pipeline(act, (copy, 0), (take, 2))

        @block.sync
        def _(sp):
            sp.wait_ge(padded, 1)
            for a, name in enumerate(["src", "dst"]):
                sp.dma_start(ints[0:full, a, :], A[name][0:full * SORTF].rearrange("(p f) -> p f", f=SORTF)).then_inc(loaded, 16)
                sp.dma_start(ints[full:full + 1, a, 0:tail],
                             A[name][full * SORTF:E].rearrange("(p f) -> p f", p=1)).then_inc(loaded, 16)
            def load_x(t, u):
                wait_item(sp, x_turned, t, u, 4)
                sp.dma_start(x[u][:], node_rows(A["x"], t, u)).then_inc(x_loaded[u], 16)

            def store_s(t, u):
                sp.wait_ge(s_ready[u], t + 1)
                if is_item(t, u, ITEMS - 1):
                    wait_item(sp, s_stored, t, u, 1, 16)
                sp.dma_start(node_rows(T["scores"], t, u), s[u][:]).then_inc(s_stored[u], 16)

            def store_xd(t, u):
                sp.wait_ge(gathered[u], 64 * t + 64)
                sp.dma_start(edge_rows(T["xdst"], t, u), xd[u][:]).then_inc(xd_stored[u], 16)
            pipeline(sp, (load_x, 0), (store_xd, 2), (store_s, 6))
            for u in range(BUFS):
                sp.wait_ge(s_stored[u], 16 * PER_BUF[u])
                sp.wait_ge(xd_stored[u], 16 * PER_BUF[u])
            phases = SORTN.bit_length() - 1
            exchanges = phases * (phases + 1) // 2
            now = (exchanges + len(turns)) % 2
            sp.wait_ge(sorted_ready, 1 + now)
            for r in range(3):
                sp.dma_start(T["sorted"][r].rearrange("(p f) -> p f", f=SORTF), rec[now][:, r, :]).then_inc(stored, 16)
            sp.wait_ge(stored, 48)
    end_stage(nc, owned)




def segment_tiles(sb, name, heads):
    seg = {"heads": heads}
    for tile in ("cont", "negcont", "nxt", "pre", "negpre", "suf", "last", "work"):
        seg[tile] = sb(f"{name}_{tile}", [P, CHUNKS])
    for row in ("first", "end", "full", "link", "neglink", "a", "nega", "arev", "linkn", "b", "c"):
        seg["r_" + row] = sb(f"{name}_r_{row}", [heads, P])
    seg["ccol"] = sb(f"{name}_ccol", [P, heads])
    seg["fullcol"] = sb(f"{name}_fullcol", [P, 1])
    return seg


def turner_of(sb, ps, sem):
    return {"scr": sb("turn_scr", [P, P]), "out": ps("turn_out", [P, P]), "ready": sem("turn_ready"),
            "done": sem("turn_done"), "turns": []}


def turn_by_vector(dve, turner, write):
    write(turner["scr"]).then_inc(turner["ready"], 1)
    turner["turns"].append(1)
    dve.wait_ge(turner["done"], len(turner["turns"]))


def turn_by_tensor(pe, turner, ident):
    for n in range(len(turner["turns"])):
        pe.wait_ge(turner["ready"], n + 1)
        pe.transpose(turner["out"][:], turner["scr"][:], ident[:]).then_inc(turner["done"], 1)


def find_segments(dve, link, turner, seg, ids):
    F, H, R = CHUNKS, seg["heads"], P
    link(dve.memset(seg["cont"][:, 0:1], 0.0))
    link(dve.tensor_tensor(seg["cont"][:, 1:F], ids[:, 1:F], ids[:, 0:F - 1], ALU.is_equal))
    link(dve.memset(seg["nxt"][:, F - 1:F], 0.0))
    link(dve.tensor_copy(seg["nxt"][:, 0:F - 1], seg["cont"][:, 1:F]))
    link(dve.tensor_scalar(seg["negcont"][:], seg["cont"][:], -1.0, BIG, ALU.add, ALU.mult))
    link(dve.tensor_scalar(seg["pre"][:], ids, ids[:, 0:1], None, ALU.is_equal))
    link(dve.tensor_scalar(seg["negpre"][:], seg["pre"][:], -1.0, BIG, ALU.add, ALU.mult))
    link(dve.tensor_scalar(seg["suf"][:], ids, ids[:, F - 1:F], None, ALU.is_equal))
    link(dve.tensor_tensor(seg["fullcol"][:], ids[:, 0:1], ids[:, F - 1:F], ALU.is_equal))
    for col, row in [(ids[:, 0:1], seg["r_first"]), (ids[:, F - 1:F], seg["r_end"]), (seg["fullcol"][:], seg["r_full"])]:
        turn_by_vector(dve, turner, lambda scr: dve.tensor_copy(scr[:, 0:H], col.broadcast_to([P, H])))
        link(dve.tensor_copy(row[:], turner["out"][0:H, :]))
    link(dve.memset(seg["r_link"][:], 0.0))
    link(dve.tensor_tensor(seg["r_link"][:, 1:R], seg["r_first"][:, 1:R], seg["r_end"][:, 0:R - 1], ALU.is_equal))
    link(dve.tensor_scalar(seg["r_neglink"][:], seg["r_link"][:], -1.0, BIG, ALU.add, ALU.mult))
    link(dve.memset(seg["r_a"][:], 0.0))
    link(dve.tensor_tensor(seg["r_a"][:, 1:R], seg["r_link"][:, 1:R], seg["r_full"][:, 0:R - 1], ALU.mult))
    link(dve.tensor_scalar(seg["r_nega"][:], seg["r_a"][:], -1.0, BIG, ALU.add, ALU.mult))
    link(dve.memset(seg["r_linkn"][:], 0.0))
    link(dve.tensor_copy(seg["r_linkn"][:, 0:R - 1], seg["r_link"][:, 1:R]))
    link(dve.memset(seg["r_arev"][:], 0.0))
    link(dve.tensor_tensor(seg["r_arev"][:, 0:R - 1], seg["r_linkn"][:, 0:R - 1], seg["r_full"][:, 1:R], ALU.mult))
    turn_by_vector(dve, turner, lambda scr: dve.tensor_copy(scr[0:H, :], seg["r_linkn"][:]))
    link(dve.tensor_copy(seg["last"][:], seg["nxt"][:]))
    link(dve.tensor_copy(seg["last"][:, F - 1:F], turner["out"][:, 0:1]))
    link(dve.tensor_scalar(seg["last"][:], seg["last"][:], -1.0, 1.0, ALU.mult, ALU.add))


def segment_scan(dve, link, turner, seg, kind, outs, ins):
    F, H, R = CHUNKS, len(outs), P
    for out, v in zip(outs, ins):
        if kind == "sum":
            link(dve.tensor_tensor_scan(out, seg["cont"][:], v, 0.0, ALU.mult, ALU.add))
        elif kind == "max":
            link(dve.tensor_tensor_scan(out, seg["negcont"][:], v, -BIG, ALU.add, ALU.max))
        else:
            link(dve.tensor_tensor(seg["work"][:], seg["last"][:], v, ALU.mult))
            link(dve.tensor_tensor_scan(out[:, ::-1], seg["nxt"][:, ::-1], seg["work"][:, ::-1], 0.0, ALU.mult, ALU.add))
    end = 0 if kind == "fill" else F - 1
    for h, out in enumerate(outs):
        link(dve.tensor_copy(turner["scr"][:, h:h + 1], out[:, end:end + 1]))
    turn_by_vector(dve, turner, lambda scr: dve.tensor_copy(scr[:, H - 1:H], outs[H - 1][:, end:end + 1]))
    ends, b, c = turner["out"][0:H, :], seg["r_b"][0:H, :], seg["r_c"][0:H, :]
    if kind == "sum":
        link(dve.memset(b[:, 0:1], 0.0))
        link(dve.tensor_tensor(b[:, 1:R], seg["r_link"][0:H, 1:R], ends[:, 0:R - 1], ALU.mult))
        link(dve.tensor_tensor_scan(c, seg["r_a"][0:H, :], b, 0.0, ALU.mult, ALU.add))
    elif kind == "max":
        link(dve.memset(b[:, 0:1], -BIG))
        link(dve.tensor_tensor(b[:, 1:R], seg["r_neglink"][0:H, 1:R], ends[:, 0:R - 1], ALU.add))
        link(dve.tensor_tensor_scan(c, seg["r_nega"][0:H, :], b, -BIG, ALU.add, ALU.max))
    else:
        link(dve.memset(b[:, R - 1:R], 0.0))
        link(dve.tensor_tensor(b[:, 0:R - 1], seg["r_linkn"][0:H, 0:R - 1], ends[:, 1:R], ALU.mult))
        link(dve.tensor_tensor_scan(c[:, ::-1], seg["r_arev"][0:H, ::-1], b[:, ::-1], 0.0, ALU.mult, ALU.add))
    turn_by_vector(dve, turner, lambda scr: dve.tensor_copy(scr[0:H, :], c))
    link(dve.tensor_copy(seg["ccol"][:, 0:H], turner["out"][:, 0:H]))
    for h, out in enumerate(outs):
        carried = seg["ccol"][:, h:h + 1]
        if kind == "sum":
            link(dve.scalar_tensor_tensor(out=out, in0=seg["pre"][:], scalar=carried, in1=out, op0=ALU.mult, op1=ALU.add))
        elif kind == "max":
            link(dve.scalar_tensor_tensor(out=out, in0=seg["negpre"][:], scalar=carried, in1=out, op0=ALU.add, op1=ALU.max))
        else:
            link(dve.scalar_tensor_tensor(out=out, in0=seg["suf"][:], scalar=carried, in1=out, op0=ALU.mult, op1=ALU.add))




def gat_softmax(nc, A, T, K):
    with ExitStack() as ctx:
        sb, ps, sem, sems, owned = stage_makers(nc, ctx, "gsm")
        rec = sb("rec", [P, 3, CHUNKS])
        src_idx = sb("src_idx", [P, CHUNKS], I32)
        dst_idx = sb("dst_idx", [P, CHUNKS], I32)
        edge_idx = sb("edge_idx", [P, CHUNKS], I32)
        ring = [sb(f"ring{u}", [P, 2, 4], I32) for u in range(BUFS)]
        out_ring = [sb(f"out_ring{u}", [P, 4], I32) for u in range(BUFS)]
        row_s = [sb(f"row_s{u}", [P, 4, 8]) for u in range(BUFS)]
        row_d = [sb(f"row_d{u}", [P, 4, 8]) for u in range(BUFS)]
        row_o = [sb(f"row_o{u}", [P, 4, HEADS]) for u in range(BUFS)]
        al = sb("al", [P, HEADS, CHUNKS])
        mx = sb("mx", [P, HEADS, CHUNKS])
        tot = sb("tot", [P, HEADS + 1, CHUNKS])
        run = sb("run", [P, HEADS + 1, CHUNKS])
        seg = segment_tiles(sb, "src", HEADS + 1)
        turner = turner_of(sb, ps, sem)
        h1 = [sb(f"h1{v}", [P, 4, P]) for v in range(2)]
        h2 = [sb(f"h2{v}", [P, 4, P]) for v in range(2)]
        w = [sb(f"w{u}", [P, 4, D]) for u in range(BUFS)]
        x = [sb(f"x{u}", [P, G, D]) for u in range(BUFS)]
        y = [sb(f"y{v}", [P, G, D]) for v in range(2)]
        o = [sb(f"o{v}", [P, G, ROW1]) for v in range(2)]
        x_loaded, x_used, o_zeroed, o_stored = sems("x_loaded"), sems("x_used"), sem("o_zeroed"), sems("o_stored")
        norm = norm_of(sb, sems, K["eps"], y * 2, [tile[:, :, 0:D] for tile in o] * 2, width=G, bufs=2)
        hp1, hp2, wp = ps("hp1", [P, 4, P]), ps("hp2", [P, 4, P]), ps("wp", [P, 4, D])
        loaded, ring_ready, gathered = sem("loaded"), sems("ring_ready"), sems("gathered")
        rows_used, chain_v = sems("rows_used"), sem("chain_v")
        shifted, ex_ready = sem("shifted"), sem("ex_ready")
        out_ready, scattered = sems("out_ready"), sems("scattered")
        h1_ready, h1_done, h2_ready, h2_done = sems("h1_ready"), sems("h1_done"), sems("h2_ready"), sems("h2_done")
        wp_ready, w_ready, w_stored = sems("wp_ready"), sems("w_ready"), sems("w_stored")
        block = ctx.enter_context(nc.Block())

        @block.sync
        def _(sp):
            for r in range(3):
                sp.dma_start(rec[:, r, :], T["sorted"][r, 0:EP].rearrange("(p f) -> p f", f=CHUNKS)).then_inc(loaded, 16)

            def store_w(t, u):
                sp.wait_ge(w_ready[u], t + 1)
                sp.dma_start(edge_rows(T["radial"], t, u), w[u][:]).then_inc(w_stored[u], 16)

            def load_x(t, u):
                wait_item(sp, x_used, t, u, 4)
                sp.dma_start(x[u][:], node_rows(A["x"], t, u)).then_inc(x_loaded[u], 16)

            def store_o(t, u):
                sp.wait_ge(norm["normed"][u], t + 1)
                if is_item(t, u, ITEMS - 1):
                    wait_item(sp, o_stored, t, u, 1, 16)
                sp.dma_start(node_rows(T["x1"], t, u), o[u % 2][:]).then_inc(o_stored[u], 16)
            pipeline(sp, (load_x, 0), (store_w, 2), (store_o, 3))
            for u in range(BUFS):
                sp.wait_ge(w_stored[u], 16 * PER_BUF[u])
                sp.wait_ge(o_stored[u], 16 * PER_BUF[u])

        @block.vector
        def _(dve):
            link = chain_of(dve, chain_v)
            link(dve.memset(turner["scr"][:], 0.0))
            dve.wait_ge(loaded, 48)
            dve.tensor_scalar(src_idx[:], rec[:, 0, :], float(N - 1), None, ALU.min)
            dve.tensor_copy(edge_idx[:], rec[:, 1, :])
            link(dve.tensor_scalar(dst_idx[:], rec[:, 2, :], float(N - 1), None, ALU.min))

            def fill_ring(t, u):
                wait_item(dve, gathered, t, u, 4, 128)
                dve.tensor_copy(ring[u][:, 0, :], four(src_idx, t, u))
                dve.tensor_copy(ring[u][:, 1, :], four(dst_idx, t, u)).then_inc(ring_ready[u], 1)

            def take_rows(t, u):
                dve.wait_ge(gathered[u], 128 * t + 128)
                dve.tensor_tensor(four_each(al, t, u), row_s[u][:, :, 0:HEADS].rearrange("p j h -> p h j"),
                                  row_d[u][:, :, HEADS:8].rearrange("p j h -> p h j"), ALU.add).then_inc(rows_used[u], 1)

            def add_bias(t, u):
                dve.wait_ge(wp_ready[u], t + 1)
                wait_item(dve, w_stored, t, u, 4, 16)
                dve.tensor_tensor(w[u][:], wp[:], K["mb2"][:].unsqueeze(1).broadcast_to([P, 4, D]), ALU.add).then_inc(w_ready[u], 1)

            def shift_x(t, u):
                dve.wait_ge(x_loaded[u], 16 * t + 16)
                wait_item(dve, norm["normed"], t, u, 2)
                dve.tensor_tensor(y[u % 2][:], x[u][:], over_rows(K["bias0"]), ALU.add).then_inc(x_used[u], 1)
                dve.wait_ge(x_used[u], t + 1)
                norm_measure(norm, dve, t, u)
            for v in range(2):
                dve.memset(o[v][:, :, D:ROW1], 0.0).then_inc(o_zeroed, 1)
            pipeline(dve, (fill_ring, 0), (shift_x, 1), (lambda t, u: norm_scale(norm, dve, t, u), 2), (add_bias, 2), (take_rows, 4))
            for u in range(BUFS):
                dve.wait_ge(rows_used[u], PER_BUF[u])
            link(dve.scalar_tensor_tensor(out=al[:], in0=al[:], scalar=0.2, in1=al[:], op0=ALU.mult, op1=ALU.max))
            find_segments(dve, link, turner, seg, rec[:, 0, :])
            heads = range(HEADS)
            segment_scan(dve, link, turner, seg, "max", [run[:, h, :] for h in heads], [al[:, h, :] for h in heads])
            segment_scan(dve, link, turner, seg, "fill", [mx[:, h, :] for h in heads], [run[:, h, :] for h in heads])
            link(dve.tensor_scalar(mx[:], mx[:], 0.0, None, ALU.max))
            dve.tensor_tensor(al[:], al[:], mx[:], ALU.subtract).then_inc(shifted, 1)
            dve.wait_ge(ex_ready, 2)
            link(dve.memset(tot[:, HEADS, :], 1.0))
            each = range(HEADS + 1)
            segment_scan(dve, link, turner, seg, "sum", [run[:, h, :] for h in each],
                         [al[:, h, :] for h in heads] + [tot[:, HEADS, :]])
            segment_scan(dve, link, turner, seg, "fill", [tot[:, h, :] for h in each], [run[:, h, :] for h in each])
            link(dve.tensor_scalar(seg["work"][:], tot[:, HEADS, :], -1.0, float(E), ALU.mult, ALU.add))
            for h in heads:
                link(dve.tensor_tensor(mx[:, h, :], mx[:, h, :], seg["work"][:], ALU.mult))
            link(dve.tensor_tensor(tot[:, 0:HEADS, :], tot[:, 0:HEADS, :], mx[:], ALU.add))
            link(dve.reciprocal(mx[:], tot[:, 0:HEADS, :]))
            link(dve.tensor_tensor(al[:], al[:], mx[:], ALU.mult))

            def give_rows(t, u):
                wait_item(dve, scattered, t, u, 4, 64)
                dve.tensor_copy(row_o[u][:], four_each(al, t, u).rearrange("p h j -> p j h"))
                dve.tensor_copy(out_ring[u][:], four(edge_idx, t, u)).then_inc(out_ready[u], 1)
            pipeline(dve, (give_rows, 0))

        @block.scalar
        def _(act):
            def first(t, u):
                act.wait_ge(h1_ready[u], t + 1)
                wait_item(act, h2_ready, t, u, 2)
                act.activation(h1[u % 2][:], hp1[:], ACT.Silu, bias=K["mb0"][:, 0:1]).then_inc(h1_done[u], 1)

            def second(t, u):
                act.wait_ge(h2_ready[u], t + 1)
                wait_item(act, wp_ready, t, u, 2)
                act.activation(h2[u % 2][:], hp2[:], ACT.Silu, bias=K["mb1"][:, 0:1]).then_inc(h2_done[u], 1)
            act.wait_ge(o_zeroed, 2)
            pipeline(act, (first, 0), (second, 1), (lambda t, u: norm_root(norm, act, t, u), 1),
                     (lambda t, u: norm_apply(norm, act, t, u, o_stored), 2))
            act.wait_ge(shifted, 1)
            nc.scalar.activation(al[:], al[:], ACT.Exp).then_inc(ex_ready, 1)
            nc.scalar.activation(mx[:], mx[:], ACT.Exp, scale=-1.0).then_inc(ex_ready, 1)

        @block.tensor
        def _(pe):
            def first(t, u):
                wait_item(pe, h1_done, t, u, 1)
                for j in range(4):
                    mm = pe.matmul(hp1[:, j, :], K["m0g"][:, (4 * u + j) % 8, :], radial_block(K, t, u), start=True, stop=True)
                mm.then_inc(h1_ready[u], 1)

            def second(t, u):
                pe.wait_ge(h1_done[u], t + 1)
                wait_item(pe, h2_done, t, u, 1)
                pe.matmul(hp2[:].rearrange("p j i -> p (j i)"), K["m1"][:], h1[u % 2][:].rearrange("p j i -> p (j i)"),
                          start=True, stop=True).then_inc(h2_ready[u], 1)

            def third(t, u):
                pe.wait_ge(h2_done[u], t + 1)
                wait_item(pe, w_ready, t, u, 1)
                for j in range(4):
                    mm = pe.matmul(wp[:, j, :], h2[u % 2][:, j, :], K["m2"][:], start=True, stop=True)
                mm.then_inc(wp_ready[u], 1)
            pipeline(pe, (first, 0), (second, 1), (third, 2))
            turn_by_tensor(pe, turner, K["ident"])

        @block.gpsimd
        def _(pool):
            def gather(t, u):
                pool.wait_ge(ring_ready[u], t + 1)
                wait_item(pool, rows_used, t, u, 4)
                pool.nop(nofuse=True)
                for j in range(4):
                    pool.indirect_dma_start(row_s[u][:, j, :], None, T["scores"],
                                            bass.IndirectOffsetOnAxis(ring[u][:, 0, j:j + 1], 0)).then_inc(gathered[u], 16)
                    pool.indirect_dma_start(row_d[u][:, j, :], None, T["scores"],
                                            bass.IndirectOffsetOnAxis(ring[u][:, 1, j:j + 1], 0)).then_inc(gathered[u], 16)

            def scatter(t, u):
                pool.wait_ge(out_ready[u], t + 1)
                pool.nop(nofuse=True)
                for j in range(4):
                    pool.indirect_dma_start(T["alpha"], bass.IndirectOffsetOnAxis(out_ring[u][:, j:j + 1], 0),
                                            row_o[u][:, j, :], None).then_inc(scattered[u], 16)
            pipeline(pool, (gather, 0))
            pipeline(pool, (scatter, 0))
            for u in range(BUFS):
                pool.wait_ge(scattered[u], 64 * PER_BUF[u])
    end_stage(nc, owned)


def gat_sums(nc, A, T, K):
    with ExitStack() as ctx:
        sb, ps, sem, sems, owned = stage_makers(nc, ctx, "gsu")
        ids = K["ids"]
        raw = sb("raw", [P, CHUNKS, HEADS])
        v = sb("v", [P, HEADS + 1, CHUNKS])
        run = sb("run", [P, HEADS + 1, CHUNKS])
        quarter = CHUNKS // 4
        rows = sb("rows", [P, HEADS + 1, 4 * P])
        turned = [ps(f"turned{i}", [P, 4, P]) for i in range(2)]
        turner = turner_of(sb, ps, sem)
        loaded, chain_v, raw_zero = sem("loaded"), sem("chain_v"), sem("raw_zero")
        totals_ready, totals_stored, rows_loaded = sem("totals_ready"), sem("totals_stored"), sem("rows_loaded")
        rows_turned, rows_taken, roots_ready = sem("rows_turned"), sem("rows_taken"), sem("roots_ready")
        block = ctx.enter_context(nc.Block())
        each = range(HEADS + 1)

        @block.sync
        def _(sp):
            sp.dma_start(ids[:], T["ids"][1, 0:EP].rearrange("(p f) -> p f", f=CHUNKS)).then_inc(loaded, 16)
            full, tail = E // CHUNKS, E % CHUNKS
            sp.wait_ge(raw_zero, 1)
            sp.dma_start(raw[0:full].rearrange("p f h -> p (f h)"),
                         T["alpha"][0:full * CHUNKS, :].rearrange("(p f) h -> p (f h)", f=CHUNKS)).then_inc(loaded, 16)
            sp.dma_start(raw[full:full + 1, 0:tail].rearrange("p f h -> p (f h)"),
                         T["alpha"][full * CHUNKS:E, :].rearrange("(p f) h -> p (f h)", p=1)).then_inc(loaded, 16)
            sp.wait_ge(totals_ready, 1)
            for h in each:
                sp.dma_start(T["totals"][h].rearrange("(p f) -> p f", f=CHUNKS), v[:, h, :]).then_inc(totals_stored, 16)
            sp.wait_ge(totals_stored, 16 * (HEADS + 1))
            for h in each:
                sp.dma_start(rows[0:quarter, h, :], T["totals"][h].rearrange("(r f) -> r f", f=4 * P)).then_inc(rows_loaded, 16)

        @block.vector
        def _(dve):
            link = chain_of(dve, chain_v)
            dve.memset(raw[:], 0.0).then_inc(raw_zero, 1)
            link(dve.memset(turner["scr"][:], 0.0))
            link(dve.memset(rows[:], 0.0))
            link(dve.memset(v[:, HEADS, :], 1.0))
            dve.wait_ge(loaded, 48)
            link(dve.tensor_copy(v[:, 0:HEADS, :], raw[:].rearrange("p f h -> p h f")))
            find_segments(dve, link, turner, K["seg"], ids[:])
            segment_scan(dve, link, turner, K["seg"], "sum", [run[:, h, :] for h in each], [v[:, h, :] for h in each])
            segment_scan(dve, link, turner, K["seg"], "fill", [v[:, h, :] for h in each], [run[:, h, :] for h in each])
            dve.sem_inc(totals_ready, 1)
            for h in each:
                dve.wait_ge(rows_turned, h + 1)
                dve.tensor_copy(K["totB"][:, h, :].rearrange("p (r b) -> p b r", b=4), turned[h % 2][:, :, 0:quarter]).then_inc(rows_taken, 1)
            dve.wait_ge(roots_ready, 1)
            dve.reciprocal(K["dinvB"][:], K["dsqrtB"][:])

        @block.scalar
        def _(act):
            act.wait_ge(rows_taken, HEADS + 1)
            act.activation(K["dsqrtB"][:], K["totB"][:, HEADS, :], ACT.Sqrt, bias=K["one"][:, 0:1]).then_inc(roots_ready, 1)

        @block.tensor
        def _(pe):
            turn_by_tensor(pe, turner, K["ident"])
            pe.wait_ge(rows_loaded, 16 * (HEADS + 1))
            for h in each:
                if h >= 2:
                    pe.wait_ge(rows_taken, h - 1)
                for b in range(4):
                    tr = pe.transpose(turned[h % 2][:, b, :], rows[:, h, b * P:(b + 1) * P], K["ident"][:])
                tr.then_inc(rows_turned, 1)
    end_stage(nc, owned)




def over_rows(vector):
    return vector[:].unsqueeze(1).broadcast_to([P, G, D])


def over_columns(scalars):
    return scalars.unsqueeze(2).broadcast_to([P, G, D])


def norm_of(sb, sems, eps, y, o, width=G, root_degree=None, bufs=BUFS):
    norm = {"y": y, "o": o, "eps": eps, "root_degree": root_degree, "width": width, "bufs": bufs}
    for name, shape in [("stats", [P, width, 6]), ("diff", [P, width]), ("mv", [P, width, 2]), ("sd", [P, width]),
                        ("rs", [P, width]), ("nb", [P, width])]:
        norm[name] = [sb(f"{name}{u}", shape) for u in range(BUFS)]
    for name in ("stats_ready", "root_ready", "scale_ready", "normed", "chain", "weighted"):
        norm[name] = sems(f"norm_{name}")
    return norm


def norm_measure(norm, dve, t, u):
    for g in range(norm["width"]):
        bn = dve.bn_stats(norm["stats"][u][:, g, :], norm["y"][u][:, g, :])
    bn.then_inc(norm["chain"][u], 1)
    dve.wait_ge(norm["chain"][u], 4 * t + 1)
    even, odd = norm["stats"][u][:, :, 0:3], norm["stats"][u][:, :, 3:6]
    dve.tensor_tensor(norm["diff"][u][:], even[:, :, 1], odd[:, :, 1], ALU.subtract)
    dve.tensor_tensor(norm["mv"][u][:, :, 0], even[:, :, 1], odd[:, :, 1], ALU.add)
    dve.tensor_tensor(norm["mv"][u][:, :, 1], even[:, :, 2], odd[:, :, 2], ALU.add).then_inc(norm["chain"][u], 1)
    dve.wait_ge(norm["chain"][u], 4 * t + 2)
    dve.scalar_tensor_tensor(out=norm["diff"][u][:], in0=norm["diff"][u][:], scalar=D / 4.0, in1=norm["diff"][u][:],
                             op0=ALU.mult, op1=ALU.mult).then_inc(norm["chain"][u], 1)
    dve.wait_ge(norm["chain"][u], 4 * t + 3)
    dve.tensor_tensor(norm["mv"][u][:, :, 1], norm["mv"][u][:, :, 1], norm["diff"][u][:], ALU.add).then_inc(norm["stats_ready"][u], 1)


def norm_root(norm, act, t, u):
    act.wait_ge(norm["stats_ready"][u], t + 1)
    act.activation(norm["sd"][u][:], norm["mv"][u][:, :, 1], ACT.Sqrt, bias=norm["eps"][:, 0:1], scale=1.0 / D).then_inc(norm["root_ready"][u], 1)


def norm_scale(norm, dve, t, u):
    dve.wait_ge(norm["root_ready"][u], t + 1)
    wait_item(dve, norm["normed"], t, u, 4)
    if norm["root_degree"] is not None:
        dve.tensor_tensor(norm["sd"][u][:], norm["sd"][u][:], norm["root_degree"](t, u), ALU.mult).then_inc(norm["weighted"][u], 1)
        dve.wait_ge(norm["weighted"][u], t + 1)
    dve.reciprocal(norm["rs"][u][:], norm["sd"][u][:]).then_inc(norm["chain"][u], 1)
    dve.wait_ge(norm["chain"][u], 4 * t + 4)
    dve.scalar_tensor_tensor(out=norm["nb"][u][:], in0=norm["mv"][u][:, :, 0], scalar=-0.5, in1=norm["rs"][u][:],
                             op0=ALU.mult, op1=ALU.mult).then_inc(norm["scale_ready"][u], 1)


def norm_apply(norm, act, t, u, stored, by=16):
    act.wait_ge(norm["scale_ready"][u], t + 1)
    wait_item(act, stored, t, u, norm["bufs"], by)
    for g in range(norm["width"]):
        ac = act.activation(norm["o"][u][:, g, :], norm["y"][u][:, g, :], ACT.Identity,
                            bias=norm["nb"][u][:, g:g + 1], scale=norm["rs"][u][:, g:g + 1])
    ac.then_inc(norm["normed"][u], 1)


def first_layer(nc, A, T, K):
    with ExitStack() as ctx:
        sb, ps, sem, sems, owned = stage_makers(nc, ctx, "l0")
        x = [sb(f"x{u}", [P, 4, D]) for u in range(BUFS)]
        xT = [sb(f"xT{v}", [P, 4, P]) for v in range(2)]
        y = [sb(f"y{u}", [P, 4, D]) for u in range(BUFS)]
        o = [sb(f"o{u}", [P, 4, ROW1]) for u in range(BUFS)]
        ring = [sb(f"ring{u}", [P, 4], I32) for u in range(BUFS)]
        tp = [ps(f"tp{v}", [P, 4, P]) for v in range(2)]
        hp = [ps(f"hp{v}", [P, 4, D]) for v in range(2)]
        loaded, turned, copied, multiplied = sems("loaded"), sems("turned"), sems("copied"), sems("multiplied")
        scaled, used, stored, scattered = sems("scaled"), sems("used"), sems("stored"), sems("scattered")
        ring_ready, o_zeroed = sems("ring_ready"), sem("o_zeroed")
        norm = norm_of(sb, sems, K["eps"], y, [tile[:, :, 0:D] for tile in o], width=4)
        block = ctx.enter_context(nc.Block())

        @block.sync
        def _(sp):
            def load(t, u):
                wait_item(sp, used, t, u, 4)
                wait_item(sp, turned, t, u, 4)
                sp.dma_start(x[u][:], edge_rows(T["xdst"], t, u)).then_inc(loaded[u], 16)

            def store(t, u):
                sp.wait_ge(norm["normed"][u], t + 1)
                sp.dma_start(edge_rows(T["x1dst"], t, u), o[u][:, :, 0:D]).then_inc(stored[u], 16)
            pipeline(sp, (load, 0), (store, 5))
            for u in range(BUFS):
                sp.wait_ge(stored[u], 16 * PER_BUF[u])

        @block.tensor
        def _(pe):
            def turn(t, u):
                pe.wait_ge(loaded[u], 16 * t + 16)
                wait_item(pe, copied, t, u, 2)
                for j in range(4):
                    tr = pe.transpose(tp[u % 2][:, j, :], x[u][:, j, :], K["ident"][:])
                tr.then_inc(turned[u], 1)

            def multiply(t, u):
                pe.wait_ge(copied[u], t + 1)
                wait_item(pe, used, t, u, 2)
                for j in range(4):
                    mm = pe.matmul(hp[u % 2][:, j, :], xT[u % 2][:, j, :], K["wh"][:], start=True, stop=True)
                mm.then_inc(multiplied[u], 1)
            pipeline(pe, (turn, 0), (multiply, 1))

        @block.scalar
        def _(act):
            def copy(t, u):
                act.wait_ge(turned[u], t + 1)
                wait_item(act, multiplied, t, u, 2)
                act.copy(xT[u % 2][:], tp[u % 2][:]).then_inc(copied[u], 1)

            def apply(t, u):
                wait_item(act, scattered, t, u, 4, 64)
                norm_apply(norm, act, t, u, stored)
            act.wait_ge(o_zeroed, BUFS)
            pipeline(act, (copy, 0), (lambda t, u: norm_root(norm, act, t, u), 2), (apply, 3))

        @block.vector
        def _(dve):
            def multiply(t, u):
                dve.wait_ge(multiplied[u], t + 1)
                wait_item(dve, norm["normed"], t, u, 4)
                dve.tensor_tensor(y[u][:].rearrange("p j (a c) -> p j a c", a=HEADS),
                                  hp[u % 2][:].rearrange("p j (a c) -> p j a c", a=HEADS),
                                  four_each(K["totB"], t, u)[:, 0:HEADS].rearrange("p a j -> p j a").unsqueeze(3).broadcast_to([P, 4, HEADS, HC]),
                                  ALU.mult)
                dve.tensor_tensor(x[u][:], x[u][:], K["bias0"][:].unsqueeze(1).broadcast_to([P, 4, D]), ALU.add).then_inc(scaled[u], 1)

            def add(t, u):
                dve.wait_ge(scaled[u], t + 1)
                dve.tensor_tensor(y[u][:], y[u][:], x[u][:], ALU.add).then_inc(used[u], 1)
                wait_item(dve, scattered, t, u, 4, 64)
                dve.tensor_copy(o[u][:, :, D:D + 1], four_each(K["totB"], t, u)[:, HEADS:HEADS + 1].rearrange("p a j -> p j a"))
                dve.tensor_copy(ring[u][:], four(K["scat_idx"], t, u)).then_inc(ring_ready[u], 1)
                dve.wait_ge(used[u], t + 1)
                norm_measure(norm, dve, t, u)
            for u in range(BUFS):
                dve.memset(o[u][:, :, D:ROW1], 0.0).then_inc(o_zeroed, 1)
            dve.wait_ge(o_zeroed, BUFS)
            pipeline(dve, (multiply, 0), (lambda t, u: norm_scale(norm, dve, t, u), 1), (add, 0))

        @block.gpsimd
        def _(pool):
            def scatter(t, u):
                pool.wait_ge(ring_ready[u], t + 1)
                pool.wait_ge(norm["normed"][u], t + 1)
                pool.nop(nofuse=True)
                for j in range(4):
                    pool.indirect_dma_start(T["x1"], bass.IndirectOffsetOnAxis(ring[u][:, j:j + 1], 0), o[u][:, j, :], None,
                                            bounds_check=N - 1, oob_is_err=False).then_inc(scattered[u], 16)
            pipeline(pool, (scatter, 0))
            for u in range(BUFS):
                pool.wait_ge(scattered[u], 64 * PER_BUF[u])
    end_stage(nc, owned)


def final_nodes(nc, A, T, K):
    with ExitStack() as ctx:
        sb, ps, sem, sems, owned = stage_makers(nc, ctx, "n3")
        x = [sb(f"x{u}", [P, G, D]) for u in range(BUFS)]
        o = [sb(f"o{u}", [P, G, D]) for u in range(BUFS)]
        xs = [sb(f"xs{u}", [P, 4, D]) for u in range(BUFS)]
        ring = [sb(f"ring{u}", [P, 4], I32) for u in range(BUFS)]
        loaded, stored = sems("loaded"), sems("stored")
        ring_ready, gathered, xs_stored = sems("ring_ready"), sems("gathered"), sems("xs_stored")
        norm = norm_of(sb, sems, K["eps"], x, o)
        block = ctx.enter_context(nc.Block())

        @block.sync
        def _(sp):
            def load(t, u):
                wait_item(sp, norm["normed"], t, u, 4)
                sp.dma_start(x[u][:], node_rows(T["x3"], t, u)).then_inc(loaded[u], 16)

            def store_xs(t, u):
                sp.wait_ge(gathered[u], 64 * t + 64)
                sp.dma_start(edge_rows(T["xsrc"], t, u), xs[u][:]).then_inc(xs_stored[u], 16)

            def store(t, u):
                sp.wait_ge(norm["normed"][u], t + 1)
                if is_item(t, u, ITEMS - 1):
                    wait_item(sp, stored, t, u, 1, 16)
                sp.dma_start(node_rows(T["out"], t, u), o[u][:]).then_inc(stored[u], 16)
            pipeline(sp, (load, 0), (store_xs, 3), (store, 3))
            for u in range(BUFS):
                sp.wait_ge(xs_stored[u], 16 * PER_BUF[u])
                sp.wait_ge(stored[u], 16 * PER_BUF[u])

        @block.vector
        def _(dve):
            def fill_ring(t, u):
                wait_item(dve, gathered, t, u, 4, 64)
                dve.tensor_copy(ring[u][:], four(K["src_idx"], t, u)).then_inc(ring_ready[u], 1)

            def measure(t, u):
                dve.wait_ge(loaded[u], 16 * t + 16)
                norm_measure(norm, dve, t, u)
            pipeline(dve, (fill_ring, 0), (measure, 1), (lambda t, u: norm_scale(norm, dve, t, u), 2))

        @block.scalar
        def _(act):
            pipeline(act, (lambda t, u: norm_root(norm, act, t, u), 0), (lambda t, u: norm_apply(norm, act, t, u, stored), 1))

        @block.gpsimd
        def _(pool):
            def gather(t, u):
                pool.wait_ge(ring_ready[u], t + 1)
                wait_item(pool, xs_stored, t, u, 4, 16)
                pool.nop(nofuse=True)
                for j in range(4):
                    pool.indirect_dma_start(xs[u][:, j, :], None, T["x3"],
                                            bass.IndirectOffsetOnAxis(ring[u][:, j:j + 1], 0)).then_inc(gathered[u], 16)
            pipeline(pool, (gather, 0))
    end_stage(nc, owned)


def gcn_nodes(nc, T, K, name, z_table, weight, bias, out_table, x_table=None):
    normed = x_table is not None
    with ExitStack() as ctx:
        sb, ps, sem, sems, owned = stage_makers(nc, ctx, name)
        z = [sb(f"z{u}", [P, G, D]) for u in range(BUFS)]
        uT = [sb(f"uT{v}", [P, G, P]) for v in range(2)]
        y = [sb(f"y{u}", [P, G, D]) for u in range(BUFS)]
        o = [sb(f"o{u}", [P, G, D]) for u in range(BUFS)]
        x = [sb(f"x{u}", [P, G, D]) for u in range(BUFS)] if normed else None
        xs = [sb(f"xs{u}", [P, 4, D]) for u in range(BUFS)]
        ring = [sb(f"ring{u}", [P, 4], I32) for u in range(BUFS)]
        tp = [ps(f"tp{v}", [P, G, P]) for v in range(2)]
        hp = [ps(f"hp{v}", [P, G, D]) for v in range(2)]
        loaded, turned, copied = sems("loaded"), sems("turned"), sems("copied")
        multiplied, taken, ready, stored = sems("multiplied"), sems("taken"), sems("ready"), sems("stored")
        x_loaded, x_scaled, x_used = sems("x_loaded"), sems("x_scaled"), sems("x_used")
        ring_ready, gathered, xs_stored = sems("ring_ready"), sems("gathered"), sems("xs_stored")
        norm = norm_of(sb, sems, K["eps"], y, o) if normed else None
        done = norm["normed"] if normed else ready
        block = ctx.enter_context(nc.Block())

        @block.sync
        def _(sp):
            def load(t, u):
                wait_item(sp, turned, t, u, 4)
                sp.dma_start(z[u][:], node_rows(z_table, t, u)).then_inc(loaded[u], 16)
                if normed:
                    wait_item(sp, x_used, t, u, 4)
                    sp.dma_start(x[u][:], node_rows(x_table, t, u)).then_inc(x_loaded[u], 16)

            def store_xs(t, u):
                sp.wait_ge(gathered[u], 64 * t + 64)
                sp.dma_start(edge_rows(T["xsrc"], t, u), xs[u][:]).then_inc(xs_stored[u], 16)

            def store(t, u):
                sp.wait_ge(done[u], t + 1)
                if is_item(t, u, ITEMS - 1):
                    wait_item(sp, stored, t, u, 1, 16)
                sp.dma_start(node_rows(out_table, t, u), o[u][:]).then_inc(stored[u], 16)
            pipeline(sp, (load, 0), (store_xs, 3), (store, 5))
            for u in range(BUFS):
                sp.wait_ge(xs_stored[u], 16 * PER_BUF[u])
                sp.wait_ge(stored[u], 16 * PER_BUF[u])

        @block.tensor
        def _(pe):
            def turn(t, u):
                pe.wait_ge(loaded[u], 16 * t + 16)
                wait_item(pe, copied, t, u, 2)
                for g in range(G):
                    tr = pe.transpose(tp[u % 2][:, g, :], z[u][:, g, :], K["ident"][:])
                tr.then_inc(turned[u], 1)

            def multiply(t, u):
                pe.wait_ge(copied[u], t + 1)
                wait_item(pe, taken, t, u, 2)
                for g in range(G):
                    mm = pe.matmul(hp[u % 2][:, g, :], uT[u % 2][:, g, :], weight[:], start=True, stop=True)
                mm.then_inc(multiplied[u], 1)
            pipeline(pe, (turn, 0), (multiply, 1))

        @block.scalar
        def _(act):
            def copy(t, u):
                act.wait_ge(turned[u], t + 1)
                wait_item(act, multiplied, t, u, 2)
                act.copy(uT[u % 2][:], tp[u % 2][:]).then_inc(copied[u], 1)

            def activate(t, u):
                act.wait_ge(taken[u], t + 1)
                wait_item(act, stored, t, u, 4, 16)
                for g in range(G):
                    ac = act.activation(o[u][:, g, :], y[u][:, g, :], ACT.Relu,
                                        scale=K["dinv"][:, bass.ds(BUFS * t + u, 1), g])
                ac.then_inc(ready[u], 1)
            if normed:
                pipeline(act, (copy, 0), (lambda t, u: norm_root(norm, act, t, u), 2),
                         (lambda t, u: norm_apply(norm, act, t, u, stored), 3))
            else:
                pipeline(act, (copy, 0), (activate, 2))

        @block.vector
        def _(dve):
            def fill_ring(t, u):
                wait_item(dve, gathered, t, u, 4, 64)
                dve.tensor_copy(ring[u][:], four(K["src_idx"], t, u)).then_inc(ring_ready[u], 1)

            def take(t, u):
                dve.wait_ge(multiplied[u], t + 1)
                wait_item(dve, done, t, u, 4)
                for g in range(G):
                    st = dve.scalar_tensor_tensor(out=y[u][:, g, :], in0=hp[u % 2][:, g, :],
                                                  scalar=K["dinv"][:, bass.ds(BUFS * t + u, 1), g], in1=bias[:],
                                                  op0=ALU.mult, op1=ALU.add)
                st.then_inc(taken[u], 1)

            def add(t, u):
                dve.wait_ge(taken[u], t + 1)
                dve.wait_ge(x_scaled[u], t + 1)
                dve.scalar_tensor_tensor(out=y[u][:], in0=y[u][:], scalar=0.0, in1=x[u][:],
                                         op0=ALU.max, op1=ALU.add).then_inc(x_used[u], 1)
                dve.wait_ge(x_used[u], t + 1)
                norm_measure(norm, dve, t, u)
            if normed:
                pipeline(dve, (fill_ring, 0), (take, 2), (lambda t, u: norm_scale(norm, dve, t, u), 3), (add, 2))
            else:
                pipeline(dve, (fill_ring, 0), (take, 2))

        @block.gpsimd
        def _(pool):
            def gather(t, u):
                pool.wait_ge(ring_ready[u], t + 1)
                wait_item(pool, xs_stored, t, u, 4, 16)
                pool.nop(nofuse=True)
                for j in range(4):
                    pool.indirect_dma_start(xs[u][:, j, :], None, z_table,
                                            bass.IndirectOffsetOnAxis(ring[u][:, j:j + 1], 0)).then_inc(gathered[u], 16)

            def scale(t, u):
                pool.wait_ge(x_loaded[u], 16 * t + 16)
                pool.tensor_tensor(x[u][:], x[u][:], over_columns(node_scalars(K["dsqrt"], t, u)), ALU.mult).then_inc(x_scaled[u], 1)
            if normed:
                pipeline(pool, (scale, 0), (gather, 0))
            else:
                pipeline(pool, (gather, 0))
    end_stage(nc, owned)


def gcn_first_nodes(nc, A, T, K):
    gcn_nodes(nc, T, K, "g0", T["z2"], K["w0"], K["b0"], T["z1"])


def gcn_second_nodes(nc, A, T, K):
    gcn_nodes(nc, T, K, "g1", T["z1"], K["w1"], K["b1"], T["x3"], T["z2"])




def attention_scores(nc, A, T, K):
    with ExitStack() as ctx:
        sb, ps, sem, sems, owned = stage_makers(nc, ctx, "asc")
        xs = [sb(f"xs{u}", [P, 4, ROW1]) for u in range(BUFS)]
        xd = [sb(f"xd{u}", [P, 4, D]) for u in range(BUFS)]
        xdT = [sb(f"xdT{v}", [P, 4, P]) for v in range(2)]
        prod = [sb(f"prod{u}", [P, 4, D]) for u in range(BUFS)]
        four_scores = [sb(f"fs{u}", [P, 4]) for u in range(BUFS)]
        ring = [sb(f"ring{u}", [P, 4], I32) for u in range(BUFS)]
        scores = sb("scores", [P, CHUNKS])
        rows = sb("rows", [P, 4, P])
        x = [sb(f"x{u}", [P, G, ROW1]) for u in range(BUFS)]
        o = [sb(f"o{u}", [P, G, D]) for u in range(BUFS)]
        x_loaded, rooted, o_stored = sems("x_loaded"), sems("rooted"), sems("o_stored")
        norm = norm_of(sb, sems, K["quarter_eps"], [tile[:, :, 0:D] for tile in x], o,
                       root_degree=lambda t, u: node_scalars(K["dsqrt"], t, u))
        tp = [ps(f"tp{v}", [P, 4, P]) for v in range(2)]
        qp = [ps(f"qp{v}", [P, 4, D]) for v in range(2)]
        sT = ps("sT", [P, 4, P])
        loaded, ring_ready, gathered, turned, copied = sems("loaded"), sems("ring_ready"), sems("gathered"), sems("turned"), sems("copied")
        multiplied, dotted, kept, stored = sems("multiplied"), sems("dotted"), sems("kept"), sems("stored")
        all_scored, scores_turned, rows_ready, rows_stored = sem("all_scored"), sem("scores_turned"), sem("rows_ready"), sem("rows_stored")
        block = ctx.enter_context(nc.Block())

        @block.gpsimd
        def _(pool):
            def gather(t, u):
                pool.wait_ge(ring_ready[u], t + 1)
                wait_item(pool, dotted, t, u, 4)
                wait_item(pool, stored, t, u, 4, 16)
                pool.nop(nofuse=True)
                for j in range(4):
                    pool.indirect_dma_start(xs[u][:, j, :], None, T["x1"],
                                            bass.IndirectOffsetOnAxis(ring[u][:, j:j + 1], 0)).then_inc(gathered[u], 16)
            pipeline(pool, (gather, 0))

        @block.sync
        def _(sp):
            def store(t, u):
                sp.wait_ge(gathered[u], 64 * t + 64)
                sp.dma_start(edge_rows(T["xsrc"], t, u), xs[u][:, :, 0:D]).then_inc(stored[u], 16)

            def load(t, u):
                wait_item(sp, turned, t, u, 4)
                sp.dma_start(xd[u][:], edge_rows(T["x1dst"], t, u)).then_inc(loaded[u], 16)

            def load_nodes(t, u):
                wait_item(sp, norm["normed"], t, u, 4)
                sp.dma_start(x[u][:], node_rows(T["x1"], t, u)).then_inc(x_loaded[u], 16)

            def store_nodes(t, u):
                sp.wait_ge(norm["normed"][u], t + 1)
                if is_item(t, u, ITEMS - 1):
                    wait_item(sp, o_stored, t, u, 1, 16)
                sp.dma_start(node_rows(T["z2"], t, u), o[u][:]).then_inc(o_stored[u], 16)
            pipeline(sp, (load, 0), (load_nodes, 0), (store, 3), (store_nodes, 4))
            for u in range(BUFS):
                sp.wait_ge(o_stored[u], 16 * PER_BUF[u])
            sp.wait_ge(rows_ready, 1)
            sp.dma_start(T["w"].rearrange("(r f) -> r f", f=4 * P), rows[0:CHUNKS // 4].rearrange("p b i -> p (b i)")).then_inc(rows_stored, 16)
            sp.wait_ge(rows_stored, 16)
            for u in range(BUFS):
                sp.wait_ge(stored[u], 16 * PER_BUF[u])

        @block.tensor
        def _(pe):
            def turn(t, u):
                pe.wait_ge(loaded[u], 16 * t + 16)
                wait_item(pe, copied, t, u, 2)
                for j in range(4):
                    tr = pe.transpose(tp[u % 2][:, j, :], xd[u][:, j, :], K["ident"][:])
                tr.then_inc(turned[u], 1)

            def multiply(t, u):
                pe.wait_ge(copied[u], t + 1)
                wait_item(pe, dotted, t, u, 2)
                for j in range(4):
                    mm = pe.matmul(qp[u % 2][:, j, :], xdT[u % 2][:, j, :], K["wqk"][:], start=True, stop=True)
                mm.then_inc(multiplied[u], 1)
            pipeline(pe, (turn, 0), (multiply, 0))
            pe.wait_ge(all_scored, 1)
            for b in range(4):
                tr = pe.transpose(sT[0:CHUNKS // 4, b, :], scores[:].rearrange("p (r b) -> p b r", b=4)[:, b, :], K["ident"][:])
            tr.then_inc(scores_turned, 1)

        @block.scalar
        def _(act):
            def copy(t, u):
                act.wait_ge(turned[u], t + 1)
                wait_item(act, multiplied, t, u, 2)
                act.copy(xdT[u % 2][:], tp[u % 2][:]).then_inc(copied[u], 1)

            def root(t, u):
                act.wait_ge(x_loaded[u], 16 * t + 16)
                act.activation(K["dsqrt"][:, bass.ds(BUFS * t + u, 1), :], x[u][:, :, D:D + 1].rearrange("p g a -> p a g"),
                               ACT.Sqrt, bias=K["one"][:, 0:1]).then_inc(rooted[u], 1)
                norm_root(norm, act, t, u)
            pipeline(act, (copy, 0), (root, 1), (lambda t, u: norm_apply(norm, act, t, u, o_stored), 2))

        @block.vector
        def _(dve):
            def fill_ring(t, u):
                wait_item(dve, gathered, t, u, 4, 64)
                dve.tensor_copy(ring[u][:], four(K["src_idx"], t, u)).then_inc(ring_ready[u], 1)

            def dot(t, u):
                dve.wait_ge(multiplied[u], t + 1)
                dve.wait_ge(gathered[u], 64 * t + 64)
                wait_item(dve, kept, t, u, 4)
                for j in range(4):
                    dt = dve.tensor_tensor_reduce(prod[u][:, j, :], qp[u % 2][:, j, :], xs[u][:, j, 0:D], 1.0, 0.0, ALU.mult, ALU.add,
                                                  four_scores[u][:, j:j + 1])
                dt.then_inc(dotted[u], 1)
                dve.wait_ge(dotted[u], t + 1)
                dve.tensor_copy(four(scores, t, u), four_scores[u][:]).then_inc(kept[u], 1)

            def measure(t, u):
                dve.wait_ge(x_loaded[u], 16 * t + 16)
                norm_measure(norm, dve, t, u)

            def scale(t, u):
                dve.wait_ge(rooted[u], t + 1)
                norm_scale(norm, dve, t, u)
            pipeline(dve, (fill_ring, 0), (measure, 1), (scale, 2), (dot, 3))
            for u in range(BUFS):
                dve.wait_ge(rooted[u], PER_BUF[u])
            dve.reciprocal(K["dinv"][:], K["dsqrt"][:])
            for u in range(BUFS):
                dve.wait_ge(kept[u], PER_BUF[u])
            dve.sem_inc(all_scored, 1)
            dve.wait_ge(scores_turned, 1)
            dve.tensor_copy(rows[0:CHUNKS // 4], sT[0:CHUNKS // 4]).then_inc(rows_ready, 1)
    end_stage(nc, owned)


def attention_softmax(nc, A, T, K):
    with ExitStack() as ctx:
        sb, ps, sem, sems, owned = stage_makers(nc, ctx, "asm")
        e = sb("e", [P, CHUNKS])
        run = sb("run", [P, CHUNKS])
        top = sb("top", [P, CHUNKS])
        tot = sb("tot", [P, CHUNKS])
        rows = sb("rows", [P, 4, P])
        wp = ps("wp", [P, 4, P])
        turner = turner_of(sb, ps, sem)
        loaded, chain_v, shifted, ex_ready = sem("loaded"), sem("chain_v"), sem("shifted"), sem("ex_ready")
        w_ready, w_stored, rows_loaded, rows_turned = sem("w_ready"), sem("w_stored"), sem("rows_loaded"), sem("rows_turned")
        block = ctx.enter_context(nc.Block())
        quarter = CHUNKS // 4

        @block.sync
        def _(sp):
            sp.dma_start(e[:], T["w"].rearrange("(p f) -> p f", f=CHUNKS)).then_inc(loaded, 16)
            sp.wait_ge(w_ready, 1)
            sp.dma_start(T["w"].rearrange("(p f) -> p f", f=CHUNKS), e[:]).then_inc(w_stored, 16)
            sp.wait_ge(w_stored, 16)
            sp.dma_start(rows[0:quarter].rearrange("p b i -> p (b i)"), T["w"].rearrange("(r f) -> r f", f=4 * P)).then_inc(rows_loaded, 16)

        @block.scalar
        def _(act):
            act.wait_ge(shifted, 1)
            act.activation(e[:], e[:], ACT.Exp).then_inc(ex_ready, 1)

        @block.vector
        def _(dve):
            link = chain_of(dve, chain_v)
            link(dve.memset(turner["scr"][:], 0.0))
            link(dve.memset(rows[:], 0.0))
            dve.wait_ge(loaded, 16)
            segment_scan(dve, link, turner, K["seg"], "max", [run[:]], [e[:]])
            segment_scan(dve, link, turner, K["seg"], "fill", [top[:]], [run[:]])
            dve.tensor_tensor(e[:], e[:], top[:], ALU.subtract).then_inc(shifted, 1)
            dve.wait_ge(ex_ready, 1)
            segment_scan(dve, link, turner, K["seg"], "sum", [run[:]], [e[:]])
            segment_scan(dve, link, turner, K["seg"], "fill", [tot[:]], [run[:]])
            link(dve.reciprocal(top[:], tot[:]))
            dve.tensor_tensor(e[:], e[:], top[:], ALU.mult).then_inc(w_ready, 1)
            dve.wait_ge(rows_turned, 1)
            dve.tensor_copy(K["wB"][:].rearrange("p (r b) -> p b r", b=4), wp[:, :, 0:quarter])

        @block.tensor
        def _(pe):
            turn_by_tensor(pe, turner, K["ident"])
            pe.wait_ge(rows_loaded, 16)
            for b in range(4):
                tr = pe.transpose(wp[:, b, :], rows[:, b, :], K["ident"][:])
            tr.then_inc(rows_turned, 1)
    end_stage(nc, owned)


def edge_layer(nc, T, K, name, mode, self_table, out_dst, out_table):
    attn, normed = mode == "attention", mode != "first"
    weight, bias = (K["w0"], K["b0"]) if mode == "first" else (K["w1"], K["b1"])
    with ExitStack() as ctx:
        sb, ps, sem, sems, owned = stage_makers(nc, ctx, name)
        xs = [sb(f"xs{u}", [P, 4, D]) for u in range(BUFS)]
        own = [sb(f"own{u}", [P, 4, D]) for u in range(BUFS)]
        drow = [sb(f"drow{u}", [P, 4, P]) for u in range(BUFS)]
        same = [sb(f"same{u}", [P, 4, P]) for u in range(BUFS)]
        carry = [sb(f"carry{u}", [P, 4, P]) for u in range(BUFS)]
        out = [sb(f"out{u}", [P, 4, D]) for u in range(BUFS)]
        y = [sb(f"y{u}", [P, 4, D]) for u in range(BUFS)]
        o = [sb(f"o{u}", [P, 4, D]) for u in range(BUFS)]
        sring = [sb(f"sring{u}", [P, 4], I32) for u in range(BUFS)]
        x2 = [sb(f"x2{u}", [P, 4, D]) for u in range(BUFS)] if mode == "second" else None
        uT = [sb(f"uT{v}", [P, 4, P]) for v in range(2)]
        op = [ps(f"op{v}", [P, 4, P]) for v in range(2)]
        tp = [ps(f"tp{v}", [P, 4, P]) for v in range(2)]
        hp = [ps(f"hp{v}", [P, 4, D]) for v in range(2)]
        row_loaded, xs_loaded, own_loaded, x2_loaded = sems("row_loaded"), sems("xs_loaded"), sems("own_loaded"), sems("x2_loaded")
        masked, turned, u_copied, multiplied = sems("masked"), sems("turned"), sems("u_copied"), sems("multiplied")
        reduced, copied, combined, taken = sems("reduced"), sems("copied"), sems("combined"), sems("taken")
        x2_scaled, x2_used, ready, sring_ready = sems("x2_scaled"), sems("x2_used"), sems("ready"), sems("sring_ready")
        scattered, stored, zero_set = sems("scattered"), sems("stored"), sem("zero_set")
        norm = norm_of(sb, sems, K["eps"], y, o, width=4,
                       root_degree=(lambda t, u: four(K["dsqrtB"], t, u)) if attn else None) if normed else None
        done = norm["normed"] if normed else ready
        block = ctx.enter_context(nc.Block())

        @block.sync
        def _(sp):
            def load(t, u):
                wait_item(sp, masked, t, u, 4)
                sp.dma_start(drow[u][:], T["ids"][1:2, bass.ds(t * (4 * BUFS * P) + u * 4 * P, 4 * P)].broadcast_to([P, 4 * P])).then_inc(row_loaded[u], 16)
                wait_item(sp, reduced, t, u, 4, 4)
                sp.dma_start(xs[u][:], edge_rows(T["xsrc"], t, u)).then_inc(xs_loaded[u], 16)
                if attn:
                    wait_item(sp, combined, t, u, 4)
                else:
                    wait_item(sp, turned, t, u, 4)
                sp.dma_start(own[u][:], edge_rows(self_table, t, u)).then_inc(own_loaded[u], 16)
                if mode == "second":
                    wait_item(sp, x2_used, t, u, 4)
                    sp.dma_start(x2[u][:], edge_rows(T["z2dst"], t, u)).then_inc(x2_loaded[u], 16)

            def store(t, u):
                sp.wait_ge(done[u], t + 1)
                sp.dma_start(edge_rows(out_dst, t, u), o[u][:]).then_inc(stored[u], 16)
            pipeline(sp, (load, 0), (store, 6))
            for u in range(BUFS):
                sp.wait_ge(stored[u], 16 * PER_BUF[u])

        @block.gpsimd
        def _(pool):
            def scatter(t, u):
                pool.wait_ge(sring_ready[u], t + 1)
                pool.wait_ge(done[u], t + 1)
                pool.nop(nofuse=True)
                for j in range(4):
                    pool.indirect_dma_start(out_table, bass.IndirectOffsetOnAxis(sring[u][:, j:j + 1], 0), o[u][:, j, :], None,
                                            bounds_check=N - 1, oob_is_err=False).then_inc(scattered[u], 16)
            def scale_x2(t, u):
                pool.wait_ge(x2_loaded[u], 16 * t + 16)
                pool.tensor_tensor(x2[u][:], x2[u][:], four(K["dsqrtB"], t, u).unsqueeze(2).broadcast_to([P, 4, D]), ALU.mult).then_inc(x2_scaled[u], 1)
            if mode == "second":
                pipeline(pool, (scale_x2, 0), (scatter, 5))
            else:
                pipeline(pool, (scatter, 0))
            for u in range(BUFS):
                pool.wait_ge(scattered[u], 64 * PER_BUF[u])

        @block.tensor
        def _(pe):
            def can_turn_sums(t, u):
                pe.wait_ge(masked[u], t + 1)
                pe.wait_ge(xs_loaded[u], 16 * t + 16)
                wait_item(pe, u_copied, t, u, 2)

            def turn_sums(t, u, j):
                mm = pe.matmul(tp[u % 2][:, j, :], xs[u][:, j, :], same[u][:, j, :], start=True, stop=True)
                if j == 3:
                    mm.then_inc(turned[u], 1)

            def reduce(t, u):
                after = (t + (u + 1) // BUFS, (u + 1) % BUFS)
                turning = attn and not is_item(t, u, ITEMS - 1)
                if turning:
                    can_turn_sums(*after)
                if attn:
                    pe.wait_ge(u_copied[u], t + 1)
                else:
                    pe.wait_ge(masked[u], t + 1)
                    pe.wait_ge(xs_loaded[u], 16 * t + 16)
                for j in range(4):
                    sums = op[j % 2][:, 0, :]
                    if attn:
                        pe.matmul(sums, uT[u % 2][:, j, :], K["wvo"][:], start=True, stop=False)
                    else:
                        pe.matmul(sums, same[u][:, j, :], xs[u][:, j, :], start=True, stop=False)
                    if turning:
                        turn_sums(*after, j)
                    if j:
                        pe.wait_ge(copied[u], 4 * t + j)
                    else:
                        wait_item(pe, copied, t, u, 1, 4)
                    before = out[u][:, j - 1, :] if j else out[(u - 1) % BUFS][:, 3, :]
                    pe.matmul(sums, carry[u][:, j, :], before, start=False, stop=True).then_inc(reduced[u], 1)

            def turn(t, u):
                pe.wait_ge(combined[u], t + 1)
                wait_item(pe, u_copied, t, u, 2)
                for j in range(4):
                    tr = pe.transpose(tp[u % 2][:, j, :], own[u][:, j, :], K["ident"][:])
                tr.then_inc(turned[u], 1)

            def multiply(t, u):
                pe.wait_ge(u_copied[u], t + 1)
                wait_item(pe, taken, t, u, 2)
                for j in range(4):
                    mm = pe.matmul(hp[u % 2][:, j, :], uT[u % 2][:, j, :], weight[:], start=True, stop=True)
                mm.then_inc(multiplied[u], 1)
            pe.wait_ge(zero_set, 1)
            if attn:
                can_turn_sums(0, 0)
                for j in range(4):
                    turn_sums(0, 0, j)
                pipeline(pe, (reduce, 0))
            else:
                pipeline(pe, (reduce, 0), (turn, 1), (multiply, 2))

        @block.scalar
        def _(act):
            def copy_u(t, u):
                act.wait_ge(turned[u], t + 1)
                if attn:
                    wait_item(act, reduced, t, u, 2, 4)
                else:
                    wait_item(act, multiplied, t, u, 2)
                act.copy(uT[u % 2][:], tp[u % 2][:]).then_inc(u_copied[u], 1)

            def copy_out(t, u):
                wait_item(act, combined, t, u, 4)
                for j in range(4):
                    act.wait_ge(reduced[u], 4 * t + j + 1)
                    act.copy(out[u][:, j, :], op[j % 2][:, 0, :]).then_inc(copied[u], 1)

            def activate(t, u):
                act.wait_ge(taken[u], t + 1)
                wait_item(act, scattered, t, u, 4, 64)
                wait_item(act, stored, t, u, 4, 16)
                for j in range(4):
                    ac = act.activation(o[u][:, j, :], y[u][:, j, :], ACT.Relu, scale=K["dinvB"][:, bass.ds(4 * BUFS * t + 4 * u + j, 1)])
                ac.then_inc(ready[u], 1)

            def root(t, u):
                norm_root(norm, act, t, u)

            def apply(t, u):
                wait_item(act, scattered, t, u, 4, 64)
                norm_apply(norm, act, t, u, stored)
            if attn:
                pipeline(act, (root, 3), (copy_out, 1), (copy_u, 0), (apply, 4))
            elif normed:
                pipeline(act, (root, 4), (copy_out, 0), (copy_u, 1), (apply, 5))
            else:
                pipeline(act, (copy_out, 0), (copy_u, 1), (activate, 4))

        @block.vector
        def _(dve):
            def masks(t, u):
                dve.wait_ge(row_loaded[u], 16 * t + 16)
                wait_item(dve, reduced, t, u, 4, 4)
                chunk = 4 * BUFS * t + 4 * u
                for j in range(4):
                    key = K["dstB"][:, bass.ds(chunk + j, 1)]
                    if attn:
                        dve.tensor_scalar(same[u][:, j, :], drow[u][:, j, :], key, K["wB"][:, bass.ds(chunk + j, 1)],
                                          ALU.is_equal, ALU.mult)
                    else:
                        dve.tensor_scalar(same[u][:, j, :], drow[u][:, j, :], key, None, ALU.is_equal)
                    mk = dve.tensor_scalar(carry[u][:, j, :], drow[u][:, j, :], K["carry_key"][:, bass.ds(chunk + j, 1)],
                                           None, ALU.is_equal)
                mk.then_inc(masked[u], 1)

            def fill_ring(t, u):
                wait_item(dve, scattered, t, u, 4, 64)
                dve.tensor_copy(sring[u][:], four(K["scat_idx"], t, u)).then_inc(sring_ready[u], 1)

            def combine(t, u):
                dve.wait_ge(copied[u], 4 * t + 4)
                dve.wait_ge(own_loaded[u], 16 * t + 16)
                if attn:
                    wait_item(dve, done, t, u, 4)
                    dve.scalar_tensor_tensor(out=y[u][:], in0=own[u][:], scalar=2.0, in1=out[u][:],
                                             op0=ALU.mult, op1=ALU.add).then_inc(combined[u], 1)
                    dve.wait_ge(combined[u], t + 1)
                    norm_measure(norm, dve, t, u)
                else:
                    dve.tensor_tensor(own[u][:], own[u][:], out[u][:], ALU.add).then_inc(combined[u], 1)

            def take(t, u):
                dve.wait_ge(multiplied[u], t + 1)
                wait_item(dve, done, t, u, 4)
                for j in range(4):
                    st = dve.scalar_tensor_tensor(out=y[u][:, j, :], in0=hp[u % 2][:, j, :],
                                                  scalar=K["dinvB"][:, bass.ds(4 * BUFS * t + 4 * u + j, 1)], in1=bias[:],
                                                  op0=ALU.mult, op1=ALU.add)
                st.then_inc(taken[u], 1)

            def add(t, u):
                dve.wait_ge(x2_scaled[u], t + 1)
                dve.wait_ge(taken[u], t + 1)
                dve.scalar_tensor_tensor(out=y[u][:], in0=y[u][:], scalar=0.0, in1=x2[u][:],
                                         op0=ALU.max, op1=ALU.add).then_inc(x2_used[u], 1)
                dve.wait_ge(x2_used[u], t + 1)
                norm_measure(norm, dve, t, u)

            def scale(t, u):
                norm_scale(norm, dve, t, u)
            dve.memset(out[BUFS - 1][:, 3, :], 0.0).then_inc(zero_set, 1)
            if attn:
                pipeline(dve, (masks, 0), (fill_ring, 4), (scale, 3), (combine, 2))
            elif normed:
                pipeline(dve, (masks, 0), (fill_ring, 4), (combine, 1), (take, 3), (scale, 4), (add, 3))
            else:
                pipeline(dve, (masks, 0), (fill_ring, 4), (combine, 1), (take, 3))
    end_stage(nc, owned)


def second_layer(nc, A, T, K):
    edge_layer(nc, T, K, "ats", "attention", T["x1dst"], T["z2dst"], T["z2"])


def gcn_first_edges(nc, A, T, K):
    edge_layer(nc, T, K, "gs0", "first", T["z2dst"], T["z1dst"], T["z1"])


def gcn_second_edges(nc, A, T, K):
    edge_layer(nc, T, K, "gs1", "second", T["z1dst"], T["x3dst"], T["x3"])


def final_edges(nc, A, T, K):
    parts = 2
    with ExitStack() as ctx:
        sb, ps, sem, sems, owned = stage_makers(nc, ctx, "mss")
        xs = [sb(f"xs{u}", [P, 4, D]) for u in range(BUFS)]
        drow = [sb(f"drow{u}", [P, 4, P]) for u in range(BUFS)]
        same = [sb(f"same{u}", [P, 4, P]) for u in range(BUFS)]
        carry = [sb(f"carry{u}", [P, 4, P]) for u in range(BUFS)]
        sums = [sb(f"sums{u}", [P, 4, D]) for u in range(BUFS)]
        y = [sb(f"y{u}", [P, 4, D]) for u in range(BUFS)]
        o = [sb(f"o{u}", [P, 4, D]) for u in range(BUFS)]
        sring = [sb(f"sring{u}", [P, 4], I32) for u in range(BUFS)]
        sumT = [sb(f"sumT{v}", [P, parts, 4, P]) for v in range(2)]
        msg = [sb(f"msg{v}", [P, 4, 2 * D]) for v in range(2)]
        xsT = [sb(f"xsT{v}", [P, 4, P]) for v in range(2)]
        wt = [sb(f"wt{u}", [P, 4, D]) for u in range(BUFS)]
        tmp = [sb(f"tmp{v}", [P, 4, 3, MUL]) for v in range(2)]
        ws = [sb(f"ws{v}", [P, 4, MUL]) for v in range(2)]
        op = [ps(f"op{v}", [P, 4, P]) for v in range(2)]
        tp = ps("tp", [P, parts, 4, P])
        xtp = ps("xtp", [P, 4, P])
        up = [ps(f"up{v}", [P, 4, D]) for v in range(2)]
        row_loaded, xs_loaded, wt_loaded, y_loaded = sems("row_loaded"), sems("xs_loaded"), sems("wt_loaded"), sems("y_loaded")
        masked, sums_turned, sums_copied = sems("masked"), sems("sums_turned"), sems("sums_copied")
        reduced, copied, scattered, sring_ready = sems("reduced"), sems("copied"), sems("scattered"), sems("sring_ready")
        x_turned, x_copied, up_ready = sems("x_turned"), sems("x_copied"), sems("up_ready")
        msg_ready, msg_chain, combined = sems("msg_ready"), sems("msg_chain"), sems("combined")
        zero_set = sem("zero_set")
        norm = norm_of(sb, sems, K["eps"], y, o, width=4)
        block = ctx.enter_context(nc.Block())

        @block.sync
        def _(sp):
            def load(t, u):
                wait_item(sp, masked, t, u, 4)
                sp.dma_start(drow[u][:], T["ids"][1:2, bass.ds(t * (4 * BUFS * P) + u * 4 * P, 4 * P)].broadcast_to([P, 4 * P])).then_inc(row_loaded[u], 16)
                wait_item(sp, x_turned, t, u, 4)
                sp.dma_start(xs[u][:], edge_rows(T["xsrc"], t, u)).then_inc(xs_loaded[u], 16)
                wait_item(sp, msg_ready, t, u, 4)
                sp.dma_start(wt[u][:], edge_rows(T["radial"], t, u)).then_inc(wt_loaded[u], 16)

            def load_y(t, u):
                wait_item(sp, norm["normed"], t, u, 4)
                sp.dma_start(y[u][:], edge_rows(T["x3dst"], t, u)).then_inc(y_loaded[u], 16)
            pipeline(sp, (load, 0), (load_y, 3))

        @block.gpsimd
        def _(pool):
            def scatter(t, u):
                pool.wait_ge(sring_ready[u], t + 1)
                pool.wait_ge(norm["normed"][u], t + 1)
                pool.nop(nofuse=True)
                for j in range(4):
                    pool.indirect_dma_start(T["out"], bass.IndirectOffsetOnAxis(sring[u][:, j:j + 1], 0), o[u][:, j, :], None,
                                            bounds_check=N - 1, oob_is_err=False).then_inc(scattered[u], 16)
            pipeline(pool, (scatter, 0))
            for u in range(BUFS):
                pool.wait_ge(scattered[u], 64 * PER_BUF[u])

        @block.tensor
        def _(pe):
            def turn_x(t, u):
                pe.wait_ge(xs_loaded[u], 16 * t + 16)
                wait_item(pe, x_copied, t, u, 1)
                for j in range(4):
                    tr = pe.transpose(xtp[:, j, :], xs[u][:, j, :], K["ident"][:])
                tr.then_inc(x_turned[u], 1)

            def project(t, u):
                pe.wait_ge(x_copied[u], t + 1)
                wait_item(pe, msg_ready, t, u, 2)
                for j in range(4):
                    mm = pe.matmul(up[u % 2][:, j, :], xsT[u % 2][:, j, :], K["wup"][:], start=True, stop=True)
                mm.then_inc(up_ready[u], 1)

            def turn_sums(t, u):
                pe.wait_ge(masked[u], t + 1)
                pe.wait_ge(msg_ready[u], t + 1)
                wait_item(pe, sums_copied, t, u, 1)
                for a in range(parts):
                    for j in range(4):
                        mm = pe.matmul(tp[:, a, j, :], msg[u % 2][:, j, a * D:(a + 1) * D], same[u][:, j, :], start=True, stop=True)
                mm.then_inc(sums_turned[u], 1)

            def reduce(t, u):
                pe.wait_ge(sums_copied[u], t + 1)
                for j in range(4):
                    total = op[j % 2][:, 0, :]
                    for a in range(parts):
                        pe.matmul(total, sumT[u % 2][:, a, j, :], K["wout"][:, a, :], start=(a == 0), stop=False)
                    if j:
                        pe.wait_ge(copied[u], 4 * t + j)
                    else:
                        wait_item(pe, copied, t, u, 1, 4)
                    before = sums[u][:, j - 1, :] if j else sums[(u - 1) % BUFS][:, 3, :]
                    pe.matmul(total, carry[u][:, j, :], before, start=False, stop=True).then_inc(reduced[u], 1)
            pe.wait_ge(zero_set, 1)
            pipeline(pe, (turn_x, 0), (reduce, 2), (turn_sums, 1), (project, 0))

        @block.scalar
        def _(act):
            def copy_x(t, u):
                act.wait_ge(x_turned[u], t + 1)
                wait_item(act, up_ready, t, u, 2)
                act.copy(xsT[u % 2][:], xtp[:]).then_inc(x_copied[u], 1)

            def copy_sums(t, u):
                act.wait_ge(sums_turned[u], t + 1)
                wait_item(act, reduced, t, u, 2, 4)
                act.copy(sumT[u % 2][:], tp[:]).then_inc(sums_copied[u], 1)

            def copy_out(t, u):
                wait_item(act, combined, t, u, 4)
                for j in range(4):
                    act.wait_ge(reduced[u], 4 * t + j + 1)
                    act.copy(sums[u][:, j, :], op[j % 2][:, 0, :]).then_inc(copied[u], 1)
            pipeline(act, (lambda t, u: norm_root(norm, act, t, u), 4), (copy_x, 0), (copy_out, 2), (copy_sums, 1),
                     (lambda t, u: norm_apply(norm, act, t, u, scattered, 64), 5))

        @block.vector
        def _(dve):
            def masks(t, u):
                dve.wait_ge(row_loaded[u], 16 * t + 16)
                wait_item(dve, reduced, t, u, 4, 4)
                chunk = 4 * BUFS * t + 4 * u
                for j in range(4):
                    dve.tensor_scalar(same[u][:, j, :], drow[u][:, j, :], K["dstB"][:, bass.ds(chunk + j, 1)], None, ALU.is_equal)
                    mk = dve.tensor_scalar(carry[u][:, j, :], drow[u][:, j, :], K["carry_key"][:, bass.ds(chunk + j, 1)],
                                           None, ALU.is_equal)
                mk.then_inc(masked[u], 1)

            def fill_ring(t, u):
                wait_item(dve, scattered, t, u, 4, 64)
                dve.tensor_copy(sring[u][:], four(K["scat_idx"], t, u)).then_inc(sring_ready[u], 1)

            def messages(t, u):
                link = loop_chain_of(dve, msg_chain[u], t, 4)
                dve.wait_ge(wt_loaded[u], 16 * t + 16)
                dve.wait_ge(up_ready[u], t + 1)
                wait_item(dve, sums_turned, t, u, 2)
                wait_item(dve, msg_ready, t, u, 1)
                w = wt[u][:].rearrange("p j (q k) -> p j q k", q=4)
                v = up[u % 2][:].rearrange("p j (q k) -> p j q k", q=4)
                m = msg[u % 2][:].rearrange("p j (q k) -> p j q k", q=8)
                dots, scaled = tmp[u % 2], ws[u % 2]
                axes = K["rhatB"][:, :, bass.ds(4 * BUFS * t + 4 * u, 4)].rearrange("p c j -> p j c").unsqueeze(3).broadcast_to([P, 4, 3, MUL])
                dve.tensor_tensor(m[:, :, 0], w[:, :, 0], v[:, :, 0], ALU.mult)
                link(dve.tensor_tensor(scaled[:], w[:, :, 1], v[:, :, 0], ALU.mult))
                dve.tensor_tensor(m[:, :, 2:5], scaled[:].unsqueeze(2).broadcast_to([P, 4, 3, MUL]), axes, ALU.mult)
                dve.tensor_tensor(m[:, :, 5:8], w[:, :, 2].unsqueeze(2).broadcast_to([P, 4, 3, MUL]), v[:, :, 1:4], ALU.mult)
                link(dve.tensor_tensor(dots[:], v[:, :, 1:4], axes, ALU.mult))
                link(dve.tensor_tensor(dots[:, :, 0], dots[:, :, 0], dots[:, :, 1], ALU.add))
                link(dve.tensor_tensor(dots[:, :, 0], dots[:, :, 0], dots[:, :, 2], ALU.add))
                dve.tensor_tensor(m[:, :, 1], w[:, :, 3], dots[:, :, 0], ALU.mult).then_inc(msg_ready[u], 1)

            def combine(t, u):
                dve.wait_ge(copied[u], 4 * t + 4)
                dve.wait_ge(y_loaded[u], 16 * t + 16)
                dve.tensor_tensor(y[u][:], y[u][:], sums[u][:], ALU.add).then_inc(combined[u], 1)
                dve.wait_ge(combined[u], t + 1)
                norm_measure(norm, dve, t, u)

            dve.memset(sums[BUFS - 1][:, 3, :], 0.0).then_inc(zero_set, 1)
            pipeline(dve, (messages, 1), (masks, 0), (fill_ring, 5), (lambda t, u: norm_scale(norm, dve, t, u), 4), (combine, 3))
    end_stage(nc, owned)


def radial_basis(nc, A, T, K):
    with ExitStack() as ctx:
        sb, ps, sem, sems, owned = stage_makers(nc, ctx, "rad")
        rows = 8 * NB
        r = sb("r", [P, EIGHTS, P])
        part = sb("part", [P, 1], I32)
        center = sb("center", [P, 1])
        inside = sb("inside", [P, EIGHTS * P])
        chain_v, loaded, iota_ready, clipped, squared, expd = [sem(n) for n in ("chain_v", "loaded", "iota_ready", "clipped", "squared", "expd")]
        w_loaded, w_zero = sem("w_loaded"), sem("w_zero")
        block = ctx.enter_context(nc.Block())

        @block.gpsimd
        def _(pool):
            pool.iota(part[:], pattern=[[0, 1]], base=0, channel_multiplier=1).then_inc(iota_ready, 1)

        @block.sync
        def _(sp):
            for g in range(8):
                chunks = T["ew"].rearrange("a (t g i) -> a g t i", g=8, i=P)[:, g]
                sp.dma_start(r[NB * g:NB * (g + 1)], chunks.broadcast_to([NB, EIGHTS, P])).then_inc(loaded, 16)
            sp.wait_ge(w_zero, 1)
            for g in range(8):
                sp.dma_start(K["m0g"][NB * g:NB * (g + 1), g, 0:64], A["L3_gnn_mlp_w0"]).then_inc(w_loaded, 16)
            sp.wait_ge(w_loaded, 128)

        @block.vector
        def _(dve):
            link = chain_of(dve, chain_v)
            dve.memset(K["m0g"][:], 0.0).then_inc(w_zero, 1)
            link(dve.memset(K["emb"][:], 0.0))
            dve.wait_ge(iota_ready, 1)
            link(dve.tensor_scalar(part[:], part[:], NB - 1, None, ALU.bitwise_and))
            link(dve.tensor_scalar(center[:], part[:], -1.0, None, ALU.mult))
            dve.wait_ge(loaded, 128)
            flat = r[0:rows].rearrange("p t i -> p (t i)")
            link(dve.tensor_scalar(inside[0:rows], flat, 1.0, float(NB) ** 0.5, ALU.is_le, ALU.mult))
            dve.tensor_scalar(flat, flat, 0.0, 1.0, ALU.max, ALU.min).then_inc(clipped, 1)
            dve.wait_ge(expd, 1)
            dve.tensor_tensor(K["emb"][0:rows], flat, inside[0:rows], ALU.mult)

        @block.scalar
        def _(act):
            flat = r[0:rows].rearrange("p t i -> p (t i)")
            act.wait_ge(clipped, 1)
            act.activation(flat, flat, ACT.Square, bias=center[0:rows, 0:1], scale=float(NB - 1)).then_inc(squared, 1)
            act.wait_ge(squared, 1)
            act.activation(flat, flat, ACT.Exp, scale=-0.5).then_inc(expd, 1)
    end_stage(nc, owned)


def radial_block(K, t, u):
    return K["emb"][:, bass.ds(t * (BUFS // 2 * P) + u // 2 * P, P)]




def tables(nc, shown=()):
    T = {}
    def dram(name, shape, dtype=F32):
        return nc.dram_tensor(name, shape, dtype, kind="ExternalOutput" if name in shown else "Internal").ap()
    T["ids"] = dram("t_ids", (2, EP + P))
    T["ew"] = dram("t_ew", (1, EP))
    T["up"] = dram("t_up", (D, D))
    T["sorted"] = dram("t_sorted", (3, SORTN))
    T["scores"] = dram("t_scores", (N, 8))
    T["alpha"] = dram("t_alpha", (SORTN, HEADS))
    T["totals"] = dram("t_totals", (HEADS + 1, EP))
    T["xdst"] = dram("t_xdst", (EP, D))
    T["x1dst"] = dram("t_x1dst", (EP, D))
    for name in ("z2dst", "z1dst", "x3dst"):
        T[name] = dram("t_" + name, (EP, D))
    T["xsrc"] = dram("t_xsrc", (EP, D))
    T["radial"] = dram("t_radial", (EP, D))
    T["w"] = dram("t_w", (EP,))
    T["x1"] = dram("t_x1", (N, ROW1))
    T["z2"] = dram("t_z2", (N, D))
    T["z1"] = dram("t_z1", (N, D))
    T["x3"] = dram("t_x3", (N, D))
    return T


def kept(sb):
    K = {}
    K["ident"] = sb("ident", [P, P])
    for_weights = [P, D]
    K["w0"], K["w1"], K["wh"] = sb("w0", for_weights), sb("w1", for_weights), sb("wh", for_weights)
    K["wqk"], K["wvo"], K["wup"] = sb("wqk", for_weights), sb("wvo", for_weights), sb("wup", for_weights)
    K["wout"] = sb("wout", [P, 2, D])
    K["wa"] = sb("wa", [P, 8])
    K["bias0"], K["b0"], K["b1"], K["mb2"] = [sb(n, for_weights) for n in ("bias0", "b0", "b1", "mb2")]
    K["m0"], K["m1"], K["m2"] = [sb(n, for_weights) for n in ("m0", "m1", "m2")]
    K["mb0"], K["mb1"], K["eps"], K["one"], K["quarter_eps"] = [sb(n, [P, 1]) for n in ("mb0", "mb1", "eps", "one", "quarter_eps")]
    K["dstB"], K["carry_key"] = sb("dstB", [P, CHUNKS]), sb("carry_key", [P, CHUNKS])
    K["rhatB"] = sb("rhatB", [P, 3, CHUNKS])
    K["src_idx"], K["dst_idx"], K["scat_idx"] = [sb(n, [P, CHUNKS], I32) for n in ("src_idx", "dst_idx", "scat_idx")]
    K["ids"] = sb("ids", [P, CHUNKS])
    K["seg"] = segment_tiles(sb, "dst", HEADS + 1)
    K["totB"] = sb("totB", [P, HEADS + 1, CHUNKS])
    K["dinv"] = sb("dinv", [P, NSUPER, G])
    K["dinvB"], K["dsqrtB"] = sb("dinvB", [P, CHUNKS]), sb("dsqrtB", [P, CHUNKS])
    K["wB"] = sb("wB", [P, CHUNKS])
    K["m0g"] = sb("m0g", [P, 8, P])
    K["emb"] = sb("emb", [P, EIGHTS * P])
    K["dsqrt"] = sb("dsqrt", [P, NSUPER, G])
    return K


def build(nc, A, out, stop=99, shown=()):
    T = tables(nc, shown)
    T["out"] = out
    with ExitStack() as ctx:
        K = kept(stage_makers(nc, ctx, "kept")[0])
        for stage in STAGES[:stop]:
            stage(nc, A, T, K)


STAGES = [prepare, radial_basis, sort_and_scores, gat_softmax, gat_sums, first_layer, attention_scores, attention_softmax,
          second_layer, gcn_first_nodes, gcn_first_edges, gcn_second_nodes, gcn_second_edges, final_nodes,
          final_edges]


_INS = ["x", "src", "dst", "edge_attr_3", "edge_weight", "L0_gnn_W", "L0_gnn_att", "L0_gnn_bias", "L1_gnn_Wq", "L1_gnn_Wk",
        "L1_gnn_Wv", "L1_gnn_Wo", "L2_gnn_W0", "L2_gnn_b0", "L2_gnn_W1", "L2_gnn_b1", "L3_gnn_W_up0", "L3_gnn_W_up1",
        "L3_gnn_mlp_w0", "L3_gnn_mlp_b0", "L3_gnn_mlp_w1", "L3_gnn_mlp_b1", "L3_gnn_mlp_w2", "L3_gnn_mlp_b2",
        "L3_gnn_W_out0", "L3_gnn_W_out1"]


def kernel(**inputs):
    import numpy as _np
    import concourse.bacc as _bacc
    from concourse import mybir as _mybir
    from concourse.bass_utils import run_bass_kernel_spmd as _run

    nc = _bacc.Bacc("TRN2", target_bir_lowering=False, num_devices=1)
    arrays, args = {}, {}
    for name in _INS:
        a = _np.ascontiguousarray(inputs[name])
        arrays[f"in_{name}_dram"] = a
        args[name] = nc.dram_tensor(f"in_{name}_dram", a.shape, _mybir.dt.from_np(a.dtype), kind="ExternalInput").ap()
    out = nc.dram_tensor("out_0_dram", (N, D), F32, kind="ExternalOutput").ap()
    build(nc, args, out)
    r = _run(nc, [arrays], core_ids=[0])
    return r.results[0]["out_0_dram"]
```
